# Optimizing a Trainium2 kernel written in Bass

```python
import numpy as np
import jax
import jax.numpy as jnp

def _softmax(x, axis=-1):
    return jax.nn.softmax(x, axis=axis)

def _gelu(x):
    return jax.nn.gelu(x, approximate=True)

def _silu(x):
    return jax.nn.silu(x)

def _sigmoid(x):
    return jax.nn.sigmoid(x)

def _layernorm(x, axis=-1, eps=1e-05):
    m = jnp.mean(x, axis=axis, keepdims=True)
    v = jnp.var(x, axis=axis, keepdims=True)
    return (x - m) / jnp.sqrt(v + eps)

def _scatter_add(tgt, idx, src, axis=0):
    return tgt.at[idx].add(src)

def _segment_sum(src, seg, n):
    return jax.ops.segment_sum(src, seg, n)
kernel_name = 'mk_hybrid_d1_jaxref_r8_42064f'

def setup_inputs(seed: int=0):
    np.random.seed(seed)
    _w = jnp.asarray

    def _L0_attn_a_setup():
        import jax, jax.numpy as jnp
        import numpy as np
        DIM = 256
        H = 16
        DH = DIM // H
        LATENT = 64
        D_ROPE = 64
        B, S = (2, 256)
        ROPE_THETA = 10000.0

        def _rope_cos_sin(seq_len, d_rope, dtype=jnp.float32):
            inv_freq = 1.0 / ROPE_THETA ** (jnp.arange(0, d_rope, 2, dtype=jnp.float32) / d_rope)
            freqs = jnp.arange(seq_len, dtype=jnp.float32)[:, None] * inv_freq[None, :]
            emb = jnp.concatenate([freqs, freqs], axis=-1)
            return (jnp.cos(emb).astype(dtype), jnp.sin(emb).astype(dtype))

        def _rotate_half(x):
            x1, x2 = jnp.split(x, 2, axis=-1)
            return jnp.concatenate([-x2, x1], axis=-1)

        def _apply_rope(x, cos, sin):
            return x * cos + _rotate_half(x) * sin
        key = jax.random.key(seed)
        ks = jax.random.split(key, 6)
        std = 0.02
        return {'x': jax.random.normal(ks[0], (B, S, DIM), jnp.float32), 'Wq': jax.random.normal(ks[1], (DIM, H * (DH + D_ROPE)), jnp.float32) * std, 'Wdkv': jax.random.normal(ks[2], (DIM, LATENT), jnp.float32) * std, 'Wkr': jax.random.normal(ks[3], (DIM, D_ROPE), jnp.float32) * std, 'Wukv': jax.random.normal(ks[4], (LATENT, H * 2 * DH), jnp.float32) * std, 'Wo': jax.random.normal(ks[5], (H * DH, DIM), jnp.float32) * std}
    _L0_attn_a_in = _L0_attn_a_setup()

    def _L0_attn_b_setup():
        import jax, jax.numpy as jnp
        import numpy as np
        HID = 256
        D_SSM = 512
        G = 1
        S = 128
        H = 64
        P = D_SSM // H
        K = 4
        EPS = 1e-05
        CONV_DIM = D_SSM + 2 * G * S
        PROJ = 2 * D_SSM + 2 * G * S + H
        MULT = [0.25, 0.5, 0.75, 1.0, 1.25]

        def _mup_vector():
            v = np.ones(PROJ, np.float32)
            gs = G * S
            v[:D_SSM] *= MULT[0]
            v[D_SSM:2 * D_SSM] *= MULT[1]
            v[2 * D_SSM:2 * D_SSM + gs] *= MULT[2]
            v[2 * D_SSM + gs:2 * D_SSM + 2 * gs] *= MULT[3]
            v[2 * D_SSM + 2 * gs:] *= MULT[4]
            return jnp.asarray(v)

        def _reference_tuple_inner(hidden_states, residual, W_in, conv_w, conv_b, A_log, D, dt_bias, norm_w, W_out, mup_vector):
            B, L, _ = hidden_states.shape
            Hg = H // G
            proj = hidden_states @ W_in * mup_vector
            z, xBC, dt = jnp.split(proj, [D_SSM, D_SSM + CONV_DIM], axis=-1)
            xp = jnp.pad(xBC, ((0, 0), (K - 1, 0), (0, 0)))
            conv = conv_b + sum((conv_w[:, k] * xp[:, k:k + L] for k in range(K)))
            xBC = jax.nn.silu(conv)
            x = xBC[..., :D_SSM].reshape(B, L, G, Hg, P)
            Bm = xBC[..., D_SSM:D_SSM + G * S].reshape(B, L, G, S)
            Cm = xBC[..., D_SSM + G * S:].reshape(B, L, G, S)
            dt = jax.nn.softplus(dt + dt_bias).reshape(B, L, G, Hg)
            dA = jnp.exp(dt * (-jnp.exp(A_log)).reshape(G, Hg))
            xs = (x.transpose(1, 0, 2, 3, 4), Bm.transpose(1, 0, 2, 3), Cm.transpose(1, 0, 2, 3), dA.transpose(1, 0, 2, 3), dt.transpose(1, 0, 2, 3))

            def step(state, inp):
                x_t, B_t, C_t, dA_t, dt_t = inp
                state = state * dA_t[..., None, None] + (dt_t[..., None] * x_t)[..., None] * B_t[:, :, None, None, :]
                y_t = jnp.einsum('bghps,bgs->bghp', state, C_t)
                return (state, y_t)
            state0 = jnp.zeros((B, G, Hg, P, S), hidden_states.dtype)
            _, ys = jax.lax.scan(step, state0, xs)
            y = ys.transpose(1, 0, 2, 3, 4) + D.reshape(G, Hg)[..., None] * x
            y = y.reshape(B, L, D_SSM)
            g = y * jax.nn.silu(z)
            g = g * jax.lax.rsqrt(jnp.mean(jnp.square(g), axis=-1, keepdims=True) + EPS) * norm_w
            out = g @ W_out
            return (out, residual)
        key = jax.random.key(seed)
        ks = jax.random.split(key, 10)
        B, L = (2, 256)
        return {'hidden_states': jax.random.normal(ks[0], (B, L, HID), jnp.float32), 'residual': jax.random.normal(ks[1], (B, L, HID), jnp.float32), 'W_in': jax.random.normal(ks[2], (HID, PROJ), jnp.float32) * 0.02, 'conv_w': jax.random.normal(ks[3], (CONV_DIM, K), jnp.float32) * 0.2, 'conv_b': jax.random.normal(ks[4], (CONV_DIM,), jnp.float32) * 0.02, 'A_log': jax.random.uniform(ks[5], (H,), jnp.float32, 0.0, 1.0), 'D': jax.random.normal(ks[6], (H,), jnp.float32) * 0.5, 'dt_bias': jax.random.normal(ks[7], (H,), jnp.float32) * 0.5, 'norm_w': jnp.ones((D_SSM,), jnp.float32), 'W_out': jax.random.normal(ks[8], (D_SSM, HID), jnp.float32) * 0.02, 'mup_vector': _mup_vector()}
    _L0_attn_b_in = _L0_attn_b_setup()

    def _L0_ffn_setup():
        import jax, jax.numpy as jnp
        import numpy as np
        B, S, D = (4, 128, 256)
        H = 512
        NE = 8
        TOPK = 2
        key = jax.random.key(seed)
        ks = jax.random.split(key, 9)
        s = lambda fan_in: 1.0 / np.sqrt(fan_in)
        return {'x': jax.random.normal(ks[0], (B, S, D), dtype=jnp.float32), 'W1': jax.random.normal(ks[1], (NE, D, H), dtype=jnp.float32) * s(D), 'b1': jnp.zeros((NE, H), dtype=jnp.float32), 'W2': jax.random.normal(ks[2], (NE, H, H), dtype=jnp.float32) * s(H), 'b2': jnp.zeros((NE, H), dtype=jnp.float32), 'W3': jax.random.normal(ks[3], (NE, H, D), dtype=jnp.float32) * s(H), 'b3': jnp.zeros((NE, D), dtype=jnp.float32), 'Wg': jax.random.normal(ks[4], (D, NE), dtype=jnp.float32) * s(D), 'bg': jnp.zeros((NE,), dtype=jnp.float32)}
    _L0_ffn_in = _L0_ffn_setup()
    _d = {'L0_attn_a_x': _L0_attn_a_in['x'], 'L0_attn_a_Wq': _L0_attn_a_in['Wq'], 'L0_attn_a_Wdkv': _L0_attn_a_in['Wdkv'], 'L0_attn_a_Wkr': _L0_attn_a_in['Wkr'], 'L0_attn_a_Wukv': _L0_attn_a_in['Wukv'], 'L0_attn_a_Wo': _L0_attn_a_in['Wo'], 'L0_attn_b_residual': _L0_attn_b_in['residual'], 'L0_attn_b_W_in': _L0_attn_b_in['W_in'], 'L0_attn_b_conv_w': _L0_attn_b_in['conv_w'], 'L0_attn_b_conv_b': _L0_attn_b_in['conv_b'], 'L0_attn_b_A_log': _L0_attn_b_in['A_log'], 'L0_attn_b_D': _L0_attn_b_in['D'], 'L0_attn_b_dt_bias': _L0_attn_b_in['dt_bias'], 'L0_attn_b_norm_w': _L0_attn_b_in['norm_w'], 'L0_attn_b_W_out': _L0_attn_b_in['W_out'], 'L0_attn_b_mup_vector': _L0_attn_b_in['mup_vector'], 'L0_ffn_W1': _L0_ffn_in['W1'], 'L0_ffn_b1': _L0_ffn_in['b1'], 'L0_ffn_W2': _L0_ffn_in['W2'], 'L0_ffn_b2': _L0_ffn_in['b2'], 'L0_ffn_W3': _L0_ffn_in['W3'], 'L0_ffn_b3': _L0_ffn_in['b3'], 'L0_ffn_Wg': _L0_ffn_in['Wg'], 'L0_ffn_bg': _L0_ffn_in['bg']}
    _x0 = _d['L0_attn_a_x']
    _d['L0_attn_a_x'] = jax.random.normal(jax.random.fold_in(jax.random.key(seed), 1), (4, 512, 256), dtype=_x0.dtype)
    del _x0
    return _d

def reference(L0_attn_a_x, L0_attn_a_Wq, L0_attn_a_Wdkv, L0_attn_a_Wkr, L0_attn_a_Wukv, L0_attn_a_Wo, L0_attn_b_residual, L0_attn_b_W_in, L0_attn_b_conv_w, L0_attn_b_conv_b, L0_attn_b_A_log, L0_attn_b_D, L0_attn_b_dt_bias, L0_attn_b_norm_w, L0_attn_b_W_out, L0_attn_b_mup_vector, L0_ffn_W1, L0_ffn_b1, L0_ffn_W2, L0_ffn_b2, L0_ffn_W3, L0_ffn_b3, L0_ffn_Wg, L0_ffn_bg):

    def _L0_attn_a_ref(x, Wq, Wdkv, Wkr, Wukv, Wo):
        import jax, jax.numpy as jnp
        import numpy as np
        DIM = 256
        H = 16
        DH = DIM // H
        LATENT = 64
        D_ROPE = 64
        B, S = (2, 256)
        ROPE_THETA = 10000.0

        def _rope_cos_sin(seq_len, d_rope, dtype=jnp.float32):
            inv_freq = 1.0 / ROPE_THETA ** (jnp.arange(0, d_rope, 2, dtype=jnp.float32) / d_rope)
            freqs = jnp.arange(seq_len, dtype=jnp.float32)[:, None] * inv_freq[None, :]
            emb = jnp.concatenate([freqs, freqs], axis=-1)
            return (jnp.cos(emb).astype(dtype), jnp.sin(emb).astype(dtype))

        def _rotate_half(x):
            x1, x2 = jnp.split(x, 2, axis=-1)
            return jnp.concatenate([-x2, x1], axis=-1)

        def _apply_rope(x, cos, sin):
            return x * cos + _rotate_half(x) * sin
        Bd, Sd, _ = x.shape
        q = (x @ Wq).reshape(Bd, Sd, H, DH + D_ROPE)
        q_nope, q_rope = (q[..., :DH], q[..., DH:])
        c_kv = x @ Wdkv
        kv = (c_kv @ Wukv).reshape(Bd, Sd, H, 2 * DH)
        k_nope, v = (kv[..., :DH], kv[..., DH:])
        k_rope = x @ Wkr
        cos, sin = _rope_cos_sin(Sd, D_ROPE, x.dtype)
        q_rope = _apply_rope(q_rope, cos[None, :, None, :], sin[None, :, None, :])
        k_rope = _apply_rope(k_rope, cos[None, :, :], sin[None, :, :])
        scale = 1.0 / jnp.sqrt(jnp.asarray(DH + D_ROPE, x.dtype))
        scores = jnp.einsum('bqhd,bkhd->bhqk', q_nope, k_nope)
        scores = scores + jnp.einsum('bqhd,bkd->bhqk', q_rope, k_rope)
        scores = scores * scale
        causal = jnp.tril(jnp.ones((Sd, Sd), dtype=bool))
        scores = jnp.where(causal[None, None, :, :], scores, jnp.asarray(-1000000000.0, x.dtype))
        attn = jax.nn.softmax(scores, axis=-1)
        out = jnp.einsum('bhqk,bkhd->bqhd', attn, v).reshape(Bd, Sd, H * DH)
        return out @ Wo

    def _L0_attn_b_ref(hidden_states, residual, W_in, conv_w, conv_b, A_log, D, dt_bias, norm_w, W_out, mup_vector):
        import jax, jax.numpy as jnp
        import numpy as np
        HID = 256
        D_SSM = 512
        G = 1
        S = 128
        H = 64
        P = D_SSM // H
        K = 4
        EPS = 1e-05
        CONV_DIM = D_SSM + 2 * G * S
        PROJ = 2 * D_SSM + 2 * G * S + H
        MULT = [0.25, 0.5, 0.75, 1.0, 1.25]

        def _mup_vector():
            v = np.ones(PROJ, np.float32)
            gs = G * S
            v[:D_SSM] *= MULT[0]
            v[D_SSM:2 * D_SSM] *= MULT[1]
            v[2 * D_SSM:2 * D_SSM + gs] *= MULT[2]
            v[2 * D_SSM + gs:2 * D_SSM + 2 * gs] *= MULT[3]
            v[2 * D_SSM + 2 * gs:] *= MULT[4]
            return jnp.asarray(v)

        def _reference_tuple_inner(hidden_states, residual, W_in, conv_w, conv_b, A_log, D, dt_bias, norm_w, W_out, mup_vector):
            B, L, _ = hidden_states.shape
            Hg = H // G
            proj = hidden_states @ W_in * mup_vector
            z, xBC, dt = jnp.split(proj, [D_SSM, D_SSM + CONV_DIM], axis=-1)
            xp = jnp.pad(xBC, ((0, 0), (K - 1, 0), (0, 0)))
            conv = conv_b + sum((conv_w[:, k] * xp[:, k:k + L] for k in range(K)))
            xBC = jax.nn.silu(conv)
            x = xBC[..., :D_SSM].reshape(B, L, G, Hg, P)
            Bm = xBC[..., D_SSM:D_SSM + G * S].reshape(B, L, G, S)
            Cm = xBC[..., D_SSM + G * S:].reshape(B, L, G, S)
            dt = jax.nn.softplus(dt + dt_bias).reshape(B, L, G, Hg)
            dA = jnp.exp(dt * (-jnp.exp(A_log)).reshape(G, Hg))
            xs = (x.transpose(1, 0, 2, 3, 4), Bm.transpose(1, 0, 2, 3), Cm.transpose(1, 0, 2, 3), dA.transpose(1, 0, 2, 3), dt.transpose(1, 0, 2, 3))

            def step(state, inp):
                x_t, B_t, C_t, dA_t, dt_t = inp
                state = state * dA_t[..., None, None] + (dt_t[..., None] * x_t)[..., None] * B_t[:, :, None, None, :]
                y_t = jnp.einsum('bghps,bgs->bghp', state, C_t)
                return (state, y_t)
            state0 = jnp.zeros((B, G, Hg, P, S), hidden_states.dtype)
            _, ys = jax.lax.scan(step, state0, xs)
            y = ys.transpose(1, 0, 2, 3, 4) + D.reshape(G, Hg)[..., None] * x
            y = y.reshape(B, L, D_SSM)
            g = y * jax.nn.silu(z)
            g = g * jax.lax.rsqrt(jnp.mean(jnp.square(g), axis=-1, keepdims=True) + EPS) * norm_w
            out = g @ W_out
            return (out, residual)
        return _reference_tuple_inner(hidden_states, residual, W_in, conv_w, conv_b, A_log, D, dt_bias, norm_w, W_out, mup_vector)[0]

    def _L0_ffn_ref(x, W1, b1, W2, b2, W3, b3, Wg, bg):
        import jax, jax.numpy as jnp
        import numpy as np
        B, S, D = (4, 128, 256)
        H = 512
        NE = 8
        TOPK = 2
        gate_logits = jnp.einsum('bsd,dn->bsn', x, Wg) + bg
        gate_weights = jax.nn.softmax(gate_logits, axis=-1)
        topv, topi = jax.lax.top_k(gate_weights, TOPK)
        h = jax.nn.gelu(jnp.einsum('bsd,ndh->nbsh', x, W1) + b1[:, None, None, :], approximate=False)
        h = jax.nn.gelu(jnp.einsum('nbsh,nhf->nbsf', h, W2) + b2[:, None, None, :], approximate=False)
        eo = jnp.einsum('nbsf,nfd->nbsd', h, W3) + b3[:, None, None, :]
        comb = jnp.sum(jax.nn.one_hot(topi, NE, dtype=x.dtype) * topv[..., None], axis=-2)
        out = jnp.einsum('nbsd,bsn->bsd', eo, comb)
        return out
    x = L0_attn_a_x
    x = x + _L0_attn_a_ref(_layernorm(x, axis=-1), L0_attn_a_Wq, L0_attn_a_Wdkv, L0_attn_a_Wkr, L0_attn_a_Wukv, L0_attn_a_Wo)
    x = x + _L0_ffn_ref(_layernorm(x, axis=-1), L0_ffn_W1, L0_ffn_b1, L0_ffn_W2, L0_ffn_b2, L0_ffn_W3, L0_ffn_b3, L0_ffn_Wg, L0_ffn_bg)
    x = x + _L0_attn_b_ref(_layernorm(x, axis=-1), L0_attn_b_residual, L0_attn_b_W_in, L0_attn_b_conv_w, L0_attn_b_conv_b, L0_attn_b_A_log, L0_attn_b_D, L0_attn_b_dt_bias, L0_attn_b_norm_w, L0_attn_b_W_out, L0_attn_b_mup_vector)
    x = x + _L0_ffn_ref(_layernorm(x, axis=-1), L0_ffn_W1, L0_ffn_b1, L0_ffn_W2, L0_ffn_b2, L0_ffn_W3, L0_ffn_b3, L0_ffn_Wg, L0_ffn_bg)
    return x

_drawn_inputs = setup_inputs


def setup_inputs(seed=0):
    import zlib

    import numpy as np

    out = dict(_drawn_inputs(seed))
    spreads = {'L0_attn_b_norm_w': (1.0, 0.6),
     'L0_ffn_b1': (0.0, 0.8),
     'L0_ffn_b2': (0.0, 0.8),
     'L0_ffn_b3': (0.0, 0.636),
     'L0_ffn_bg': (0.0, 0.8)}
    factors = {'L0_attn_a_Wq': 8.0,
     'L0_attn_a_Wdkv': 8.0,
     'L0_attn_a_Wkr': 8.0,
     'L0_attn_a_Wukv': 8.0,
     'L0_attn_a_Wo': 8.0,
     'L0_attn_b_A_log': 64.0,
     'L0_attn_b_dt_bias': 64.0,
     'L0_attn_b_W_in': 2.987,
     'L0_attn_b_conv_w': 3.312,
     'L0_attn_b_conv_b': 8.0,
     'L0_attn_b_D': 2.668,
     'L0_attn_b_W_out': 3.019,
     'L0_attn_b_mup_vector': 3.809}
    for name, (base, spread) in spreads.items():
        noise = np.random.default_rng([zlib.crc32(name.encode()), seed]).standard_normal(out[name].shape)
        drawn = base * np.exp(spread * noise) if base else spread * noise
        out[name] = jnp.asarray(drawn.astype(out[name].dtype))
    for name, factor in factors.items():
        out[name] = (out[name] * factor).astype(out[name].dtype)
    return out
```

```python
from contextlib import ExitStack

import numpy as np

import concourse.bass as bass
from concourse import mybir

F32 = mybir.dt.float32
F16 = mybir.dt.float16
BF16 = mybir.dt.bfloat16
I32 = mybir.dt.int32
ALU = mybir.AluOpType
ACT = mybir.ActivationFunctionType
AX = mybir.AxisListType
ds = bass.ds

P = 128
B, S, D = 4, 512, 256
NT = B * S // P
TB = S // P
KD = D // P
EPS = 1e-5

NH, DH, DR, LAT = 16, 16, 64, 64
HD = DH + DR
HALF = DR // 2
ATT_SCALE = float(HD) ** -0.5


class Tensors:

    def __init__(self, nc, ctx, stage):
        self.nc, self.ctx, self.stage, self.sems = nc, ctx, stage, []

    def sb(self, name, shape, dt=F32):
        return self.ctx.enter_context(self.nc.sbuf_tensor(f"{self.stage}_{name}", shape, dt))

    def banks(self, n=8):
        return [self.ctx.enter_context(self.nc.psum_tensor(f"{self.stage}_bank{i}", [P, 512], F32)) for i in range(n)]

    def sem(self, name):
        self.sems.append(self.ctx.enter_context(self.nc.semaphore(f"{self.stage}_{name}")))
        return self.sems[-1]

    def block(self):
        self.ctx.callback(self.clear)
        return self.ctx.enter_context(self.nc.Block())

    def clear(self):
        numbers = sorted(s.num for s in self.sems)
        with self.nc.Block() as block:

            @block.gpsimd
            def _(pool):
                start = numbers[0]
                for at, n in enumerate(numbers):
                    if n + 1 not in numbers[at:]:
                        pool.sem_clear(range(start, n + 1))
                        start = numbers[at + 1] if at + 1 < len(numbers) else None


def wait_alone(eng, sem, value, passed):
    eng.wait_ge(sem, value)
    eng.sem_inc(passed, 1)


class Chain:

    def __init__(self, eng, sem, passed=None):
        self.eng, self.sem, self.passed, self.base, self.n = eng, sem, passed, 0, 0

    def __call__(self, ins):
        self.n += 1
        ins.then_inc(self.sem, 1)
        if self.passed is None:
            self.eng.wait_ge(self.sem, self.base + self.n)
        else:
            wait_alone(self.eng, self.sem, self.base + self.n, self.passed)


def product3(pe, out, a, b, start, stop):
    (ah, al), (bh, bl) = a, b
    pe.matmul(out, ah, bh, start=start, stop=False)
    pe.matmul(out, ah, bl, start=False, stop=False)
    return pe.matmul(out, al, bh, start=False, stop=stop)


def layer_norm_stage(nc, stage, X, XN, XTh, XTl, identf):
    G = NT // TB
    with ExitStack() as ctx:
        t = Tensors(nc, ctx, stage)
        stats = t.sb("stats", [P, TB, 6])
        mv = t.sb("mv", [P, TB, 2])
        sd = t.sb("sd", [P, TB])
        rs = t.sb("rs", [P, TB])
        xs = t.sb("xs", [P, 2, TB, D])
        bank = t.banks()
        ordered, passed = t.sem("ordered"), t.sem("passed")
        var_ready, sd_ready, norm_ready = t.sem("var_ready"), t.sem("sd_ready"), t.sem("norm_ready")
        xpose_ready, high_ready, low_ready, kept = (t.sem(n) for n in ("xpose_ready", "high_ready", "low_ready", "kept"))
        block = t.block()

        @block.vector
        def _(dve):
            link = Chain(dve, ordered, passed)
            dve.sem_inc(low_ready, 2 * KD)
            PER = 2 + TB

            def low_parts(g, half):
                for k in range(KD):
                    dve.wait_ge(high_ready, (g * KD) + k + 1)
                    dve.tensor_tensor(XTl[:, k, ds(g * S, S)], bank[2 * half + k][:, :], XTh[:, k, ds(g * S, S)],
                                      ALU.subtract).then_inc(low_ready, 1)

            with dve.Fori(0, G // 2) as m:
                for half in range(2):
                    g = m * 2 + half
                    link.base, link.n = g * PER, 0
                    for i in range(TB):
                        last = dve.bn_stats(stats[:, i, :], X[:, ds(g * TB + i, 1), :].rearrange("p a d -> p (a d)"))
                    link(last)
                    for i in range(TB):
                        last = dve.bn_aggr(mv[:, i, :], stats[:, i, :])
                    link(last)
                    dve.tensor_scalar(mv[:, :, 1], mv[:, :, 1], EPS, None, ALU.add).then_inc(var_ready, 1)
                    dve.wait_ge(sd_ready, g + 1)
                    link(dve.reciprocal(rs[:, :], sd[:, :]))
                    dve.wait_ge(xpose_ready, KD * (g + 1))
                    if XN is not None:
                        dve.wait_ge(kept, g + 1)
                    for i in range(TB):
                        ins = dve.tensor_scalar(xs[:, half, i, :], X[:, ds(g * TB + i, 1), :].rearrange("p a d -> p (a d)"),
                                                mv[:, i, 0:1], rs[:, i:i + 1], ALU.subtract, ALU.mult)
                        if i == TB - 1:
                            ins.then_inc(norm_ready, 1)
                        else:
                            link(ins)
                    dve.wait_ge(norm_ready, g + 1)
                    low_parts(g, half)

        @block.scalar
        def _(act):
            with act.Fori(0, G // 2) as m:
                for half in range(2):
                    g = m * 2 + half
                    act.wait_ge(var_ready, g + 1)
                    act.activation(sd[:, :], mv[:, :, 1], ACT.Sqrt).then_inc(sd_ready, 1)
                    for k in range(KD):
                        act.wait_ge(xpose_ready, KD * 2 + KD * g + k + 1)
                        act.activation(XTh[:, k, ds(g * S, S)], bank[2 * half + k][:, :], ACT.Copy).then_inc(high_ready, 1)

        @block.tensor
        def _(pe):
            pe.sem_inc(xpose_ready, 2 * KD)
            with pe.Fori(0, G // 2) as m:
                for half in range(2):
                    g = m * 2 + half
                    pe.wait_ge(norm_ready, g + 1)
                    if half == 0:
                        pe.wait_ge(low_ready, KD * 2 * (m + 1))
                    for k in range(KD):
                        for i in range(TB):
                            ins = pe.transpose(bank[2 * half + k][:, i * P:(i + 1) * P],
                                               xs[:, half, i, k * P:(k + 1) * P], identf[:, :])
                        ins.then_inc(xpose_ready, 1)

        @block.gpsimd
        def _(pool):
            pool.sem_inc(kept, 2)
            if XN is not None:
                with pool.Fori(0, G // 2) as m:
                    for half in range(2):
                        g = m * 2 + half
                        wait_alone(pool, norm_ready, g + 1, passed)
                        pool.tensor_copy(XN[:, ds(g * TB, TB), :], xs[:, half, :, :]).then_inc(kept, 1)


def constants_stage(nc, x, cos, sin, X, identf, ident16, identb, upper_neg, cosr, sinr):
    with ExitStack() as ctx:
        t = Tensors(nc, ctx, "const")
        loaded, cleared, made = t.sem("loaded"), t.sem("cleared"), t.sem("made")
        block = t.block()

        @block.sync
        def _(sp):
            sp.dma_start(X[:, :, :], x.rearrange("b (t p) d -> p (b t) d", p=P)).then_inc(loaded, 16)
            sp.dma_start(cosr[:, :, :], cos.rearrange("(t p) f -> p t f", p=P)).then_inc(loaded, 16)
            sp.dma_start(sinr[:, :, :], sin.rearrange("(t p) f -> p t f", p=P)).then_inc(loaded, 16)
            sp.wait_ge(loaded, 48)

        @block.gpsimd
        def _(pool):
            pool.memset(identf[:, :], 0.0).then_inc(cleared, 1)
            pool.memset(upper_neg[:, :], 0.0).then_inc(cleared, 1)
            pool.wait_ge(cleared, 2)
            pool.affine_select(out=identf[:, :], in_=identf[:, :], compare_op=ALU.not_equal, fill=1.0, base=0,
                               pattern=[[-1, P]], channel_multiplier=1).then_inc(made, 1)
            pool.affine_select(out=upper_neg[:, :], in_=upper_neg[:, :], compare_op=ALU.is_ge, fill=-1e30, base=0,
                               pattern=[[-1, P]], channel_multiplier=1).then_inc(made, 1)
            pool.wait_ge(made, 2)
            pool.tensor_copy(ident16[:, :], identf[:, :]).then_inc(made, 1)
            pool.tensor_copy(identb[:, :], identf[:, :]).then_inc(made, 1)
            pool.wait_ge(made, 4)


def split_weights(nc, stage, parts):
    with ExitStack() as ctx:
        t = Tensors(nc, ctx, stage)
        staged = [t.sb(f"staged{i}", list(high.shape)) for i, (_, high, _) in enumerate(parts)]
        loaded = [t.sem(f"loaded{i}") for i in range(len(parts))]
        high_ready, low_ready = t.sem("high_ready"), t.sem("low_ready")
        block = t.block()

        def whole(a):
            return a[tuple(slice(None) for _ in a.shape)]

        @block.sync
        def _(sp):
            for i, (src, _, _) in enumerate(parts):
                sp.dma_start(whole(staged[i]), src).then_inc(loaded[i], 16)

        @block.scalar
        def _(act):
            for i, (_, high, _) in enumerate(parts):
                act.wait_ge(loaded[i], 16)
                act.activation(whole(high), whole(staged[i]), ACT.Copy).then_inc(high_ready, 1)

        @block.vector
        def _(dve):
            for i, (_, high, low) in enumerate(parts):
                dve.wait_ge(high_ready, i + 1)
                dve.tensor_tensor(whole(low), whole(staged[i]), whole(high), ALU.subtract).then_inc(low_ready, 1)


def attention_stage(nc, X, XTh, XTl, weights, identf, ident16, identb, upper_neg, cosr, sinr):
    (wqh, wql), (wdh, wdl), (wkh, wkl), (wuh, wul), (woh, wol) = weights
    with ExitStack() as ctx:
        t = Tensors(nc, ctx, "att")
        QR = t.sb("QR", [P, TB, NH + 1, HD])
        rot = t.sb("rot", [P, 2, NH + 1, DR])
        ckh, ckl = t.sb("ckh", [LAT, S], F16), t.sb("ckl", [LAT, S], F16)
        KN = t.sb("KN", [P, TB, NH, DH])
        vh, vl = t.sb("vh", [P, TB, NH, DH], F16), t.sb("vl", [P, TB, NH, DH], F16)
        qks = t.sb("qks", [P, 2, 2, 2, TB, HD], F16)
        qkT = t.sb("qkT", [HD, 2, 2, 2, S], F16)
        prob = t.sb("prob", [P, 2, 10 * P])
        pth, ptl = t.sb("pth", [P, 2, 10 * P], F16), t.sb("ptl", [P, 2, 10 * P], F16)
        nmax = t.sb("nmax", [P, 2, TB])
        rsum = t.sb("rsum", [P, 2, TB])
        rinv = t.sb("rinv", [P, TB])
        O = t.sb("O", [P, TB, D])
        oTh, oTl = t.sb("oTh", [P, KD, S], F16), t.sb("oTl", [P, KD, S], F16)
        bank = t.banks()
        sem = t.sem
        lat_ready, lat_high, lat_low = sem("lat_ready"), sem("lat_high"), sem("lat_low")
        q_ready, kv_ready = sem("q_ready"), sem("kv_ready")
        q_copied, kv_copied, v_low = sem("q_copied"), sem("kv_copied"), sem("v_low")
        rot_ready, roped, ordered = sem("rot_ready"), sem("roped"), sem("ordered")
        pool_ordered, passed = sem("pool_ordered"), sem("passed")
        split_ready, qkT_ready, qkT_copied = sem("split_ready"), sem("qkT_ready"), sem("qkT_copied")
        score_ready, max_ready, prob_ready = sem("score_ready"), sem("max_ready"), sem("prob_ready")
        pT_ready, pT_high, pT_low = sem("pT_ready"), sem("pT_high"), sem("pT_low")
        out_ready, out_copied = sem("out_ready"), sem("out_copied")
        oT_ready, oT_high, oT_low = sem("oT_ready"), sem("oT_high"), sem("oT_low")
        proj_ready, added = sem("proj_ready"), sem("added")
        block = t.block()

        q_cols = [(0, 6), (6, 12), (12, 16)]
        KR_AT = 384

        def proj_banks(i):
            return ([bank[1], bank[2], bank[3]], bank[4]) if i % 2 == 0 else ([bank[5], bank[6], bank[7]], bank[0])

        units = [(2, [(3, 0)]), (3, [(2, 0)]), (4, [(1, 0), (0, 2 * P)])]
        p_at = {3: 0, 2: 4 * P, 1: 7 * P, 0: 9 * P}
        chunks = [(0, 4 * P), (4 * P, 3 * P), (7 * P, 3 * P)]

        def over_heads(eng, g0, head):
            head(g0, 0, 0, False, True, True)
            with eng.Fori(0, NH // 2 - 2) as m:
                for step in range(2):
                    head(g0 + m * 2 + (1 + step), m * 2 + (1 + step), 1 - step, True, True, True)
            head(g0 + NH - 3, NH - 3, 1, True, True, True)
            head(g0 + NH - 2, NH - 2, 0, True, True, False)
            head(g0 + NH - 1, NH - 1, 1, True, False, False)

        @block.tensor
        def _(pe):
            pe.sem_inc(qkT_ready, 4)

            def project(b):
                for k in range(KD):
                    tok = ds(b * S, S)
                    ins = product3(pe, bank[0][0:LAT, :], (wdh[:, k, :], wdl[:, k, :]), (XTh[:, k, tok], XTl[:, k, tok]),
                                   k == 0, k == KD - 1)
                ins.then_inc(lat_ready, 1)
                for i in range(TB):
                    qb, kvb = proj_banks(i)
                    tok = ds(b * S + i * P, P)
                    if i >= 2:
                        pe.wait_ge(q_copied, b * TB + i - 1)
                    for n, (h0, h1) in enumerate(q_cols):
                        for k in range(KD):
                            ins = product3(pe, qb[n][:, 0:(h1 - h0) * HD], (XTh[:, k, tok], XTl[:, k, tok]),
                                           (wqh[:, k, h0 * HD:h1 * HD], wql[:, k, h0 * HD:h1 * HD]), k == 0, k == KD - 1)
                    for k in range(KD):
                        ins = product3(pe, qb[2][:, KR_AT:KR_AT + DR], (XTh[:, k, tok], XTl[:, k, tok]),
                                       (wkh[:, k, :], wkl[:, k, :]), k == 0, k == KD - 1)
                    ins.then_inc(q_ready, 1)
                    if i == 0:
                        pe.wait_ge(lat_low, b + 1)
                    if i >= 2:
                        pe.wait_ge(v_low, b * TB + i - 1)
                    product3(pe, kvb[:, :], (ckh[:, i * P:(i + 1) * P], ckl[:, i * P:(i + 1) * P]),
                             (wuh[:, :], wul[:, :]), True, True).then_inc(kv_ready, 1)

            def transpose_qk(g, par):
                pe.wait_ge(split_ready, g + 1)
                pe.wait_ge(qkT_copied, 2 * g + 1)
                for x in range(2):
                    pe.wait_ge(qkT_copied, 2 * g + x + 1)
                    out = bank[x][0:HD, :].bitcast(F16)
                    for part in range(2):
                        for i in range(TB):
                            ins = pe.transpose(out[:, (part * TB + i) * P:(part * TB + i + 1) * P],
                                               qks[:, par, x, part, i, :], ident16[:, :])
                    ins.then_inc(qkT_ready, 1)

            def scores(g, par, us=(0, 1, 2)):
                if us[0] == 0:
                    pe.wait_ge(qkT_copied, 2 * g + 4)
                for u in us:
                    bk, tiles = units[u]
                    pe.wait_ge(prob_ready, 3 * g + u + 1)
                    for i, at in tiles:
                        n = (i + 1) * P
                        out = bank[bk][:, at:at + n]
                        q = qkT[:, par, 0, :, i * P:(i + 1) * P]
                        kk = qkT[:, par, 1, :, 0:n]
                        product3(pe, out, (q[:, 0, :], q[:, 1, :]), (kk[:, 0, :], kk[:, 1, :]), True, False)
                        ins = pe.matmul(out[:, n - P:n], identb[:, :], upper_neg[:, :], start=False, stop=True)
                    ins.then_inc(score_ready, 1)

            def transpose_probs(g, par, cs):
                for c in cs:
                    at, n = chunks[c]
                    pe.wait_ge(prob_ready, 3 * g + c + 4)
                    pe.wait_ge(pT_low, 3 * g + c + 1)
                    bk = bank[5 + (3 * par + c) % 2]
                    for j in range(n // P):
                        ins = pe.transpose(bk[:, j * P:(j + 1) * P], prob[:, par, at + j * P:at + (j + 1) * P], identf[:, :])
                    ins.then_inc(pT_ready, 1)

            def weigh_values(g, h, par):
                pe.wait_ge(pT_low, 3 * g + 3 + 2)
                pe.wait_ge(out_copied, g + 1)
                for i in range(TB):
                    for j in range(i + 1):
                        at = p_at[i] + j * P
                        ins = product3(pe, bank[7][:, i * DH:(i + 1) * DH],
                                       (pth[:, par, at:at + P], ptl[:, par, at:at + P]),
                                       (vh[:, j, ds(h, 1), :].rearrange("p a d -> p (a d)"),
                                        vl[:, j, ds(h, 1), :].rearrange("p a d -> p (a d)")), j == 0, j == i)
                ins.then_inc(out_ready, 1)

            def head(g, h, par, before, after, after2):
                transpose_probs(g, par, (0,))
                transpose_probs(g, par, (1,))
                if after:
                    scores(g + 1, 1 - par, (0,))
                if before:
                    weigh_values(g - 1, h - 1, 1 - par)
                if after:
                    scores(g + 1, 1 - par, (1,))
                transpose_probs(g, par, (2,))
                if after:
                    scores(g + 1, 1 - par, (2,))
                if after2:
                    transpose_qk(g + 2, par)

            with pe.Fori(0, B) as b:
                pe.wait_ge(added, b * TB + 1)
                project(b)
                pe.wait_ge(q_copied, b * TB + TB)
                pe.wait_ge(v_low, b * TB + TB)
                g0 = b * NH
                transpose_qk(g0, 0)
                scores(g0, 0)
                transpose_qk(g0 + 1, 1)
                over_heads(pe, g0, head)
                weigh_values(g0 + NH - 1, NH - 1, 1)
                pe.wait_ge(out_copied, g0 + NH + 1)
                for k in range(KD):
                    for i in range(TB):
                        ins = pe.transpose(bank[k][:, i * P:(i + 1) * P], O[:, i, k * P:(k + 1) * P], identf[:, :])
                    ins.then_inc(oT_ready, 1)
                pe.wait_ge(oT_low, KD * b + KD)
                for i in range(TB):
                    for k in range(KD):
                        tok = slice(i * P, (i + 1) * P)
                        ins = product3(pe, bank[2 + i][:, 0:D], (oTh[:, k, tok], oTl[:, k, tok]),
                                       (woh[:, k, :], wol[:, k, :]), k == 0, k == KD - 1)
                    ins.then_inc(proj_ready, 1)

        @block.scalar
        def _(act):
            act.sem_inc(prob_ready, 3)

            def probs(g, par, us=(0, 1, 2)):
                for u in us:
                    bk, tiles = units[u]
                    act.wait_ge(max_ready, 3 * g + u + 1)
                    for i, at in tiles:
                        n = (i + 1) * P
                        ins = act.activation(prob[:, par, p_at[i]:p_at[i] + n], bank[bk][:, at:at + n], ACT.Exp,
                                             bias=nmax[:, par, i:i + 1], accum_out=rsum[:, par, i:i + 1])
                    ins.then_inc(prob_ready, 1)

            def high_probs(g, par, cs):
                for c in cs:
                    at, n = chunks[c]
                    act.wait_ge(pT_ready, 3 * g + c + 1)
                    act.activation(pth[:, par, at:at + n], bank[5 + (3 * par + c) % 2][:, 0:n], ACT.Copy).then_inc(pT_high, 1)

            def head(g, h, par, before, after, after2):
                high_probs(g, par, (0,))
                probs(g, par, (2,))
                high_probs(g, par, (1,))
                if after:
                    probs(g + 1, 1 - par, (0,))
                high_probs(g, par, (2,))
                if after:
                    probs(g + 1, 1 - par, (1,))

            with act.Fori(0, B) as b:
                act.wait_ge(lat_ready, b + 1)
                act.activation(ckh[:, :], bank[0][0:LAT, :], ACT.Copy).then_inc(lat_high, 1)
                for i in range(TB):
                    qb, kvb = proj_banks(i)
                    act.wait_ge(q_ready, b * TB + i + 1)
                    for n, (h0, h1) in enumerate(q_cols):
                        act.activation(QR[:, i, h0:h1, :], qb[n][:, 0:(h1 - h0) * HD].rearrange("p (h d) -> p h d", d=HD),
                                       ACT.Copy, scale=ATT_SCALE)
                    act.activation(QR[:, i, NH, DH:HD], qb[2][:, KR_AT:KR_AT + DR], ACT.Copy).then_inc(q_copied, 1)
                    act.wait_ge(kv_ready, b * TB + i + 1)
                    kv = kvb[:, :].rearrange("p (h x d) -> p h x d", x=2, d=DH)
                    act.activation(KN[:, i, :, :], kv[:, :, 0, :], ACT.Copy)
                    act.activation(vh[:, i, :, :], kv[:, :, 1, :], ACT.Copy).then_inc(kv_copied, 1)
                g0 = b * NH
                probs(g0, 0, (0, 1))
                over_heads(act, g0, head)
                for k in range(KD):
                    act.wait_ge(oT_ready, KD * b + k + 1)
                    act.activation(oTh[:, k, :], bank[k][:, :], ACT.Copy).then_inc(oT_high, 1)

        @block.vector
        def _(dve):
            dve.sem_inc(qkT_copied, 2)
            dve.sem_inc(pT_low, 2)
            dve.sem_inc(out_copied, 1)
            dve.sem_inc(added, 1)

            def copy_qkT(g, par):
                for x in range(2):
                    dve.wait_ge(qkT_ready, 2 * g + x + 5)
                    dve.tensor_copy(qkT[:, par, x, :, :].rearrange("p a n -> p (a n)"),
                                    bank[x][0:HD, :].bitcast(F16)).then_inc(qkT_copied, 1)

            def maxima(g, par, us=(0, 1, 2)):
                for u in us:
                    bk, tiles = units[u]
                    dve.wait_ge(score_ready, 3 * g + u + 1)
                    for i, at in tiles:
                        ins = dve.tensor_reduce(nmax[:, par, i:i + 1], bank[bk][:, at:at + (i + 1) * P], AX.X, ALU.max,
                                                negate=True)
                    ins.then_inc(max_ready, 1)

            def low_probs(g, par, cs):
                for c in cs:
                    at, n = chunks[c]
                    dve.wait_ge(pT_high, 3 * g + c + 1)
                    dve.tensor_tensor(ptl[:, par, at:at + n], bank[5 + (3 * par + c) % 2][:, 0:n], pth[:, par, at:at + n],
                                      ALU.subtract).then_inc(pT_low, 1)

            def invert_sums(g, par):
                dve.wait_ge(prob_ready, 3 * g + 6)
                link.base, link.n = g, 0
                link(dve.reciprocal(rinv[:, :], rsum[:, par, :]))

            def normalise(g, h):
                dve.wait_ge(out_ready, g + 1)
                dve.tensor_tensor(O[:, :, ds(h * DH, DH)], bank[7][:, 0:TB * DH].rearrange("p (i d) -> p i d", d=DH),
                                  rinv[:, :].unsqueeze(2).broadcast_to([P, TB, DH]), ALU.mult).then_inc(out_copied, 1)

            def head(g, h, par, before, after, after2):
                low_probs(g, par, (0,))
                if after:
                    maxima(g + 1, 1 - par, (0,))
                low_probs(g, par, (1,))
                if before:
                    normalise(g - 1, h - 1)
                if after:
                    maxima(g + 1, 1 - par, (1,))
                low_probs(g, par, (2,))
                if after2:
                    copy_qkT(g + 2, par)
                dve.wait_ge(out_copied, g + 1)
                invert_sums(g, par)
                if after:
                    maxima(g + 1, 1 - par, (2,))

            link = Chain(dve, ordered)
            with dve.Fori(0, B) as b:
                dve.wait_ge(lat_high, b + 1)
                dve.tensor_tensor(ckl[:, :], bank[0][0:LAT, :], ckh[:, :], ALU.subtract).then_inc(lat_low, 1)
                for i in range(TB):
                    dve.wait_ge(q_copied, b * TB + i + 1)
                    dve.wait_ge(roped, b * TB + i + 1)
                    x = QR[:, i, :, DH:HD].rearrange("p h (x f) -> p h x f", x=2)
                    r = rot[:, i % 2, :, :].rearrange("p h (x f) -> p h x f", x=2)
                    for xx in range(2):
                        sn = sinr[:, i, :].unsqueeze(1).broadcast_to([P, NH + 1, HALF])
                        ins = dve.tensor_tensor(r[:, :, xx, :], x[:, :, xx, :], sn, ALU.mult)
                    ins.then_inc(rot_ready, 1)
                    dve.wait_ge(rot_ready, 2 * (b * TB + i) + 1)
                    for xx in range(2):
                        cs = cosr[:, i, :].unsqueeze(1).broadcast_to([P, NH + 1, HALF])
                        ins = dve.tensor_tensor(x[:, :, xx, :], x[:, :, xx, :], cs, ALU.mult)
                    ins.then_inc(rot_ready, 1)
                    _, kvb = proj_banks(i)
                    dve.wait_ge(kv_copied, b * TB + i + 1)
                    dve.tensor_tensor(vl[:, i, :, :], kvb[:, :].rearrange("p (h x d) -> p h x d", x=2, d=DH)[:, :, 1, :],
                                      vh[:, i, :, :], ALU.subtract).then_inc(v_low, 1)
                g0 = b * NH
                copy_qkT(g0, 0)
                maxima(g0, 0)
                copy_qkT(g0 + 1, 1)
                over_heads(dve, g0, head)
                normalise(g0 + NH - 1, NH - 1)
                for k in range(KD):
                    dve.wait_ge(oT_high, KD * b + k + 1)
                    dve.tensor_tensor(oTl[:, k, :], bank[k][:, :], oTh[:, k, :], ALU.subtract).then_inc(oT_low, 1)
                for i in range(TB):
                    dve.wait_ge(proj_ready, TB * b + i + 1)
                    xt = X[:, ds(b * TB + i, 1), :].rearrange("p a d -> p (a d)")
                    dve.tensor_tensor(xt, bank[2 + i][:, 0:D], xt, ALU.add).then_inc(added, 1)

        @block.gpsimd
        def _(pool):
            pool.sem_inc(roped, 2)
            link = Chain(pool, pool_ordered, passed)

            def split(g, h, par):
                wait_alone(pool, qkT_ready, 2 * g + 1, passed)
                wait_alone(pool, qkT_ready, 2 * g + 2, passed)
                q = QR[:, :, ds(h, 1), :].rearrange("p t a d -> p t (a d)")
                kn = KN[:, :, ds(h, 1), :].rearrange("p t a d -> p t (a d)")
                pool.tensor_copy(qks[:, par, 0, 0, :, :], q)
                link(pool.tensor_copy(qks[:, par, 1, 0, :, 0:DH], kn))
                pool.tensor_tensor(qks[:, par, 0, 1, :, :], q, qks[:, par, 0, 0, :, :], ALU.subtract)
                pool.tensor_tensor(qks[:, par, 1, 1, :, 0:DH], kn, qks[:, par, 1, 0, :, 0:DH],
                                   ALU.subtract).then_inc(split_ready, 1)

            PER = NH + 2
            with pool.Fori(0, B) as b:
                for i in range(TB):
                    wait_alone(pool, rot_ready, 2 * (b * TB + i) + 2, passed)
                    x = QR[:, i, :, DH:HD]
                    r = rot[:, i % 2, :, :]
                    pool.tensor_tensor(x[:, :, 0:HALF], x[:, :, 0:HALF], r[:, :, HALF:DR], ALU.subtract)
                    pool.tensor_tensor(x[:, :, HALF:DR], x[:, :, HALF:DR], r[:, :, 0:HALF], ALU.add).then_inc(roped, 1)
                wait_alone(pool, roped, b * TB + TB + 2, passed)
                wait_alone(pool, kv_copied, b * TB + TB, passed)
                wait_alone(pool, qkT_ready, 2 * (b * NH) + 4, passed)
                link.base, link.n = b * PER, 0
                for par in range(2):
                    ins = pool.tensor_copy(qks[:, par, 1, 0, :, DH:HD], QR[:, :, NH, DH:HD])
                link(ins)
                for par in range(2):
                    ins = pool.tensor_tensor(qks[:, par, 1, 1, :, DH:HD], QR[:, :, NH, DH:HD], qks[:, par, 1, 0, :, DH:HD],
                                             ALU.subtract)
                link(ins)
                with pool.Fori(0, NH // 2) as m:
                    for par in range(2):
                        link.base, link.n = b * PER + 2 + m * 2 + par, 0
                        split(b * NH + m * 2 + par, m * 2 + par, par)


NE, H1, TOPK = 8, 512, 2
ST = 2 * P
NSLOT = (B * S * TOPK + NE * (ST - 1)) // ST
KH = H1 // P
W2_AT, W3_AT = KD * H1, KD * H1 + KH * H1
WCOLS = W3_AT + KH * D


def expert_weights_stage(nc, stage, ins, WH, WL, b12, b3b):
    with ExitStack() as ctx:
        t = Tensors(nc, ctx, stage)
        staged = t.sb("staged", [P, 2, WCOLS])
        loaded = [t.sem(f"loaded{i}") for i in range(2)]
        high_ready, low_ready = t.sem("high_ready"), t.sem("low_ready")
        biases = t.sem("biases")
        block = t.block()

        @block.sync
        def _(sp):
            sp.dma_start(b12[:, 0, :], ins["L0_ffn_b1"].rearrange("e (m p) -> p (e m)", p=P),
                         allow_slow_non_contiguous=True).then_inc(biases, 16)
            sp.dma_start(b12[:, 1, :], ins["L0_ffn_b2"].rearrange("e (m p) -> p (e m)", p=P),
                         allow_slow_non_contiguous=True).then_inc(biases, 16)
            sp.dma_start(b3b[:, :, :], ins["L0_ffn_b3"].unsqueeze(0).broadcast_to([P, NE, D])).then_inc(biases, 16)
            with sp.Fori(0, NE // 2) as m:
                for half in range(2):
                    e = m * 2 + half
                    sp.wait_ge(low_ready, e + 1)
                    for name, k, n, at in (("L0_ffn_W1", KD, H1, 0), ("L0_ffn_W2", KH, H1, W2_AT), ("L0_ffn_W3", KH, D, W3_AT)):
                        src = ins[name][ds(e, 1), :, :].rearrange("e (k p) n -> p (e k) n", p=P)
                        sp.dma_start(staged[:, half, at:at + k * n].rearrange("p (k n) -> p k n", k=k), src).then_inc(loaded[half], 16)
            sp.wait_ge(biases, 48)

        @block.scalar
        def _(act):
            with act.Fori(0, NE // 2) as m:
                for half in range(2):
                    e = m * 2 + half
                    act.wait_ge(loaded[half], 48 * (m + 1))
                    act.activation(WH[:, ds(e * WCOLS, WCOLS)], staged[:, half, :], ACT.Copy).then_inc(high_ready, 1)

        @block.vector
        def _(dve):
            dve.sem_inc(low_ready, 2)
            with dve.Fori(0, NE // 2) as m:
                for half in range(2):
                    e = m * 2 + half
                    dve.wait_ge(high_ready, e + 1)
                    dve.tensor_tensor(WL[:, ds(e * WCOLS, WCOLS)], staged[:, half, :], WH[:, ds(e * WCOLS, WCOLS)],
                                      ALU.subtract).then_inc(low_ready, 1)


def routing_stage(nc, stage, ins, XTh, XTl, gate, slots, tile_expert):
    with ExitStack() as ctx:
        t = Tensors(nc, ctx, stage)
        wg, wgh, wgl = t.sb("wg", [P, KD, NE]), t.sb("wgh", [P, KD, NE], F16), t.sb("wgl", [P, KD, NE], F16)
        bg = t.sb("bg", [P, NE])
        grid = [P, NT, NE]
        expert_m8 = t.sb("expert_m8", grid)
        tile_start = t.sb("tile_start", [P, NSLOT])
        before = t.sb("before", [P, P], BF16)
        ones = t.sb("ones", [P, P], BF16)
        keep = t.sb("keep", [P, NE, NT])
        ones8 = t.sb("ones8", [P, NE])
        logit, prob, same, rest = (t.sb(n, grid) for n in ("logit", "prob", "same", "rest"))
        mask = [t.sb("mask0", grid), t.sb("mask1", grid)]
        both = t.sb("both", grid, BF16)
        col = t.sb("col", [P, NT])
        total, running = t.sb("total", [P, NE, NT]), t.sb("running", [P, NE, NT])
        padded_i = t.sb("padded_i", [P, NE], I32)
        padded, ends = t.sb("padded", [P, NE]), t.sb("ends", [P, NE])
        where = t.sb("where", grid)
        slot_f = t.sb("slot_f", [P, NT])
        past = t.sb("past", [P, NSLOT, NE])
        tile_e = t.sb("tile_e", [P, NSLOT])
        bank = t.banks(3)
        loaded, made, cleared = t.sem("loaded"), t.sem("made"), t.sem("cleared")
        wg_high, wg_ready, logits_ready = t.sem("wg_high"), t.sem("wg_ready"), t.sem("logits_ready")
        shifted, exp_ready, both_ready, ranks_ready = (t.sem(n) for n in ("shifted", "exp_ready", "both_ready", "ranks_ready"))
        ordered = t.sem("ordered")
        block = t.block()

        @block.sync
        def _(sp):
            sp.dma_start(wg[:, :, :], ins["L0_ffn_Wg"].rearrange("(k p) n -> p k n", p=P)).then_inc(loaded, 16)
            sp.dma_start(bg[:, :], ins["L0_ffn_bg"].unsqueeze(0).broadcast_to([P, NE])).then_inc(loaded, 16)

        @block.gpsimd
        def _(pool):
            pool.memset(before[:, :], 1.0).then_inc(cleared, 1)
            pool.memset(ones[:, :], 1.0).then_inc(made, 1)
            pool.memset(keep[:, :, :], 1.0).then_inc(cleared, 1)
            pool.memset(ones8[:, :], 1.0).then_inc(made, 1)
            pool.iota(expert_m8[:, :, :], [[0, NT], [1, NE]], base=-NE, channel_multiplier=0,
                      allow_small_or_imprecise_dtypes=True).then_inc(made, 1)
            pool.iota(tile_start[:, :], [[ST, NSLOT]], base=0, channel_multiplier=0,
                      allow_small_or_imprecise_dtypes=True).then_inc(made, 1)
            pool.wait_ge(cleared, 2)
            pool.memset(keep[:, :, 0:1], 0.0).then_inc(made, 1)
            pool.affine_select(out=before[:, :], in_=before[:, :], compare_op=ALU.is_gt, fill=0.0, base=0,
                               pattern=[[1, P]], channel_multiplier=-1).then_inc(made, 1)

        @block.scalar
        def _(act):
            act.wait_ge(loaded, 32)
            act.activation(wgh[:, :, :], wg[:, :, :], ACT.Copy).then_inc(wg_high, 1)
            act.wait_ge(shifted, 1)
            act.activation(prob[:, :, :], logit[:, :, :], ACT.Exp).then_inc(exp_ready, 1)

        @block.tensor
        def _(pe):
            pe.wait_ge(wg_ready, 1)
            with pe.Fori(0, NT) as n:
                for k in range(KD):
                    tok = ds(n * P, P)
                    ins_ = product3(pe, bank[0][:, ds(n * NE, NE)], (XTh[:, k, tok], XTl[:, k, tok]),
                                    (wgh[:, k, :], wgl[:, k, :]), k == 0, k == KD - 1)
                ins_.then_inc(logits_ready, 1)
            pe.wait_ge(made, 6)
            pe.wait_ge(both_ready, 1)
            flat = both[:, :, :].rearrange("p n e -> p (n e)")
            pe.matmul(bank[1][:, 0:NT * NE], before[:, :], flat, start=True, stop=True)
            pe.matmul(bank[2][:, 0:NT * NE], ones[:, :], flat, start=True, stop=True).then_inc(ranks_ready, 1)

        @block.vector
        def _(dve):
            link = Chain(dve, ordered)
            wide = lambda a: a.unsqueeze(2).broadcast_to(grid)
            dve.wait_ge(wg_high, 1)
            dve.tensor_tensor(wgl[:, :, :], wg[:, :, :], wgh[:, :, :], ALU.subtract).then_inc(wg_ready, 1)
            dve.wait_ge(logits_ready, NT)
            link(dve.tensor_tensor(logit[:, :, :], bank[0][:, 0:NT * NE].rearrange("p (n e) -> p n e", e=NE),
                                   bg[:, :].unsqueeze(1).broadcast_to(grid), ALU.add))
            link(dve.tensor_reduce(col[:, :], logit[:, :, :], AX.X, ALU.max))
            dve.tensor_tensor(logit[:, :, :], logit[:, :, :], wide(col[:, :]), ALU.subtract).then_inc(shifted, 1)
            dve.wait_ge(exp_ready, 1)
            link(dve.tensor_reduce(slot_f[:, :], prob[:, :, :], AX.X, ALU.add))
            link(dve.reciprocal(col[:, :], slot_f[:, :]))
            link(dve.tensor_tensor(prob[:, :, :], prob[:, :, :], wide(col[:, :]), ALU.mult))
            dve.wait_ge(made, 6)
            for k in range(TOPK):
                src = prob if k == 0 else rest
                link(dve.tensor_reduce(gate[:, :, k], src[:, :, :], AX.X, ALU.max))
                link(dve.tensor_tensor(same[:, :, :], src[:, :, :], wide(gate[:, :, k]), ALU.is_equal))
                link(dve.tensor_tensor(same[:, :, :], same[:, :, :], expert_m8[:, :, :], ALU.mult))
                link(dve.tensor_reduce(col[:, :], same[:, :, :], AX.X, ALU.min))
                link(dve.tensor_tensor(mask[k][:, :, :], expert_m8[:, :, :], wide(col[:, :]), ALU.is_equal))
                if k == 0:
                    link(dve.scalar_tensor_tensor(rest[:, :, :], mask[0][:, :, :], -2.0, prob[:, :, :], ALU.mult, ALU.add))
            dve.tensor_tensor(both[:, :, :], mask[0][:, :, :], mask[1][:, :, :], ALU.add).then_inc(both_ready, 1)
            dve.wait_ge(ranks_ready, 1)
            by_expert = "p (n e) -> p e n"
            link(dve.tensor_copy(total[:, :, :], bank[2][:, 0:NT * NE].rearrange(by_expert, e=NE)))
            flat = lambda a: a[:, :, :].rearrange("p e n -> p (e n)")
            link(dve.tensor_tensor_scan(flat(running), flat(keep), flat(total), 0.0, ALU.mult, ALU.add))
            link(dve.tensor_scalar(padded[:, :], running[:, :, NT - 1], float(ST - 1), None, ALU.add))
            link(dve.tensor_copy(padded_i[:, :], padded[:, :]))
            shift = ST.bit_length() - 1
            link(dve.tensor_scalar(padded_i[:, :], padded_i[:, :], shift, shift, ALU.logical_shift_right, ALU.logical_shift_left))
            link(dve.tensor_copy(padded[:, :], padded_i[:, :]))
            link(dve.tensor_tensor_scan(ends[:, :], ones8[:, :], padded[:, :], 0.0, ALU.mult, ALU.add))
            link(dve.tensor_tensor(padded[:, :], ends[:, :], padded[:, :], ALU.subtract))
            link(dve.tensor_tensor(running[:, :, :], running[:, :, :], total[:, :, :], ALU.subtract))
            link(dve.tensor_tensor(running[:, :, :], running[:, :, :], padded[:, :].unsqueeze(2).broadcast_to([P, NE, NT]), ALU.add))
            link(dve.tensor_tensor(where[:, :, :], bank[1][:, 0:NT * NE].rearrange("p (n e) -> p n e", e=NE),
                                   running[:, :, :].rearrange("p e n -> p n e"), ALU.add))
            for k in range(TOPK):
                link(dve.tensor_tensor(same[:, :, :], where[:, :, :], mask[k][:, :, :], ALU.mult))
                link(dve.tensor_reduce(slot_f[:, :], same[:, :, :], AX.X, ALU.add))
                link(dve.tensor_copy(slots[:, k, :], slot_f[:, :]))
            tiles = [P, NSLOT, NE]
            link(dve.tensor_tensor(past[:, :, :], tile_start[:, :].unsqueeze(2).broadcast_to(tiles),
                                   ends[:, :].unsqueeze(1).broadcast_to(tiles), ALU.is_ge))
            link(dve.tensor_reduce(tile_e[:, :], past[:, :, :], AX.X, ALU.add))
            link(dve.tensor_scalar(tile_e[:, :], tile_e[:, :], float(NE - 1), None, ALU.min))
            link(dve.tensor_copy(tile_expert[:, :], tile_e[:, :]))


def experts_stage(nc, stage, X, XN, WH, WL, b12, b3b, gate, slots, tile_expert, identf, sorted_x, sorted_y):
    RING = 8
    with ExitStack() as ctx:
        t = Tensors(nc, ctx, stage)
        xs = t.sb("xs", [P, 2, 2, D])
        xTh, xTl = t.sb("xTh", [P, KD, ST], F16), t.sb("xTl", [P, KD, ST], F16)
        h = [t.sb(f"h{n}", [P, KH, ST]) for n in range(2)]
        hh = [t.sb(f"hh{n}", [P, KH, ST], F16) for n in range(2)]
        hl = [t.sb(f"hl{n}", [P, KH, ST], F16) for n in range(2)]
        y = t.sb("y", [P, 2, 2, D])
        back = t.sb("back", [P, RING, D])
        bank = t.banks(6)
        scattered, passed = t.sem("scattered"), t.sem("passed")
        xs_loaded = [t.sem(f"xs_loaded{i}") for i in range(2)]
        xT_ready, xT_high, xT_low = t.sem("xT_ready"), t.sem("xT_high"), t.sem("xT_low")
        lin_ready = [t.sem(f"lin_ready{n}") for n in range(2)]
        gelu_ready = [t.sem(f"gelu_ready{n}") for n in range(2)]
        h_high, h_low = [t.sem(f"h_high{n}") for n in range(2)], [t.sem(f"h_low{n}") for n in range(2)]
        y_psum, y_ready = t.sem("y_psum"), t.sem("y_ready")
        y_stored = [t.sem(f"y_stored{i}") for i in range(2)]
        gathered = [t.sem(f"gathered{i}") for i in range(RING)]
        added, stored = t.sem("added"), t.sem("stored")
        block = t.block()
        NB = (NSLOT - 3) // 2
        rows_of = lambda dram, j: dram[ds(j * ST, ST), :].rearrange("(a p) d -> p a d", p=P)

        def tiles(eng, body):
            with eng.Fori(0, NB) as m:
                for par in range(2):
                    body(m * 2 + par, par, 2)
            for j in range(2 * NB, NSLOT):
                body(j, j % 2, min(2, NSLOT - 1 - j))

        @block.sync
        def _(sp):
            def load(j, par, ahead):
                sp.wait_ge(xT_ready, j + 1)
                sp.dma_start(xs[:, par, :, :], rows_of(sorted_x, j)).then_inc(xs_loaded[par], 16)

            def store(j, par):
                sp.wait_ge(y_ready, j + 2)
                sp.dma_start(rows_of(sorted_y, j), y[:, par, :, :]).then_inc(y_stored[par], 16)

            def body(j, par, ahead):
                if ahead >= 2:
                    load(j + 2, par, ahead)
                store(j, par)

            for par in range(2):
                sp.sem_inc(y_stored[par], 16)
            sp.wait_ge(scattered, 16 * TOPK * NT)
            load(0, 0, 2)
            load(1, 1, 2)
            tiles(sp, body)

        @block.gpsimd
        def _(pool):
            for n in range(NT):
                for k in range(TOPK):
                    pool.indirect_dma_start(out=sorted_x, out_offset=bass.IndirectOffsetOnAxis(ap=slots[:, k, n:n + 1], axis=0),
                                            in_=XN[:, n, :], in_offset=None).then_inc(scattered, 16)
            for par in range(2):
                pool.wait_ge(y_stored[par], 16 * ((NSLOT - par + 1) // 2) + 16)
            for n in range(NT):
                for k in range(TOPK):
                    i = n * TOPK + k
                    if i >= RING:
                        pool.wait_ge(added, i - RING + 1)
                    pool.indirect_dma_start(out=back[:, i % RING, :], out_offset=None, in_=sorted_y,
                                            in_offset=bass.IndirectOffsetOnAxis(ap=slots[:, k, n:n + 1], axis=0)
                                            ).then_inc(gathered[i % RING], 16)

        def expert_of(eng, j, scale):
            e = eng.value_load(tile_expert[0:1, ds(j, 1)] if not isinstance(j, int) else tile_expert[0:1, j:j + 1],
                               min_val=0, max_val=NE - 1)
            return e * scale

        @block.tensor
        def _(pe):
            pe.sem_inc(xT_ready, 2)

            def transpose_in(j, par):
                pe.wait_ge(xs_loaded[par], (j - par) * 8 + 16)
                for k in range(KD):
                    for a in range(2):
                        ins = pe.transpose(bank[0][:, k * ST + a * P:k * ST + (a + 1) * P], xs[:, par, a, k * P:(k + 1) * P],
                                           identf[:, :])
                ins.then_inc(xT_ready, 1)

            def layer1(j):
                w = expert_of(pe, j, WCOLS)
                pe.wait_ge(xT_low, j + 1)
                for m in range(KH):
                    for k in range(KD):
                        at = w + (k * H1 + m * P)
                        ins = product3(pe, bank[1 + m // 2][:, (m % 2) * ST:(m % 2 + 1) * ST],
                                       (WH[:, ds(at, P)], WL[:, ds(at, P)]), (xTh[:, k, :], xTl[:, k, :]), k == 0, k == KD - 1)
                    if m % 2:
                        ins.then_inc(lin_ready[0], 1)

            def layer2(j):
                w = expert_of(pe, j, WCOLS)
                pe.wait_ge(h_low[0], 2 * j + 2)
                for m in range(KH):
                    for k in range(KH):
                        at = w + (W2_AT + k * H1 + m * P)
                        ins = product3(pe, bank[3 + m // 2][:, (m % 2) * ST:(m % 2 + 1) * ST],
                                       (WH[:, ds(at, P)], WL[:, ds(at, P)]), (hh[0][:, k, :], hl[0][:, k, :]),
                                       k == 0, k == KH - 1)
                    if m % 2:
                        ins.then_inc(lin_ready[1], 1)

            def layer3(j):
                w = expert_of(pe, j, WCOLS)
                pe.wait_ge(h_low[1], 2 * j + 2)
                pe.wait_ge(y_ready, j + 1)
                for a in range(2):
                    for k in range(KH):
                        at = w + (W3_AT + k * D)
                        rows = slice(a * P, (a + 1) * P)
                        ins = product3(pe, bank[5][:, a * D:(a + 1) * D], (hh[1][:, k, rows], hl[1][:, k, rows]),
                                       (WH[:, ds(at, D)], WL[:, ds(at, D)]), k == 0, k == KH - 1)
                ins.then_inc(y_psum, 1)

            def body(j, par, ahead):
                layer2(j)
                if ahead >= 1:
                    layer1(j + 1)
                if ahead >= 2:
                    transpose_in(j + 2, par)
                layer3(j)

            transpose_in(0, 0)
            layer1(0)
            transpose_in(1, 1)
            tiles(pe, body)

        @block.scalar
        def _(act):
            def gelus(layer, j):
                e = expert_of(act, j, KH)
                bias = b12[:, layer, :]
                for u in range(2):
                    act.wait_ge(lin_ready[layer], 2 * j + u + 1)
                    for m in (2 * u, 2 * u + 1):
                        ins = act.activation(h[layer][:, m, :], bank[1 + 2 * layer + u][:, (m % 2) * ST:(m % 2 + 1) * ST],
                                             ACT.Gelu, bias=bias[:, ds(e + m, 1)])
                    ins.then_inc(gelu_ready[layer], 1)

            def high_in(j):
                act.wait_ge(xT_ready, j + 3)
                act.activation(xTh[:, :, :].rearrange("p k n -> p (k n)"), bank[0][:, :], ACT.Copy).then_inc(xT_high, 1)

            def body(j, par, ahead):
                gelus(1, j)
                if ahead >= 1:
                    gelus(0, j + 1)
                if ahead >= 2:
                    high_in(j + 2)

            high_in(0)
            gelus(0, 0)
            high_in(1)
            tiles(act, body)

        @block.vector
        def _(dve):
            dve.sem_inc(y_ready, 1)

            def low_in(j):
                dve.wait_ge(xT_high, j + 1)
                dve.tensor_tensor(xTl[:, :, :].rearrange("p k n -> p (k n)"), bank[0][:, :],
                                  xTh[:, :, :].rearrange("p k n -> p (k n)"), ALU.subtract).then_inc(xT_low, 1)

            def split(layer, j):
                for u in range(2):
                    dve.wait_ge(gelu_ready[layer], 2 * j + u + 1)
                    two = slice(2 * u, 2 * u + 2)
                    dve.tensor_copy(hh[layer][:, two, :], h[layer][:, two, :]).then_inc(h_high[layer], 1)
                    dve.wait_ge(h_high[layer], 2 * j + u + 1)
                    dve.tensor_tensor(hl[layer][:, two, :], h[layer][:, two, :], hh[layer][:, two, :],
                                      ALU.subtract).then_inc(h_low[layer], 1)

            def finish(j, par):
                e = expert_of(dve, j, 1)
                dve.wait_ge(y_psum, j + 1)
                dve.wait_ge(y_stored[par], (j - par) * 8 + 16)
                dve.tensor_tensor(y[:, par, :, :], bank[5][:, :].rearrange("p (a d) -> p a d", a=2),
                                  b3b[:, ds(e, 1), :].broadcast_to([P, 2, D]), ALU.add).then_inc(y_ready, 1)

            def body(j, par, ahead):
                split(1, j)
                if ahead >= 1:
                    split(0, j + 1)
                if ahead >= 2:
                    low_in(j + 2)
                finish(j, par)

            low_in(0)
            split(0, 0)
            low_in(1)
            tiles(dve, body)
            for i in range(NT * TOPK):
                dve.wait_ge(gathered[i % RING], 16 * (i // RING + 1))
                n, k = i // TOPK, i % TOPK
                if i:
                    dve.wait_ge(added, i)
                dve.scalar_tensor_tensor(X[:, n, :], back[:, i % RING, :], gate[:, n, k:k + 1], X[:, n, :],
                                         ALU.mult, ALU.add).then_inc(added, 1)


SH, SP_, SS, SK = 64, 8, 128, 4
SD = SH * SP_
CONV = SD + 2 * SS
CB = CONV // P
PROJ = SD + CONV + SH
XB = SD // P
LOG_TERMS = 8
UNSCALE = 2.0 ** -14


def ssm_weights_stage(nc, ins, wih, wil, wo, conv_w, conv_b, norm_w, dt_bias, neg_a, d_skip, eye4, one_hot):
    with ExitStack() as ctx:
        t = Tensors(nc, ctx, "ssmw")
        w = t.sb("w", [P, KD, PROJ])
        mup = t.sb("mup", [P, PROJ])
        a_log = t.sb("a_log", [SH, 1])
        d_row = t.sb("d_row", [P, SH])
        w_loaded, loaded = t.sem("w_loaded"), t.sem("loaded")
        scaled, high_ready, exp_ready, cleared = t.sem("scaled"), t.sem("high_ready"), t.sem("exp_ready"), t.sem("cleared")
        block = t.block()

        @block.sync
        def _(sp):
            col = lambda name: ins["L0_attn_b_" + name].unsqueeze(1)
            sp.dma_start(w[:, :, :], ins["L0_attn_b_W_in"].rearrange("(k p) n -> p k n", p=P)).then_inc(w_loaded, 16)
            sp.dma_start(mup[:, :], ins["L0_attn_b_mup_vector"].unsqueeze(0).broadcast_to([P, PROJ])).then_inc(w_loaded, 16)
            sp.dma_start(a_log[:, :], col("A_log")).then_inc(loaded, 16)
            sp.dma_start(dt_bias[:, :], col("dt_bias")).then_inc(loaded, 16)
            sp.dma_start(d_row[:, :], ins["L0_attn_b_D"].unsqueeze(0).broadcast_to([P, SH])).then_inc(loaded, 16)
            sp.dma_start(wo[:, :, :], ins["L0_attn_b_W_out"].rearrange("(k p) n -> p k n", p=P)).then_inc(loaded, 16)
            sp.dma_start(conv_w[:, :, :], ins["L0_attn_b_conv_w"].rearrange("(c p) k -> p c k", p=P)).then_inc(loaded, 16)
            sp.dma_start(conv_b[:, :], ins["L0_attn_b_conv_b"].rearrange("(c p) -> p c", p=P),
                         allow_slow_non_contiguous=True).then_inc(loaded, 16)
            sp.dma_start(norm_w[:, :], ins["L0_attn_b_norm_w"].rearrange("(c p) -> p c", p=P),
                         allow_slow_non_contiguous=True).then_inc(loaded, 16)
            sp.wait_ge(loaded, 7 * 16)

        @block.vector
        def _(dve):
            dve.wait_ge(w_loaded, 32)
            dve.tensor_tensor(w[:, :, :], w[:, :, :], mup[:, :].unsqueeze(1).broadcast_to([P, KD, PROJ]),
                              ALU.mult).then_inc(scaled, 1)
            dve.wait_ge(high_ready, 1)
            dve.tensor_tensor(wil[:, :, :], w[:, :, :], wih[:, :, :], ALU.subtract)
            dve.wait_ge(exp_ready, 1)
            dve.tensor_scalar(neg_a[:, :], a_log[:, :], -1.0, None, ALU.mult)
            dve.wait_ge(loaded, 7 * 16)
            dve.tensor_copy(d_skip[:, :, :], d_row[:, :].unsqueeze(2).broadcast_to([P, SH, SP_]))

        @block.scalar
        def _(act):
            act.wait_ge(loaded, 7 * 16)
            act.activation(a_log[:, :], a_log[:, :], ACT.Exp).then_inc(exp_ready, 1)
            act.wait_ge(scaled, 1)
            act.activation(wih[:, :, :], w[:, :, :], ACT.Copy).then_inc(high_ready, 1)

        @block.gpsimd
        def _(pool):
            pool.memset(eye4[:, :, :], 0.0).then_inc(cleared, 1)
            pool.memset(one_hot[:, :], 0.0).then_inc(cleared, 1)
            pool.wait_ge(cleared, 2)
            pool.affine_select(out=one_hot[:, :], in_=one_hot[:, :], compare_op=ALU.not_equal, fill=UNSCALE, base=0,
                               pattern=[[-1, SH]], channel_multiplier=1).then_inc(cleared, 1)
            pool.wait_ge(cleared, 3)
            pool.affine_select(out=one_hot[:, :], in_=one_hot[:, :], compare_op=ALU.not_equal, fill=UNSCALE, base=-SH,
                               pattern=[[-1, SH]], channel_multiplier=1)
            pool.affine_select(out=eye4[:, :, :], in_=eye4[:, :, :], compare_op=ALU.not_equal, fill=1.0, base=0,
                               pattern=[[0, TB], [-1, P]], channel_multiplier=1)


def ssm_stage(nc, X, XTh, XTl, weights, identf, identb):
    wih, wil, wo, conv_w, conv_b, norm_w, dt_bias, neg_a, d_skip, eye4, one_hot = weights
    RING = 4
    with ExitStack() as ctx:
        t = Tensors(nc, ctx, "ssm")
        sb, sem = t.sb, t.sem
        padded = sb("padded", [P, 2, S + SK - 1])
        taps = sb("taps", [P, 2, S])
        XC = sb("XC", [P, CB, S])
        zs = sb("zs", [P, TB, SD])
        u, e, zz, z2, poly = (sb(n, [SH, S]) for n in ("u", "e", "zz", "z2", "poly"))
        dT, dA, FT, starts = (sb(n, [SH, S]) for n in ("dT", "dA", "FT", "starts"))
        piece = sb("piece", [2 * SH, S], F16)
        xt, dtx = sb("xt", [P, TB, SD]), sb("dtx", [P, TB, SD])
        Bt = sb("Bt", [P, TB, SS])
        G = sb("G", [P, TB, P])
        dF = sb("dF", [P, TB, 2, SH])
        Ee = sb("Ee", [P, TB, SH])
        L, GL = sb("L", [P, RING, TB, P]), sb("GL", [P, RING, TB, P])
        edtx = sb("edtx", [P, SD])
        state = sb("state", [P, SD])
        dec = sb("dec", [P, SH])
        yv, gv, skip = sb("yv", [P, SD]), sb("gv", [P, SD]), sb("skip", [P, SD])
        square = sb("square", [P, SD])
        ssum, sd, rstd = sb("ssum", [P, TB]), sb("sd", [P, TB]), sb("rstd", [P, TB])
        gT = sb("gT", [P, XB, TB, P])
        bank = t.banks()
        names = ("padz conv_psum copied tapped silu z_psum z_done dt_psum dt_u dt_exp dt_done da_done da_ready ft_ready "
                 "piece_hi pieces xt_psum xt_done b_psum b_done df_psum df_done g_psum g_done dtx_done ordered passed "
                 "bc_ready scan_done mult_pool mult_dve e_done y_done inter_psum upd_psum dec_psum dec_done edtx_done skip_done "
                 "state_done gated sq_done gt_psum gt_done sd_done out_psum added chained pe_passed").split()
        s = {n: sem(n) for n in names}
        block = t.block()
        z0, dt0 = 0, SD + CONV

        def half_of(g, slot):
            return (g - slot) // 2 + slot // 2

        @block.tensor
        def _(pe):
            pe.sem_inc(s["y_done"], RING)
            with pe.Fori(0, B) as b:
                tok = ds(b * S, S)
                pe.wait_ge(s["added"], b * TB + 1)
                for c in range(CB):
                    if c >= 2:
                        pe.wait_ge(s["copied"], b * CB + c - 1)
                    for k in range(KD):
                        w = slice(SD + c * P, SD + (c + 1) * P)
                        ins = product3(pe, bank[c % 2][:, :], (wih[:, k, w], wil[:, k, w]), (XTh[:, k, tok], XTl[:, k, tok]),
                                       k == 0, k == KD - 1)
                    ins.then_inc(s["conv_psum"], 1)
                for k in range(KD):
                    w = slice(dt0, dt0 + SH)
                    ins = product3(pe, bank[4][0:SH, :], (wih[:, k, w], wil[:, k, w]), (XTh[:, k, tok], XTl[:, k, tok]),
                                   k == 0, k == KD - 1)
                ins.then_inc(s["dt_psum"], 1)
                for i in range(TB):
                    if i >= 2:
                        pe.wait_ge(s["z_done"], b * TB + i - 1)
                    one = ds(b * S + i * P, P)
                    for k in range(KD):
                        ins = product3(pe, bank[2 + i % 2][:, :], (XTh[:, k, one], XTl[:, k, one]),
                                       (wih[:, k, z0:z0 + SD], wil[:, k, z0:z0 + SD]), k == 0, k == KD - 1)
                    ins.then_inc(s["z_psum"], 1)
                pe.wait_ge(s["silu"], b * CB + XB)
                for i in range(TB):
                    if i >= 2:
                        pe.wait_ge(s["xt_done"], b * TB + i - 1)
                    for c in range(XB):
                        ins = pe.transpose(bank[5 + i % 2][:, c * P:(c + 1) * P], XC[:, c, i * P:(i + 1) * P], identf[:, :])
                    ins.then_inc(s["xt_psum"], 1)
                pe.wait_ge(s["silu"], b * CB + CB)
                for i in range(TB):
                    ins = pe.transpose(bank[7][:, i * P:(i + 1) * P], XC[:, XB, i * P:(i + 1) * P], identf[:, :])
                ins.then_inc(s["b_psum"], 1)
                pe.wait_ge(s["z_done"], b * TB + TB)
                for i in range(TB):
                    one = slice(i * P, (i + 1) * P)
                    ins = pe.matmul(bank[2][:, one], XC[:, XB, one], XC[:, XB + 1, one], start=True, stop=True)
                ins.then_inc(s["g_psum"], 1)
                wait_alone(pe, s["dt_done"], b + 1, s["pe_passed"])
                wait_alone(pe, s["ft_ready"], b + 1, s["pe_passed"])
                for i in range(TB):
                    one = slice(i * P, (i + 1) * P)
                    pe.transpose(bank[3][:, 2 * i * SH:(2 * i + 1) * SH], dT[:, one], identf[0:SH, 0:SH])
                    ins = pe.transpose(bank[3][:, (2 * i + 1) * SH:(2 * i + 2) * SH], FT[:, one], identf[0:SH, 0:SH])
                ins.then_inc(s["df_psum"], 1)

                g0 = b * SH

                def spread(g, h, slot):
                    pe.wait_ge(s["scan_done"], g + 1)
                    pe.matmul(bank[slot][:, :], one_hot[:, ds(h, 1)].broadcast_to([P, P]), piece[:, :], start=True,
                              stop=True).then_inc(s["bc_ready"], 1)

                def outputs(g, h, slot):
                    pe.wait_ge(s["mult_pool" if slot % 2 == 0 else "mult_dve"], half_of(g, slot) + RING // 2 + 1)
                    for i in range(TB):
                        ins = pe.matmul(bank[4 + i][:, ds(h * SP_, SP_)], GL[:, slot, i, :], dtx[:, i, ds(h * SP_, SP_)],
                                        start=True, stop=True)
                    ins.then_inc(s["y_done"], 1)

                pe.wait_ge(s["pieces"], b + 1)
                pe.wait_ge(s["copied"], b * CB + CB)
                spread(g0, 0, 0)
                spread(g0 + 1, 1, 1)
                pe.wait_ge(s["g_done"], b + 1)
                pe.wait_ge(s["df_done"], b + 1)
                pe.wait_ge(s["xt_done"], b * TB + TB)
                pe.wait_ge(s["b_done"], b + 1)
                wait_alone(pe, s["dtx_done"], b * TB + TB, s["pe_passed"])
                with pe.Fori(0, SH // RING - 1) as m:
                    for slot in range(RING):
                        h = m * RING + slot
                        spread(g0 + h + 2, h + 2, (slot + 2) % RING)
                        outputs(g0 + h, h, slot)
                for h in range(SH - RING, SH):
                    if h + 2 < SH:
                        spread(g0 + h + 2, h + 2, (h + 2) % RING)
                    outputs(g0 + h, h, h % RING)
                pe.wait_ge(s["scan_done"], g0 + SH + RING)
                for i in range(TB):
                    one = slice(i * P, (i + 1) * P)
                    if i > 0:
                        pe.wait_ge(s["state_done"], b * (TB - 1) + i)
                        pe.matmul(bank[0][:, :], XC[:, XB + 1, one], state[:, :], start=True, stop=True).then_inc(s["inter_psum"], 1)
                    if i < TB - 1:
                        pe.wait_ge(s["edtx_done"], b * (TB - 1) + i + 1)
                        pe.matmul(bank[1][:, :], Bt[:, i, :], edtx[:, :], start=True, stop=True).then_inc(s["upd_psum"], 1)
                        if i > 0:
                            pe.matmul(bank[2][:, 0:SH], identf[:, P - 1:P].broadcast_to([P, P]), dF[:, i, 1, :], start=True,
                                      stop=True).then_inc(s["dec_psum"], 1)
                    pe.wait_ge(s["gated"], b * TB + i + 1)
                    for c in range(XB):
                        ins = pe.transpose(bank[3][:, c * P:(c + 1) * P], gv[:, c * P:(c + 1) * P], identf[:, :])
                    ins.then_inc(s["gt_psum"], 1)
                    pe.wait_ge(s["gt_done"], b * TB + i + 1)
                    for c in range(XB):
                        ins = pe.matmul(bank[4 + i][:, 0:D], gT[:, c, i, :], wo[:, c, :], start=c == 0, stop=c == XB - 1)
                    ins.then_inc(s["out_psum"], 1)

        @block.scalar
        def _(act):
            act.sem_inc(s["e_done"], RING)
            with act.Fori(0, B) as b:
                for c in range(CB):
                    act.wait_ge(s["conv_psum"], b * CB + c + 1)
                    act.wait_ge(s["tapped"], b * CB + c + 1)
                    act.activation(padded[:, c % 2, SK - 1:], bank[c % 2][:, :], ACT.Copy).then_inc(s["copied"], 1)
                    if c >= 1:
                        act.wait_ge(s["tapped"], b * CB + c + 2)
                        act.activation(XC[:, c - 1, :], taps[:, (c - 1) % 2, :], ACT.Silu, bias=conv_b[:, c - 1:c]).then_inc(s["silu"], 1)
                act.wait_ge(s["tapped"], b * CB + CB + 2)
                act.activation(XC[:, CB - 1, :], taps[:, (CB - 1) % 2, :], ACT.Silu, bias=conv_b[:, CB - 1:CB]).then_inc(s["silu"], 1)
                for i in range(TB):
                    act.wait_ge(s["z_psum"], b * TB + i + 1)
                    act.activation(zs[:, i, :], bank[2 + i % 2][:, :], ACT.Silu).then_inc(s["z_done"], 1)
                act.wait_ge(s["dt_psum"], b + 1)
                act.activation(u[:, :], bank[4][0:SH, :], ACT.Identity, bias=dt_bias[:, :]).then_inc(s["chained"], 1)
                act.wait_ge(s["chained"], 2 * b + 1)
                act.activation(e[:, :], u[:, :], ACT.Abs).then_inc(s["chained"], 1)
                act.wait_ge(s["chained"], 2 * b + 2)
                act.activation(e[:, :], e[:, :], ACT.Exp, scale=-1.0).then_inc(s["dt_exp"], 1)
                act.wait_ge(s["dt_exp"], b + 1)
                act.activation(u[:, :], u[:, :], ACT.Relu).then_inc(s["dt_u"], 1)
                for i in range(TB):
                    act.wait_ge(s["xt_psum"], b * TB + i + 1)
                    act.activation(xt[:, i, :], bank[5 + i % 2][:, :], ACT.Copy).then_inc(s["xt_done"], 1)
                act.wait_ge(s["b_psum"], b + 1)
                act.activation(Bt[:, :, :].rearrange("p i n -> p (i n)"), bank[7][:, :], ACT.Copy).then_inc(s["b_done"], 1)
                act.wait_ge(s["g_psum"], b + 1)
                act.activation(G[:, :, :].rearrange("p i n -> p (i n)"), bank[2][:, :], ACT.Copy).then_inc(s["g_done"], 1)
                act.wait_ge(s["dt_done"], b + 1)
                act.activation(dA[:, :], dT[:, :], ACT.Exp, scale=neg_a[:, :]).then_inc(s["da_done"], 1)
                act.wait_ge(s["df_psum"], b + 1)
                act.activation(dF[:, :, :, :].rearrange("p i x h -> p (i x h)"), bank[3][:, :], ACT.Copy).then_inc(s["df_done"], 1)
                g0 = b * SH
                with act.Fori(0, SH // RING) as m:
                    for slot in range(RING):
                        h = m * RING + slot
                        act.wait_ge(s["scan_done"], g0 + h + RING + 1)
                        act.activation(Ee[:, :, ds(h, 1)], L[:, slot, :, P - 1:P], ACT.Copy).then_inc(s["e_done"], 1)
                for i in range(TB):
                    if 0 < i < TB - 1:
                        act.wait_ge(s["dec_psum"], b * (TB - 2) + i)
                        act.activation(dec[:, :], bank[2][:, 0:SH], ACT.Copy).then_inc(s["dec_done"], 1)
                    act.wait_ge(s["gated"], b * TB + i + 1)
                    act.activation(square[:, :], gv[:, :], ACT.Square, accum_out=ssum[:, i:i + 1]).then_inc(s["sq_done"], 1)
                    act.wait_ge(s["gt_psum"], b * TB + i + 1)
                    for c in range(XB):
                        ins = act.activation(gT[:, c, i, :], bank[3][:, c * P:(c + 1) * P], ACT.Copy, scale=norm_w[:, c:c + 1])
                    ins.then_inc(s["gt_done"], 1)
                act.wait_ge(s["sd_done"], 2 * b + 1)
                act.activation(sd[:, :], sd[:, :], ACT.Sqrt).then_inc(s["sd_done"], 1)

        @block.vector
        def _(dve):
            dve.sem_inc(s["tapped"], 2)
            dve.sem_inc(s["scan_done"], RING)
            dve.sem_inc(s["mult_dve"], RING // 2)
            dve.sem_inc(s["added"], 1)
            link = Chain(dve, s["ordered"])
            link(dve.memset(padded[:, :, 0:SK - 1], 0.0))
            link(dve.memset(starts[:, :], 0.0))
            first = link.n
            PER = CB * (SK - 1) + (LOG_TERMS + 5) + 2 + 2 + 1 + 3 * (TB - 1) + (TB - 2) + 1
            with dve.Fori(0, B) as b:
                link.base, link.n = b * PER + first, 0
                for c in range(CB):
                    dve.wait_ge(s["copied"], b * CB + c + 1)
                    if c >= 2:
                        dve.wait_ge(s["silu"], b * CB + c - 1)
                    x, acc = padded[:, c % 2, :], taps[:, c % 2, :]
                    link(dve.tensor_scalar(acc, x[:, 0:S], conv_w[:, c, 0:1], None, ALU.mult))
                    for k in range(1, SK):
                        ins = dve.scalar_tensor_tensor(acc, x[:, k:k + S], conv_w[:, c, k:k + 1], acc, ALU.mult, ALU.add)
                        if k < SK - 1:
                            link(ins)
                    ins.then_inc(s["tapped"], 1)
                dve.wait_ge(s["dt_exp"], b + 1)
                link(dve.tensor_scalar(zz[:, :], e[:, :], 2.0, None, ALU.add))
                link(dve.reciprocal(zz[:, :], zz[:, :]))
                link(dve.tensor_tensor(zz[:, :], zz[:, :], e[:, :], ALU.mult))
                link(dve.tensor_tensor(z2[:, :], zz[:, :], zz[:, :], ALU.mult))
                link(dve.tensor_scalar(poly[:, :], z2[:, :], 1.0 / (2 * LOG_TERMS + 1), None, ALU.mult))
                for k in range(LOG_TERMS - 1, 0, -1):
                    link(dve.scalar_tensor_tensor(poly[:, :], poly[:, :], 1.0 / (2 * k + 1), z2[:, :], ALU.add, ALU.mult))
                link(dve.scalar_tensor_tensor(poly[:, :], poly[:, :], 1.0, zz[:, :], ALU.add, ALU.mult))
                dve.wait_ge(s["dt_u"], b + 1)
                dve.scalar_tensor_tensor(dT[:, :], poly[:, :], 2.0, u[:, :], ALU.mult, ALU.add).then_inc(s["dt_done"], 1)
                dve.wait_ge(s["dt_done"], b + 1)
                dve.wait_ge(s["da_done"], b + 1)
                first_steps = lambda a: a.rearrange("p (i n) -> p i n", n=P)[:, :, 0:1]
                link(dve.tensor_copy(first_steps(starts[:, :]), first_steps(dA[:, :])))
                link(dve.memset(first_steps(dA[:, :]), 0.0))
                dve.tensor_tensor_scan(FT[:, :], dA[:, :], starts[:, :], 0.0, ALU.mult, ALU.add).then_inc(s["ft_ready"], 1)
                link(dve.tensor_scalar(poly[:, :], dA[:, :], 1.0 / UNSCALE, None, ALU.mult))
                link(dve.tensor_copy(piece[0:SH, :], poly[:, :]))
                dve.tensor_tensor(piece[SH:2 * SH, :], poly[:, :], piece[0:SH, :], ALU.subtract).then_inc(s["pieces"], 1)
                g0 = b * SH
                flat = lambda a: a.rearrange("p i n -> p (i n)")
                with dve.Fori(0, SH // RING) as m:
                    for slot in range(RING):
                        g = g0 + m * RING + slot
                        dve.wait_ge(s["bc_ready"], g + 1)
                        dve.wait_ge(s["mult_pool" if slot % 2 == 0 else "mult_dve"], half_of(g, slot) + 1)
                        dve.wait_ge(s["e_done"], g + 1)
                        dve.tensor_tensor_scan(flat(L[:, slot, :, :]), bank[slot][:, :], flat(eye4[:, :, :]), 0.0,
                                               ALU.mult, ALU.add).then_inc(s["scan_done"], 1)
                        if slot % 2:
                            dve.wait_ge(s["scan_done"], g + RING + 1)
                            dve.wait_ge(s["g_done"], b + 1)
                            dve.wait_ge(s["y_done"], g + 1)
                            dve.tensor_tensor(GL[:, slot, :, :], L[:, slot, :, :], G[:, :, :], ALU.mult).then_inc(s["mult_dve"], 1)
                for i in range(TB):
                    if i == 0:
                        dve.wait_ge(s["upd_psum"], b * (TB - 1) + 1)
                        dve.wait_ge(s["y_done"], g0 + SH + RING)
                        dve.tensor_copy(state[:, :], bank[1][:, :]).then_inc(s["state_done"], 1)
                        dve.wait_ge(s["skip_done"], b * TB + i + 1)
                        link(dve.tensor_tensor(yv[:, :], bank[4 + i][:, :], skip[:, :], ALU.add))
                    else:
                        dve.wait_ge(s["inter_psum"], b * (TB - 1) + i)
                        per_head = lambda a: a.rearrange("p (h q) -> p h q", q=SP_)
                        link(dve.tensor_tensor(per_head(yv[:, :]), per_head(bank[0][:, :]),
                                               dF[:, i, 1, :].unsqueeze(2).broadcast_to([P, SH, SP_]), ALU.mult))
                        if i < TB - 1:
                            dve.wait_ge(s["dec_done"], b * (TB - 2) + i)
                            link(dve.tensor_tensor(per_head(state[:, :]), per_head(state[:, :]),
                                                   dec[:, :].unsqueeze(2).broadcast_to([P, SH, SP_]), ALU.mult))
                            dve.wait_ge(s["upd_psum"], b * (TB - 1) + i + 1)
                            dve.tensor_tensor(state[:, :], state[:, :], bank[1][:, :], ALU.add).then_inc(s["state_done"], 1)
                        link(dve.tensor_tensor(yv[:, :], yv[:, :], bank[4 + i][:, :], ALU.add))
                        dve.wait_ge(s["skip_done"], b * TB + i + 1)
                        link(dve.tensor_tensor(yv[:, :], yv[:, :], skip[:, :], ALU.add))
                    if i:
                        dve.wait_ge(s["gt_psum"], b * TB + i)
                        dve.wait_ge(s["sq_done"], b * TB + i)
                    dve.tensor_tensor(gv[:, :], yv[:, :], zs[:, i, :], ALU.mult).then_inc(s["gated"], 1)
                    dve.wait_ge(s["gated"], b * TB + i + 1)
                dve.wait_ge(s["sq_done"], b * TB + TB)
                dve.tensor_scalar(sd[:, :], ssum[:, :], 1.0 / SD, EPS, ALU.mult, ALU.add).then_inc(s["sd_done"], 1)
                dve.wait_ge(s["sd_done"], 2 * b + 2)
                link(dve.reciprocal(rstd[:, :], sd[:, :]))
                for i in range(TB):
                    dve.wait_ge(s["out_psum"], b * TB + i + 1)
                    x = X[:, ds(b * TB + i, 1), :].rearrange("p a d -> p (a d)")
                    dve.scalar_tensor_tensor(x, bank[4 + i][:, 0:D], rstd[:, i:i + 1], x, ALU.mult, ALU.add).then_inc(s["added"], 1)
                assert link.n == PER, (link.n, PER)

        @block.gpsimd
        def _(pool):
            per_head = lambda a: a.rearrange("p (h q) -> p h q", q=SP_)
            wide = lambda a: a.unsqueeze(2).broadcast_to([P, SH, SP_])
            pool.sem_inc(s["mult_pool"], RING // 2)
            with pool.Fori(0, B) as b:
                wait_alone(pool, s["df_done"], b + 1, s["passed"])
                for i in range(TB):
                    wait_alone(pool, s["xt_done"], b * TB + i + 1, s["passed"])
                    pool.tensor_tensor(per_head(dtx[:, i, :]), per_head(xt[:, i, :]), wide(dF[:, i, 0, :]),
                                       ALU.mult).then_inc(s["dtx_done"], 1)
                wait_alone(pool, s["g_done"], b + 1, s["passed"])
                g0 = b * SH
                with pool.Fori(0, SH // RING) as m:
                    for slot in range(0, RING, 2):
                        g = g0 + m * RING + slot
                        wait_alone(pool, s["scan_done"], g + RING + 1, s["passed"])
                        wait_alone(pool, s["y_done"], g + 1, s["passed"])
                        pool.tensor_tensor(GL[:, slot, :, :], L[:, slot, :, :], G[:, :, :], ALU.mult).then_inc(s["mult_pool"], 1)
                wait_alone(pool, s["e_done"], g0 + SH + RING, s["passed"])
                for i in range(TB):
                    if i:
                        wait_alone(pool, s["gated"], b * TB + i, s["passed"])
                    pool.tensor_tensor(skip[:, :], xt[:, i, :], d_skip[:, :, :].rearrange("p h q -> p (h q)"),
                                       ALU.mult).then_inc(s["skip_done"], 1)
                    if i < TB - 1:
                        if i:
                            wait_alone(pool, s["upd_psum"], b * (TB - 1) + i, s["passed"])
                        pool.tensor_tensor(per_head(edtx[:, :]), per_head(dtx[:, i, :]), wide(Ee[:, i, :]),
                                           ALU.mult).then_inc(s["edtx_done"], 1)


def ssm_layer(nc, ins, X, c):
    with ExitStack() as ctx:
        t = Tensors(nc, ctx, "ssml")
        XTh, XTl = t.sb("XTh", [P, KD, B * S], F16), t.sb("XTl", [P, KD, B * S], F16)
        weights = (t.sb("wih", [P, KD, PROJ], F16), t.sb("wil", [P, KD, PROJ], F16), t.sb("wo", [P, XB, D]),
                   t.sb("conv_w", [P, CB, SK]), t.sb("conv_b", [P, CB]), t.sb("norm_w", [P, XB]), t.sb("dt_bias", [SH, 1]),
                   t.sb("neg_a", [SH, 1]), t.sb("d_skip", [P, SH, SP_]), t.sb("eye4", [P, TB, P]), t.sb("one_hot", [P, SH], F16))
        ssm_weights_stage(nc, ins, *weights)
        layer_norm_stage(nc, "ln2", X, None, XTh, XTl, c["identf"])
        ssm_stage(nc, X, XTh, XTl, weights, c["identf"], c["identb"])


def store_stage(nc, X, out):
    with ExitStack() as ctx:
        t = Tensors(nc, ctx, "store")
        stored = t.sem("stored")
        block = t.block()

        @block.sync
        def _(sp):
            sp.dma_start(out.rearrange("b (t p) d -> p (b t) d", p=P), X[:, :, :]).then_inc(stored, 16)
            sp.wait_ge(stored, 16)


def attention_layer(nc, ins, X, c):
    with ExitStack() as ctx:
        t = Tensors(nc, ctx, "attw")
        pair = lambda name, shape: (t.sb(name + "h", shape, F16), t.sb(name + "l", shape, F16))
        XTh, XTl = pair("XT", [P, KD, B * S])
        wq, wd, wk = pair("wq", [P, KD, NH * HD]), pair("wd", [P, KD, LAT]), pair("wk", [P, KD, DR])
        wu, wo = pair("wu", [LAT, NH * 2 * DH]), pair("wo", [P, KD, D])
        rows = lambda a: a.rearrange("(k p) n -> p k n", p=P)
        split_weights(nc, "attsplit", [
            (rows(ins["L0_attn_a_Wq"]), *wq), (rows(ins["L0_attn_a_Wdkv"]), *wd), (rows(ins["L0_attn_a_Wkr"]), *wk),
            (ins["L0_attn_a_Wukv"], *wu), (rows(ins["L0_attn_a_Wo"]), *wo)])
        layer_norm_stage(nc, "ln0", X, None, XTh, XTl, c["identf"])
        attention_stage(nc, X, XTh, XTl, (wq, wd, wk, wu, wo), c["identf"], c["ident16"], c["identb"], c["upper_neg"],
                        c["cosr"], c["sinr"])


def zero_rows_stage(nc, sorted_x):
    with ExitStack() as ctx:
        t = Tensors(nc, ctx, "zero")
        zeros = t.sb("zeros", [P, D])
        cleared, stored = t.sem("cleared"), t.sem("stored")
        block = t.block()
        n = NSLOT * ST // P

        @block.vector
        def _(dve):
            dve.memset(zeros[:, :], 0.0).then_inc(cleared, 1)

        @block.sync
        def _(sp):
            sp.wait_ge(cleared, 1)
            sp.dma_start(sorted_x.rearrange("(n p) d -> p n d", p=P),
                         zeros[:, :].unsqueeze(1).broadcast_to([P, n, D])).then_inc(stored, 16)
            sp.wait_ge(stored, 16)


def ffn_layer(nc, stage, ins, X, experts, sorted_x, sorted_y, c):
    with ExitStack() as ctx:
        t = Tensors(nc, ctx, stage)
        XN = t.sb("XN", [P, NT, D])
        gate = t.sb("gate", [P, NT, TOPK])
        slots = t.sb("slots", [P, TOPK, NT], I32)
        tile_expert = t.sb("tile_expert", [P, NSLOT], I32)
        with ExitStack() as inner:
            t = Tensors(nc, inner, stage + "t")
            XTh, XTl = t.sb("XTh", [P, KD, B * S], F16), t.sb("XTl", [P, KD, B * S], F16)
            layer_norm_stage(nc, stage + "ln", X, XN, XTh, XTl, c["identf"])
            routing_stage(nc, stage + "r", ins, XTh, XTl, gate, slots, tile_expert)
        experts_stage(nc, stage + "x", X, XN, *experts, gate, slots, tile_expert, c["identf"], sorted_x, sorted_y)


def build(nc, ins, out, layers=("attn", "ffn", "ssm", "ffn")):
    with ExitStack() as ctx:
        t = Tensors(nc, ctx, "main")
        X = t.sb("X", [P, NT, D])
        c = {"identf": t.sb("identf", [P, P]), "ident16": t.sb("ident16", [P, P], F16), "identb": t.sb("identb", [P, P], BF16),
             "upper_neg": t.sb("upper_neg", [P, P], BF16), "cosr": t.sb("cosr", [P, TB, HALF]), "sinr": t.sb("sinr", [P, TB, HALF])}
        constants_stage(nc, ins["x"], ins["cos"], ins["sin"], X, **c)
        zeroed = False
        sorted_x = nc.dram_tensor("sorted_x", [NSLOT * ST, D], F32, kind="Internal").ap()
        sorted_y = nc.dram_tensor("sorted_y", [NSLOT * ST, D], F32, kind="Internal").ap()
        for n, layer in enumerate(layers):
            if layer == "attn":
                attention_layer(nc, ins, X, c)
            if layer == "ssm":
                ssm_layer(nc, ins, X, c)
            if layer == "ffn":
                with ExitStack() as inner:
                    w = Tensors(nc, inner, f"ew{n}")
                    experts = (w.sb("WH", [P, NE * WCOLS], F16), w.sb("WL", [P, NE * WCOLS], F16),
                               w.sb("b12", [P, 2, NE * KH]), w.sb("b3b", [P, NE, D]))
                    expert_weights_stage(nc, f"ewl{n}", ins, *experts)
                    if not zeroed:
                        zero_rows_stage(nc, sorted_x)
                        zeroed = True
                    ffn_layer(nc, f"ffn{n}", ins, X, experts, sorted_x, sorted_y, c)
        store_stage(nc, X, out)


def rope_tables():
    inv_freq = np.float32(1.0) / np.power(np.float32(10000.0), np.arange(0, DR, 2, dtype=np.float32) / np.float32(DR))
    freqs = np.arange(S, dtype=np.float32)[:, None] * inv_freq[None, :]
    return np.cos(freqs), np.sin(freqs)


_INS = ["L0_attn_a_Wq", "L0_attn_a_Wdkv", "L0_attn_a_Wkr", "L0_attn_a_Wukv", "L0_attn_a_Wo", "L0_attn_b_W_in",
        "L0_attn_b_conv_w", "L0_attn_b_conv_b", "L0_attn_b_A_log", "L0_attn_b_D", "L0_attn_b_dt_bias", "L0_attn_b_norm_w",
        "L0_attn_b_W_out", "L0_attn_b_mup_vector", "L0_ffn_W1", "L0_ffn_b1", "L0_ffn_W2", "L0_ffn_b2", "L0_ffn_W3",
        "L0_ffn_b3", "L0_ffn_Wg", "L0_ffn_bg"]


def kernel(**inputs):
    import concourse.bacc as bacc
    from concourse.bass_utils import run_bass_kernel_spmd as run

    cos, sin = rope_tables()
    arrays = {"x": inputs["L0_attn_a_x"], "cos": cos, "sin": sin} | {n: inputs[n] for n in _INS}
    nc = bacc.Bacc("TRN2", target_bir_lowering=False, num_devices=1)
    given, placed = {}, {}
    for name, a in arrays.items():
        given[f"in_{name}"] = np.ascontiguousarray(a)
        placed[name] = nc.dram_tensor(f"in_{name}", given[f"in_{name}"].shape, mybir.dt.from_np(given[f"in_{name}"].dtype),
                                      kind="ExternalInput").ap()
    out = nc.dram_tensor("out", (B, S, D), F32, kind="ExternalOutput").ap()
    build(nc, placed, out)
    r = run(nc, [given], core_ids=[0])
    return r.results[0]["out"]
```

```python
from contextlib import ExitStack

import numpy as np

import concourse.bass as bass
from concourse import mybir

F32 = mybir.dt.float32
F16 = mybir.dt.float16
BF16 = mybir.dt.bfloat16
I32 = mybir.dt.int32
ALU = mybir.AluOpType
ACT = mybir.ActivationFunctionType
AX = mybir.AxisListType
ds = bass.ds

P = 128
B, S, D = 4, 512, 256
NT = B * S // P
TB = S // P
KD = D // P
EPS = 1e-5

NH, DH, DR, LAT = 16, 16, 64, 64
HD = DH + DR
HALF = DR // 2
ATT_SCALE = float(HD) ** -0.5

NE, H1, TOPK = 8, 512, 2
ST = 2 * P
NSLOT = (B * S * TOPK + NE * (ST - 1)) // ST
KH = H1 // P
W2_AT, W3_AT = KD * H1, KD * H1 + KH * H1
WCOLS = W3_AT + KH * D
PIECES = 4
PIECE = WCOLS // PIECES


class Tensors:

    def __init__(self, nc, ctx, stage):
        self.nc, self.ctx, self.stage, self.sems = nc, ctx, stage, []

    def sb(self, name, shape, dt=F32):
        return self.ctx.enter_context(self.nc.sbuf_tensor(f"{self.stage}_{name}", shape, dt))

    def banks(self, n=8):
        return [self.ctx.enter_context(self.nc.psum_tensor(f"{self.stage}_bank{i}", [P, 512], F32)) for i in range(n)]

    def sem(self, name):
        self.sems.append(self.ctx.enter_context(self.nc.semaphore(f"{self.stage}_{name}")))
        return self.sems[-1]

    def block(self):
        self.ctx.callback(self.clear)
        return self.ctx.enter_context(self.nc.Block())

    def clear(self):
        numbers = sorted(s.num for s in self.sems)
        with self.nc.Block() as block:

            @block.gpsimd
            def _(pool):
                start = numbers[0]
                for at, n in enumerate(numbers):
                    if n + 1 not in numbers[at:]:
                        pool.sem_clear(range(start, n + 1))
                        start = numbers[at + 1] if at + 1 < len(numbers) else None


def wait_alone(eng, sem, value, passed):
    eng.wait_ge(sem, value)
    eng.sem_inc(passed, 1)


class Chain:

    def __init__(self, eng, sem, passed=None):
        self.eng, self.sem, self.passed, self.base, self.n = eng, sem, passed, 0, 0

    def __call__(self, ins):
        self.n += 1
        ins.then_inc(self.sem, 1)
        if self.passed is None:
            self.eng.wait_ge(self.sem, self.base + self.n)
        else:
            wait_alone(self.eng, self.sem, self.base + self.n, self.passed)


def product3(pe, out, a, b, start, stop):
    (ah, al), (bh, bl) = a, b
    pe.matmul(out, ah, bh, start=start, stop=False)
    pe.matmul(out, ah, bl, start=False, stop=False)
    return pe.matmul(out, al, bh, start=False, stop=stop)


class ExpertFeed:

    def __init__(self, t, ins, WH, WL, staged):
        self.ins, self.WH, self.WL, self.staged = ins, WH, WL, staged
        self.loaded = [t.sem(f"weights_loaded{p}") for p in range(PIECES)]
        self.high_ready = t.sem("weights_high")
        self.low_ready = [t.sem(f"weights_low{p}") for p in range(PIECES)]

    def start(self, eng):
        for low_ready in self.low_ready:
            eng.sem_inc(low_ready, 1)

    def wait_all(self, eng, experts):
        for low_ready in self.low_ready:
            eng.wait_ge(low_ready, experts + 1)

    def load(self, sp, e, k):
        for p in range(PIECES):
            name, rows = (("W1", slice(0, D)), ("W2", slice(0, H1 // 2)), ("W2", slice(H1 // 2, H1)), ("W3", slice(0, H1)))[p]
            src = self.ins["L0_ffn_" + name][ds(e, 1), rows, :].rearrange("e (k p) n -> p (e k) n", p=P)
            sp.wait_ge(self.low_ready[p], k + 1)
            sp.dma_start(self.staged[p].rearrange("p (k n) -> p k n", n=D if name == "W3" else H1), src).then_inc(self.loaded[p], 16)

    def high(self, act, e, k, pieces=range(PIECES)):
        for p in pieces:
            act.wait_ge(self.loaded[p], k * 16 + 16)
            act.activation(self.WH[:, ds(e * WCOLS + p * PIECE, PIECE)], self.staged[p], ACT.Copy).then_inc(self.high_ready, 1)

    def low(self, eng, e, k, passed=None, pieces=range(PIECES)):
        for p in pieces:
            if passed is None:
                eng.wait_ge(self.high_ready, k * PIECES + (p + 1))
            else:
                wait_alone(eng, self.high_ready, k * PIECES + (p + 1), passed)
            at = ds(e * WCOLS + p * PIECE, PIECE)
            eng.tensor_tensor(self.WL[:, at], self.staged[p], self.WH[:, at], ALU.subtract).then_inc(self.low_ready[p], 1)


def staging(t):
    staged = t.sb("staged", [P, PIECES, PIECE])
    return [staged[:, p, :] for p in range(PIECES)]


def layer_norm_stage(nc, stage, X, XN, XTh, XTl, identf, experts=None):
    G = NT // TB
    straight = XN is not None

    def passes(eng, body):
        if straight:
            for g in range(G):
                body(g, g % 2, g // 2)
        else:
            with eng.Fori(0, G // 2) as m:
                for half in range(2):
                    body(m * 2 + half, half, m)
    with ExitStack() as ctx:
        t = Tensors(nc, ctx, stage)
        stats = t.sb("stats", [P, TB, 6])
        mv = t.sb("mv", [P, TB, 2])
        sd = t.sb("sd", [P, TB])
        rs = t.sb("rs", [P, TB])
        if not straight:
            ring = t.sb("ring", [P, 2, TB, D])
        if experts:
            feed = ExpertFeed(t, *experts, staging(t))
        bank = t.banks()
        ordered, passed = t.sem("ordered"), t.sem("passed")
        var_ready, sd_ready, norm_ready = t.sem("var_ready"), t.sem("sd_ready"), t.sem("norm_ready")
        xpose_ready, high_ready, low_ready = (t.sem(n) for n in ("xpose_ready", "high_ready", "low_ready"))
        block = t.block()

        def normed(g, half, i):
            return XN[:, g * TB + i, :] if straight else ring[:, half, i, :]

        @block.vector
        def _(dve):
            link = Chain(dve, ordered)
            dve.sem_inc(low_ready, 2 * KD)
            PER = 2 + TB

            def low_parts(g, half):
                for k in range(KD):
                    dve.wait_ge(high_ready, (g * KD) + k + 1)
                    dve.tensor_tensor(XTl[:, k, ds(g * S, S)], bank[2 * half + k][:, :], XTh[:, k, ds(g * S, S)],
                                      ALU.subtract).then_inc(low_ready, 1)

            def body(g, half, m):
                link.base, link.n = g * PER, 0
                for i in range(TB):
                    last = dve.bn_stats(stats[:, i, :], X[:, ds(g * TB + i, 1), :].rearrange("p a d -> p (a d)"))
                link(last)
                if not straight:
                    dve.sem_inc(passed, 1)
                for i in range(TB):
                    last = dve.bn_aggr(mv[:, i, :], stats[:, i, :])
                link(last)
                dve.tensor_scalar(mv[:, :, 1], mv[:, :, 1], EPS, None, ALU.add).then_inc(var_ready, 1)
                dve.wait_ge(sd_ready, g + 1)
                link(dve.reciprocal(rs[:, :], sd[:, :]))
                dve.wait_ge(xpose_ready, KD * (g + 1))
                for i in range(TB):
                    ins = dve.tensor_scalar(normed(g, half, i), X[:, ds(g * TB + i, 1), :].rearrange("p a d -> p (a d)"),
                                            mv[:, i, 0:1], rs[:, i:i + 1], ALU.subtract, ALU.mult)
                    if i == TB - 1:
                        ins.then_inc(norm_ready, 1)
                    else:
                        link(ins)
                dve.wait_ge(norm_ready, g + 1)
                low_parts(g, half)

            passes(dve, body)

        @block.scalar
        def _(act):
            def body(g, half, m):
                act.wait_ge(var_ready, g + 1)
                act.activation(sd[:, :], mv[:, :, 1], ACT.Sqrt).then_inc(sd_ready, 1)
                for k in range(KD):
                    act.wait_ge(xpose_ready, KD * 2 + KD * g + k + 1)
                    act.activation(XTh[:, k, ds(g * S, S)], bank[2 * half + k][:, :], ACT.Copy).then_inc(high_ready, 1)
                if experts:
                    feed.high(act, m, m, range(2 * half, 2 * half + 2))

            passes(act, body)

        @block.tensor
        def _(pe):
            pe.sem_inc(xpose_ready, 2 * KD)

            def body(g, half, m):
                pe.wait_ge(norm_ready, g + 1)
                if half == 0:
                    pe.wait_ge(low_ready, KD * 2 * (m + 1))
                for k in range(KD):
                    for i in range(TB):
                        ins = pe.transpose(bank[2 * half + k][:, i * P:(i + 1) * P], normed(g, half, i)[:, k * P:(k + 1) * P],
                                           identf[:, :])
                    ins.then_inc(xpose_ready, 1)

            passes(pe, body)

        if experts:
            @block.sync
            def _(sp):
                for e in range(2):
                    feed.load(sp, e, e)

            @block.gpsimd
            def _(pool):
                feed.start(pool)
                for e in range(2):
                    feed.low(pool, e, e, passed)


def constants_stage(nc, x, cos, sin, X, identf, ident16, identb, upper_neg, cosr, sinr):
    with ExitStack() as ctx:
        t = Tensors(nc, ctx, "const")
        loaded, cleared, made = t.sem("loaded"), t.sem("cleared"), t.sem("made")
        block = t.block()

        @block.sync
        def _(sp):
            sp.dma_start(X[:, :, :], x.rearrange("b (t p) d -> p (b t) d", p=P)).then_inc(loaded, 16)
            sp.dma_start(cosr[:, :, :], cos.rearrange("(t p) f -> p t f", p=P)).then_inc(loaded, 16)
            sp.dma_start(sinr[:, :, :], sin.rearrange("(t p) f -> p t f", p=P)).then_inc(loaded, 16)
            sp.wait_ge(loaded, 48)

        @block.gpsimd
        def _(pool):
            pool.memset(identf[:, :], 0.0).then_inc(cleared, 1)
            pool.memset(upper_neg[:, :], 0.0).then_inc(cleared, 1)
            pool.wait_ge(cleared, 2)
            pool.affine_select(out=identf[:, :], in_=identf[:, :], compare_op=ALU.not_equal, fill=1.0, base=0,
                               pattern=[[-1, P]], channel_multiplier=1).then_inc(made, 1)
            pool.affine_select(out=upper_neg[:, :], in_=upper_neg[:, :], compare_op=ALU.is_ge, fill=-1e30, base=0,
                               pattern=[[-1, P]], channel_multiplier=1).then_inc(made, 1)
            pool.wait_ge(made, 2)
            pool.tensor_copy(ident16[:, :], identf[:, :]).then_inc(made, 1)
            pool.tensor_copy(identb[:, :], identf[:, :]).then_inc(made, 1)
            pool.wait_ge(made, 4)


def split_weights(nc, stage, parts):
    with ExitStack() as ctx:
        t = Tensors(nc, ctx, stage)
        staged = [t.sb(f"staged{i}", list(high.shape)) for i, (_, high, _) in enumerate(parts)]
        loaded = [t.sem(f"loaded{i}") for i in range(len(parts))]
        high_ready, low_ready = t.sem("high_ready"), t.sem("low_ready")
        block = t.block()

        def whole(a):
            return a[tuple(slice(None) for _ in a.shape)]

        @block.sync
        def _(sp):
            for i, (src, _, _) in enumerate(parts):
                sp.dma_start(whole(staged[i]), src).then_inc(loaded[i], 16)

        @block.scalar
        def _(act):
            for i, (_, high, _) in enumerate(parts):
                act.wait_ge(loaded[i], 16)
                act.activation(whole(high), whole(staged[i]), ACT.Copy).then_inc(high_ready, 1)

        @block.vector
        def _(dve):
            for i, (_, high, low) in enumerate(parts):
                dve.wait_ge(high_ready, i + 1)
                dve.tensor_tensor(whole(low), whole(staged[i]), whole(high), ALU.subtract).then_inc(low_ready, 1)


def attention_stage(nc, X, XTh, XTl, weights, identf, ident16, identb, upper_neg, cosr, sinr, sorted_x):
    (wqh, wql), (wdh, wdl), (wkh, wkl), (wuh, wul), (woh, wol) = weights
    with ExitStack() as ctx:
        t = Tensors(nc, ctx, "att")
        QR = t.sb("QR", [P, TB, NH + 1, HD])
        rot = t.sb("rot", [P, 2, NH + 1, DR])
        ckh, ckl = t.sb("ckh", [LAT, S], F16), t.sb("ckl", [LAT, S], F16)
        KN = t.sb("KN", [P, TB, NH, DH])
        vh, vl = t.sb("vh", [P, TB, NH, DH], F16), t.sb("vl", [P, TB, NH, DH], F16)
        qks = t.sb("qks", [P, 2, 2, 2, TB, HD], F16)
        qkT = t.sb("qkT", [HD, 2, 2, 2, S], F16)
        prob = t.sb("prob", [P, 2, 10 * P])
        pth, ptl = t.sb("pth", [P, 2, 10 * P], F16), t.sb("ptl", [P, 2, 10 * P], F16)
        nmax = t.sb("nmax", [P, 2, TB])
        rsum = t.sb("rsum", [P, 2, TB])
        rinv = t.sb("rinv", [P, TB])
        O = t.sb("O", [P, TB, D])
        oTh, oTl = t.sb("oTh", [P, KD, S], F16), t.sb("oTl", [P, KD, S], F16)
        bank = t.banks()
        sem = t.sem
        lat_ready, lat_high, lat_low = sem("lat_ready"), sem("lat_high"), sem("lat_low")
        q_ready, kv_ready = sem("q_ready"), sem("kv_ready")
        q_copied, kv_copied, v_low = sem("q_copied"), sem("kv_copied"), sem("v_low")
        rot_ready, roped, ordered = sem("rot_ready"), sem("roped"), sem("ordered")
        pool_ordered, passed = sem("pool_ordered"), sem("passed")
        split_ready, qkT_ready, qkT_copied = sem("split_ready"), sem("qkT_ready"), sem("qkT_copied")
        score_ready, max_ready, prob_ready = sem("score_ready"), sem("max_ready"), sem("prob_ready")
        pT_ready, pT_high, pT_low = sem("pT_ready"), sem("pT_high"), sem("pT_low")
        out_ready, out_copied = sem("out_ready"), sem("out_copied")
        oT_ready, oT_high, oT_low = sem("oT_ready"), sem("oT_high"), sem("oT_low")
        proj_ready, added = sem("proj_ready"), sem("added")
        zeros = t.sb("zeros", [P, D])
        zeros_made, rows_cleared = sem("zeros_made"), sem("rows_cleared")
        block = t.block()

        @block.sync
        def _(sp):
            n = NSLOT * ST // P
            sp.wait_ge(zeros_made, 1)
            sp.dma_start(sorted_x.rearrange("(n p) d -> p n d", p=P),
                         zeros[:, :].unsqueeze(1).broadcast_to([P, n, D])).then_inc(rows_cleared, 16)
            sp.wait_ge(rows_cleared, 16)

        q_cols = [(0, 6), (6, 12), (12, 16)]
        KR_AT = 384

        def proj_banks(i):
            return ([bank[1], bank[2], bank[3]], bank[4]) if i % 2 == 0 else ([bank[5], bank[6], bank[7]], bank[0])

        units = [(2, [(3, 0)]), (3, [(2, 0)]), (4, [(1, 0), (0, 2 * P)])]
        p_at = {3: 0, 2: 4 * P, 1: 7 * P, 0: 9 * P}
        chunks = [(0, 4 * P), (4 * P, 3 * P), (7 * P, 3 * P)]

        def over_heads(eng, g0, head):
            head(g0, 0, 0, False, True, True)
            with eng.Fori(0, NH // 2 - 2) as m:
                for step in range(2):
                    head(g0 + m * 2 + (1 + step), m * 2 + (1 + step), 1 - step, True, True, True)
            head(g0 + NH - 3, NH - 3, 1, True, True, True)
            head(g0 + NH - 2, NH - 2, 0, True, True, False)
            head(g0 + NH - 1, NH - 1, 1, True, False, False)

        @block.tensor
        def _(pe):
            pe.sem_inc(qkT_ready, 4)

            def project(b):
                for k in range(KD):
                    tok = ds(b * S, S)
                    ins = product3(pe, bank[0][0:LAT, :], (wdh[:, k, :], wdl[:, k, :]), (XTh[:, k, tok], XTl[:, k, tok]),
                                   k == 0, k == KD - 1)
                ins.then_inc(lat_ready, 1)
                for i in range(TB):
                    qb, kvb = proj_banks(i)
                    tok = ds(b * S + i * P, P)
                    if i >= 2:
                        pe.wait_ge(q_copied, b * TB + i - 1)
                    for n, (h0, h1) in enumerate(q_cols):
                        for k in range(KD):
                            ins = product3(pe, qb[n][:, 0:(h1 - h0) * HD], (XTh[:, k, tok], XTl[:, k, tok]),
                                           (wqh[:, k, h0 * HD:h1 * HD], wql[:, k, h0 * HD:h1 * HD]), k == 0, k == KD - 1)
                    for k in range(KD):
                        ins = product3(pe, qb[2][:, KR_AT:KR_AT + DR], (XTh[:, k, tok], XTl[:, k, tok]),
                                       (wkh[:, k, :], wkl[:, k, :]), k == 0, k == KD - 1)
                    ins.then_inc(q_ready, 1)
                    if i == 0:
                        pe.wait_ge(lat_low, b + 1)
                    if i >= 2:
                        pe.wait_ge(v_low, b * TB + i - 1)
                    product3(pe, kvb[:, :], (ckh[:, i * P:(i + 1) * P], ckl[:, i * P:(i + 1) * P]),
                             (wuh[:, :], wul[:, :]), True, True).then_inc(kv_ready, 1)

            def transpose_qk(g, par):
                pe.wait_ge(split_ready, g + 1)
                pe.wait_ge(qkT_copied, 2 * g + 1)
                for x in range(2):
                    pe.wait_ge(qkT_copied, 2 * g + x + 1)
                    out = bank[x][0:HD, :].bitcast(F16)
                    for part in range(2):
                        for i in range(TB):
                            ins = pe.transpose(out[:, (part * TB + i) * P:(part * TB + i + 1) * P],
                                               qks[:, par, x, part, i, :], ident16[:, :])
                    ins.then_inc(qkT_ready, 1)

            def scores(g, par, us=(0, 1, 2)):
                if us[0] == 0:
                    pe.wait_ge(qkT_copied, 2 * g + 4)
                for u in us:
                    bk, tiles = units[u]
                    pe.wait_ge(prob_ready, 3 * g + u + 1)
                    for i, at in tiles:
                        n = (i + 1) * P
                        out = bank[bk][:, at:at + n]
                        q = qkT[:, par, 0, :, i * P:(i + 1) * P]
                        kk = qkT[:, par, 1, :, 0:n]
                        product3(pe, out, (q[:, 0, :], q[:, 1, :]), (kk[:, 0, :], kk[:, 1, :]), True, False)
                        ins = pe.matmul(out[:, n - P:n], identb[:, :], upper_neg[:, :], start=False, stop=True)
                    ins.then_inc(score_ready, 1)

            def transpose_probs(g, par, cs):
                for c in cs:
                    at, n = chunks[c]
                    pe.wait_ge(prob_ready, 3 * g + c + 4)
                    pe.wait_ge(pT_low, 3 * g + c + 1)
                    bk = bank[5 + (3 * par + c) % 2]
                    for j in range(n // P):
                        ins = pe.transpose(bk[:, j * P:(j + 1) * P], prob[:, par, at + j * P:at + (j + 1) * P], identf[:, :])
                    ins.then_inc(pT_ready, 1)

            def weigh_values(g, h, par):
                pe.wait_ge(pT_low, 3 * g + 3 + 2)
                pe.wait_ge(out_copied, g + 1)
                for i in range(TB):
                    for j in range(i + 1):
                        at = p_at[i] + j * P
                        ins = product3(pe, bank[7][:, i * DH:(i + 1) * DH],
                                       (pth[:, par, at:at + P], ptl[:, par, at:at + P]),
                                       (vh[:, j, ds(h, 1), :].rearrange("p a d -> p (a d)"),
                                        vl[:, j, ds(h, 1), :].rearrange("p a d -> p (a d)")), j == 0, j == i)
                ins.then_inc(out_ready, 1)

            def head(g, h, par, before, after, after2):
                transpose_probs(g, par, (0,))
                transpose_probs(g, par, (1,))
                if after:
                    scores(g + 1, 1 - par, (0,))
                if before:
                    weigh_values(g - 1, h - 1, 1 - par)
                if after:
                    scores(g + 1, 1 - par, (1,))
                transpose_probs(g, par, (2,))
                if after:
                    scores(g + 1, 1 - par, (2,))
                if after2:
                    transpose_qk(g + 2, par)

            with pe.Fori(0, B) as b:
                pe.wait_ge(added, b * TB + 1)
                project(b)
                pe.wait_ge(q_copied, b * TB + TB)
                pe.wait_ge(v_low, b * TB + TB)
                g0 = b * NH
                transpose_qk(g0, 0)
                scores(g0, 0)
                transpose_qk(g0 + 1, 1)
                over_heads(pe, g0, head)
                weigh_values(g0 + NH - 1, NH - 1, 1)
                pe.wait_ge(out_copied, g0 + NH + 1)
                for k in range(KD):
                    for i in range(TB):
                        ins = pe.transpose(bank[k][:, i * P:(i + 1) * P], O[:, i, k * P:(k + 1) * P], identf[:, :])
                    ins.then_inc(oT_ready, 1)
                pe.wait_ge(oT_low, KD * b + KD)
                for i in range(TB):
                    for k in range(KD):
                        tok = slice(i * P, (i + 1) * P)
                        ins = product3(pe, bank[2 + i][:, 0:D], (oTh[:, k, tok], oTl[:, k, tok]),
                                       (woh[:, k, :], wol[:, k, :]), k == 0, k == KD - 1)
                    ins.then_inc(proj_ready, 1)

        @block.scalar
        def _(act):
            act.sem_inc(prob_ready, 3)

            def probs(g, par, us=(0, 1, 2)):
                for u in us:
                    bk, tiles = units[u]
                    act.wait_ge(max_ready, 3 * g + u + 1)
                    for i, at in tiles:
                        n = (i + 1) * P
                        ins = act.activation(prob[:, par, p_at[i]:p_at[i] + n], bank[bk][:, at:at + n], ACT.Exp,
                                             bias=nmax[:, par, i:i + 1], accum_out=rsum[:, par, i:i + 1])
                    ins.then_inc(prob_ready, 1)

            def high_probs(g, par, cs):
                for c in cs:
                    at, n = chunks[c]
                    act.wait_ge(pT_ready, 3 * g + c + 1)
                    act.activation(pth[:, par, at:at + n], bank[5 + (3 * par + c) % 2][:, 0:n], ACT.Copy).then_inc(pT_high, 1)

            def head(g, h, par, before, after, after2):
                high_probs(g, par, (0,))
                probs(g, par, (2,))
                high_probs(g, par, (1,))
                if after:
                    probs(g + 1, 1 - par, (0,))
                high_probs(g, par, (2,))
                if after:
                    probs(g + 1, 1 - par, (1,))

            with act.Fori(0, B) as b:
                act.wait_ge(lat_ready, b + 1)
                act.activation(ckh[:, :], bank[0][0:LAT, :], ACT.Copy).then_inc(lat_high, 1)
                for i in range(TB):
                    qb, kvb = proj_banks(i)
                    act.wait_ge(q_ready, b * TB + i + 1)
                    for n, (h0, h1) in enumerate(q_cols):
                        act.activation(QR[:, i, h0:h1, :], qb[n][:, 0:(h1 - h0) * HD].rearrange("p (h d) -> p h d", d=HD),
                                       ACT.Copy, scale=ATT_SCALE)
                    act.activation(QR[:, i, NH, DH:HD], qb[2][:, KR_AT:KR_AT + DR], ACT.Copy).then_inc(q_copied, 1)
                    act.wait_ge(kv_ready, b * TB + i + 1)
                    kv = kvb[:, :].rearrange("p (h x d) -> p h x d", x=2, d=DH)
                    act.activation(KN[:, i, :, :], kv[:, :, 0, :], ACT.Copy)
                    act.activation(vh[:, i, :, :], kv[:, :, 1, :], ACT.Copy).then_inc(kv_copied, 1)
                g0 = b * NH
                probs(g0, 0, (0, 1))
                over_heads(act, g0, head)
                for k in range(KD):
                    act.wait_ge(oT_ready, KD * b + k + 1)
                    act.activation(oTh[:, k, :], bank[k][:, :], ACT.Copy).then_inc(oT_high, 1)

        @block.vector
        def _(dve):
            dve.memset(zeros[:, :], 0.0).then_inc(zeros_made, 1)
            dve.sem_inc(qkT_copied, 2)
            dve.sem_inc(pT_low, 2)
            dve.sem_inc(out_copied, 1)
            dve.sem_inc(added, 1)

            def copy_qkT(g, par):
                for x in range(2):
                    dve.wait_ge(qkT_ready, 2 * g + x + 5)
                    dve.tensor_copy(qkT[:, par, x, :, :].rearrange("p a n -> p (a n)"),
                                    bank[x][0:HD, :].bitcast(F16)).then_inc(qkT_copied, 1)

            def maxima(g, par, us=(0, 1, 2)):
                for u in us:
                    bk, tiles = units[u]
                    dve.wait_ge(score_ready, 3 * g + u + 1)
                    for i, at in tiles:
                        ins = dve.tensor_reduce(nmax[:, par, i:i + 1], bank[bk][:, at:at + (i + 1) * P], AX.X, ALU.max,
                                                negate=True)
                    ins.then_inc(max_ready, 1)

            def low_probs(g, par, cs):
                for c in cs:
                    at, n = chunks[c]
                    dve.wait_ge(pT_high, 3 * g + c + 1)
                    dve.tensor_tensor(ptl[:, par, at:at + n], bank[5 + (3 * par + c) % 2][:, 0:n], pth[:, par, at:at + n],
                                      ALU.subtract).then_inc(pT_low, 1)

            def invert_sums(g, par):
                dve.wait_ge(prob_ready, 3 * g + 6)
                link.base, link.n = g, 0
                link(dve.reciprocal(rinv[:, :], rsum[:, par, :]))

            def normalise(g, h):
                dve.wait_ge(out_ready, g + 1)
                dve.tensor_tensor(O[:, :, ds(h * DH, DH)], bank[7][:, 0:TB * DH].rearrange("p (i d) -> p i d", d=DH),
                                  rinv[:, :].unsqueeze(2).broadcast_to([P, TB, DH]), ALU.mult).then_inc(out_copied, 1)

            def head(g, h, par, before, after, after2):
                low_probs(g, par, (0,))
                if after:
                    maxima(g + 1, 1 - par, (0,))
                low_probs(g, par, (1,))
                if before:
                    normalise(g - 1, h - 1)
                if after:
                    maxima(g + 1, 1 - par, (1,))
                low_probs(g, par, (2,))
                if after2:
                    copy_qkT(g + 2, par)
                dve.wait_ge(out_copied, g + 1)
                invert_sums(g, par)
                if after:
                    maxima(g + 1, 1 - par, (2,))

            link = Chain(dve, ordered)
            with dve.Fori(0, B) as b:
                dve.wait_ge(lat_high, b + 1)
                dve.tensor_tensor(ckl[:, :], bank[0][0:LAT, :], ckh[:, :], ALU.subtract).then_inc(lat_low, 1)
                for i in range(TB):
                    dve.wait_ge(q_copied, b * TB + i + 1)
                    dve.wait_ge(roped, b * TB + i + 1)
                    x = QR[:, i, :, DH:HD].rearrange("p h (x f) -> p h x f", x=2)
                    r = rot[:, i % 2, :, :].rearrange("p h (x f) -> p h x f", x=2)
                    for xx in range(2):
                        sn = sinr[:, i, :].unsqueeze(1).broadcast_to([P, NH + 1, HALF])
                        ins = dve.tensor_tensor(r[:, :, xx, :], x[:, :, xx, :], sn, ALU.mult)
                    ins.then_inc(rot_ready, 1)
                    dve.wait_ge(rot_ready, 2 * (b * TB + i) + 1)
                    for xx in range(2):
                        cs = cosr[:, i, :].unsqueeze(1).broadcast_to([P, NH + 1, HALF])
                        ins = dve.tensor_tensor(x[:, :, xx, :], x[:, :, xx, :], cs, ALU.mult)
                    ins.then_inc(rot_ready, 1)
                    _, kvb = proj_banks(i)
                    dve.wait_ge(kv_copied, b * TB + i + 1)
                    dve.tensor_tensor(vl[:, i, :, :], kvb[:, :].rearrange("p (h x d) -> p h x d", x=2, d=DH)[:, :, 1, :],
                                      vh[:, i, :, :], ALU.subtract).then_inc(v_low, 1)
                g0 = b * NH
                copy_qkT(g0, 0)
                maxima(g0, 0)
                copy_qkT(g0 + 1, 1)
                over_heads(dve, g0, head)
                normalise(g0 + NH - 1, NH - 1)
                for k in range(KD):
                    dve.wait_ge(oT_high, KD * b + k + 1)
                    dve.tensor_tensor(oTl[:, k, :], bank[k][:, :], oTh[:, k, :], ALU.subtract).then_inc(oT_low, 1)
                for i in range(TB):
                    dve.wait_ge(proj_ready, TB * b + i + 1)
                    xt = X[:, ds(b * TB + i, 1), :].rearrange("p a d -> p (a d)")
                    dve.tensor_tensor(xt, bank[2 + i][:, 0:D], xt, ALU.add).then_inc(added, 1)

        @block.gpsimd
        def _(pool):
            pool.sem_inc(roped, 2)
            link = Chain(pool, pool_ordered, passed)

            def split(g, h, par):
                wait_alone(pool, qkT_ready, 2 * g + 1, passed)
                wait_alone(pool, qkT_ready, 2 * g + 2, passed)
                q = QR[:, :, ds(h, 1), :].rearrange("p t a d -> p t (a d)")
                kn = KN[:, :, ds(h, 1), :].rearrange("p t a d -> p t (a d)")
                pool.tensor_copy(qks[:, par, 0, 0, :, :], q)
                link(pool.tensor_copy(qks[:, par, 1, 0, :, 0:DH], kn))
                pool.tensor_tensor(qks[:, par, 0, 1, :, :], q, qks[:, par, 0, 0, :, :], ALU.subtract)
                pool.tensor_tensor(qks[:, par, 1, 1, :, 0:DH], kn, qks[:, par, 1, 0, :, 0:DH],
                                   ALU.subtract).then_inc(split_ready, 1)

            PER = NH + 2
            with pool.Fori(0, B) as b:
                for i in range(TB):
                    wait_alone(pool, rot_ready, 2 * (b * TB + i) + 2, passed)
                    x = QR[:, i, :, DH:HD]
                    r = rot[:, i % 2, :, :]
                    pool.tensor_tensor(x[:, :, 0:HALF], x[:, :, 0:HALF], r[:, :, HALF:DR], ALU.subtract)
                    pool.tensor_tensor(x[:, :, HALF:DR], x[:, :, HALF:DR], r[:, :, 0:HALF], ALU.add).then_inc(roped, 1)
                wait_alone(pool, roped, b * TB + TB + 2, passed)
                wait_alone(pool, kv_copied, b * TB + TB, passed)
                wait_alone(pool, qkT_ready, 2 * (b * NH) + 4, passed)
                link.base, link.n = b * PER, 0
                for par in range(2):
                    ins = pool.tensor_copy(qks[:, par, 1, 0, :, DH:HD], QR[:, :, NH, DH:HD])
                link(ins)
                for par in range(2):
                    ins = pool.tensor_tensor(qks[:, par, 1, 1, :, DH:HD], QR[:, :, NH, DH:HD], qks[:, par, 1, 0, :, DH:HD],
                                             ALU.subtract)
                link(ins)
                with pool.Fori(0, NH // 2) as m:
                    for par in range(2):
                        link.base, link.n = b * PER + 2 + m * 2 + par, 0
                        split(b * NH + m * 2 + par, m * 2 + par, par)




def routing_stage(nc, stage, ins, XTh, XTl, gate, slots, tile_expert, WH, WL):
    with ExitStack() as ctx:
        t = Tensors(nc, ctx, stage)
        wg, wgh, wgl = t.sb("wg", [P, KD, NE]), t.sb("wgh", [P, KD, NE], F16), t.sb("wgl", [P, KD, NE], F16)
        bg = t.sb("bg", [P, NE])
        grid = [P, NT, NE]
        expert_m8 = t.sb("expert_m8", grid)
        tile_start = t.sb("tile_start", [P, NSLOT])
        before = t.sb("before", [P, P], BF16)
        ones = t.sb("ones", [P, P], BF16)
        keep = t.sb("keep", [P, NE, NT])
        ones8 = t.sb("ones8", [P, NE])
        logit, prob, same, rest = (t.sb(n, grid) for n in ("logit", "prob", "same", "rest"))
        mask = [t.sb("mask0", grid), t.sb("mask1", grid)]
        both = t.sb("both", grid, BF16)
        col = t.sb("col", [P, NT])
        total, running = t.sb("total", [P, NE, NT]), t.sb("running", [P, NE, NT])
        padded_i = t.sb("padded_i", [P, NE], I32)
        padded, ends = t.sb("padded", [P, NE]), t.sb("ends", [P, NE])
        where = t.sb("where", grid)
        slot_f = t.sb("slot_f", [P, NT])
        past = t.sb("past", [P, NSLOT, NE])
        tile_e = t.sb("tile_e", [P, NSLOT])
        bank = t.banks(3)
        loaded, made, cleared = t.sem("loaded"), t.sem("made"), t.sem("cleared")
        wg_high, wg_ready, logits_ready = t.sem("wg_high"), t.sem("wg_ready"), t.sem("logits_ready")
        shifted, exp_ready, both_ready, ranks_ready = (t.sem(n) for n in ("shifted", "exp_ready", "both_ready", "ranks_ready"))
        ordered, passed = t.sem("ordered"), t.sem("passed")
        feed = ExpertFeed(t, ins, WH, WL, staging(t))
        block = t.block()

        @block.sync
        def _(sp):
            sp.dma_start(wg[:, :, :], ins["L0_ffn_Wg"].rearrange("(k p) n -> p k n", p=P)).then_inc(loaded, 16)
            sp.dma_start(bg[:, :], ins["L0_ffn_bg"].unsqueeze(0).broadcast_to([P, NE])).then_inc(loaded, 16)
            for k in range(3):
                feed.load(sp, 2 + k, k)

        @block.gpsimd
        def _(pool):
            feed.start(pool)
            pool.memset(before[:, :], 1.0).then_inc(cleared, 1)
            pool.memset(ones[:, :], 1.0).then_inc(made, 1)
            pool.memset(keep[:, :, :], 1.0).then_inc(cleared, 1)
            pool.memset(ones8[:, :], 1.0).then_inc(made, 1)
            pool.iota(expert_m8[:, :, :], [[0, NT], [1, NE]], base=-NE, channel_multiplier=0,
                      allow_small_or_imprecise_dtypes=True).then_inc(made, 1)
            pool.iota(tile_start[:, :], [[ST, NSLOT]], base=0, channel_multiplier=0,
                      allow_small_or_imprecise_dtypes=True).then_inc(made, 1)
            pool.wait_ge(cleared, 2)
            pool.memset(keep[:, :, 0:1], 0.0).then_inc(made, 1)
            pool.affine_select(out=before[:, :], in_=before[:, :], compare_op=ALU.is_gt, fill=0.0, base=0,
                               pattern=[[1, P]], channel_multiplier=-1).then_inc(made, 1)
            for k in range(1, 3):
                feed.low(pool, 2 + k, k, passed)

        @block.scalar
        def _(act):
            act.wait_ge(loaded, 32)
            act.activation(wgh[:, :, :], wg[:, :, :], ACT.Copy).then_inc(wg_high, 1)
            feed.high(act, 2, 0)
            act.wait_ge(shifted, 1)
            act.activation(prob[:, :, :], logit[:, :, :], ACT.Exp).then_inc(exp_ready, 1)
            for k in range(1, 3):
                feed.high(act, 2 + k, k)

        @block.tensor
        def _(pe):
            pe.wait_ge(wg_ready, 1)
            for n in range(NT):
                for k in range(KD):
                    tok = slice(n * P, (n + 1) * P)
                    ins_ = product3(pe, bank[0][:, n * NE:(n + 1) * NE], (XTh[:, k, tok], XTl[:, k, tok]),
                                    (wgh[:, k, :], wgl[:, k, :]), k == 0, k == KD - 1)
                ins_.then_inc(logits_ready, 1)
            pe.wait_ge(made, 6)
            pe.wait_ge(both_ready, 1)
            flat = both[:, :, :].rearrange("p n e -> p (n e)")
            pe.matmul(bank[1][:, 0:NT * NE], before[:, :], flat, start=True, stop=True)
            pe.matmul(bank[2][:, 0:NT * NE], ones[:, :], flat, start=True, stop=True).then_inc(ranks_ready, 1)

        @block.vector
        def _(dve):
            link = Chain(dve, ordered)
            wide = lambda a: a.unsqueeze(2).broadcast_to(grid)
            dve.wait_ge(wg_high, 1)
            dve.tensor_tensor(wgl[:, :, :], wg[:, :, :], wgh[:, :, :], ALU.subtract).then_inc(wg_ready, 1)
            feed.low(dve, 2, 0, None, range(2))
            dve.wait_ge(logits_ready, NT)
            link(dve.tensor_tensor(logit[:, :, :], bank[0][:, 0:NT * NE].rearrange("p (n e) -> p n e", e=NE),
                                   bg[:, :].unsqueeze(1).broadcast_to(grid), ALU.add))
            link(dve.tensor_reduce(col[:, :], logit[:, :, :], AX.X, ALU.max))
            dve.tensor_tensor(logit[:, :, :], logit[:, :, :], wide(col[:, :]), ALU.subtract).then_inc(shifted, 1)
            feed.low(dve, 2, 0, None, range(2, PIECES))
            dve.wait_ge(exp_ready, 1)
            link(dve.tensor_reduce(slot_f[:, :], prob[:, :, :], AX.X, ALU.add))
            link(dve.reciprocal(col[:, :], slot_f[:, :]))
            link(dve.tensor_tensor(prob[:, :, :], prob[:, :, :], wide(col[:, :]), ALU.mult))
            dve.wait_ge(made, 6)
            for k in range(TOPK):
                src = prob if k == 0 else rest
                link(dve.tensor_reduce(gate[:, :, k], src[:, :, :], AX.X, ALU.max))
                link(dve.tensor_tensor(same[:, :, :], src[:, :, :], wide(gate[:, :, k]), ALU.is_equal))
                link(dve.tensor_tensor(same[:, :, :], same[:, :, :], expert_m8[:, :, :], ALU.mult))
                link(dve.tensor_reduce(col[:, :], same[:, :, :], AX.X, ALU.min))
                link(dve.tensor_tensor(mask[k][:, :, :], expert_m8[:, :, :], wide(col[:, :]), ALU.is_equal))
                if k == 0:
                    link(dve.scalar_tensor_tensor(rest[:, :, :], mask[0][:, :, :], -2.0, prob[:, :, :], ALU.mult, ALU.add))
            dve.tensor_tensor(both[:, :, :], mask[0][:, :, :], mask[1][:, :, :], ALU.add).then_inc(both_ready, 1)
            dve.wait_ge(ranks_ready, 1)
            by_expert = "p (n e) -> p e n"
            link(dve.tensor_copy(total[:, :, :], bank[2][:, 0:NT * NE].rearrange(by_expert, e=NE)))
            flat = lambda a: a[:, :, :].rearrange("p e n -> p (e n)")
            link(dve.tensor_tensor_scan(flat(running), flat(keep), flat(total), 0.0, ALU.mult, ALU.add))
            link(dve.tensor_scalar(padded[:, :], running[:, :, NT - 1], float(ST - 1), None, ALU.add))
            link(dve.tensor_copy(padded_i[:, :], padded[:, :]))
            shift = ST.bit_length() - 1
            link(dve.tensor_scalar(padded_i[:, :], padded_i[:, :], shift, shift, ALU.logical_shift_right, ALU.logical_shift_left))
            link(dve.tensor_copy(padded[:, :], padded_i[:, :]))
            link(dve.tensor_tensor_scan(ends[:, :], ones8[:, :], padded[:, :], 0.0, ALU.mult, ALU.add))
            link(dve.tensor_tensor(padded[:, :], ends[:, :], padded[:, :], ALU.subtract))
            link(dve.tensor_tensor(running[:, :, :], running[:, :, :], total[:, :, :], ALU.subtract))
            link(dve.tensor_tensor(running[:, :, :], running[:, :, :], padded[:, :].unsqueeze(2).broadcast_to([P, NE, NT]), ALU.add))
            link(dve.tensor_tensor(where[:, :, :], bank[1][:, 0:NT * NE].rearrange("p (n e) -> p n e", e=NE),
                                   running[:, :, :].rearrange("p e n -> p n e"), ALU.add))
            for k in range(TOPK):
                link(dve.tensor_tensor(same[:, :, :], where[:, :, :], mask[k][:, :, :], ALU.mult))
                link(dve.tensor_reduce(slot_f[:, :], same[:, :, :], AX.X, ALU.add))
                link(dve.tensor_copy(slots[:, k, :], slot_f[:, :]))
            tiles = [P, NSLOT, NE]
            link(dve.tensor_tensor(past[:, :, :], tile_start[:, :].unsqueeze(2).broadcast_to(tiles),
                                   ends[:, :].unsqueeze(1).broadcast_to(tiles), ALU.is_ge))
            link(dve.tensor_reduce(tile_e[:, :], past[:, :, :], AX.X, ALU.add))
            link(dve.tensor_scalar(tile_e[:, :], tile_e[:, :], float(NE - 1), None, ALU.min))
            link(dve.tensor_copy(tile_expert[:, :], tile_e[:, :]))


def experts_stage(nc, stage, ins, X, XN, WH, WL, gate, slots, tile_expert, identf, sorted_x, sorted_y, row_moves):
    RING = len(row_moves) - 1
    with ExitStack() as ctx:
        t = Tensors(nc, ctx, stage)
        xs = t.sb("xs", [P, 2, 2, D])
        xTh, xTl = t.sb("xTh", [P, KD, ST], F16), t.sb("xTl", [P, KD, ST], F16)
        h = [t.sb(f"h{n}", [P, KH, ST]) for n in range(2)]
        hh = [t.sb(f"hh{n}", [P, KH, ST], F16) for n in range(2)]
        hl = [t.sb(f"hl{n}", [P, KH, ST], F16) for n in range(2)]
        y = t.sb("y", [P, 2, 2, D])
        back = t.sb("back", [P, RING, D])
        b12, b3b = t.sb("b12", [P, 2, NE * KH]), t.sb("b3b", [P, NE, D])
        bank = t.banks(6)
        whole = lambda a: a.rearrange("p a n -> p (a n)")
        feed = ExpertFeed(t, ins, WH, WL, [whole(h[0][:, :, :]), whole(h[1][:, :, :]), whole(back[:, 0:RING // 2, :]),
                                           whole(back[:, RING // 2:RING, :])])
        biases = t.sem("biases")
        scattered, *gathered = row_moves
        passed = t.sem("passed")
        xs_loaded = [t.sem(f"xs_loaded{i}") for i in range(2)]
        xT_ready, xT_high, xT_low = t.sem("xT_ready"), t.sem("xT_high"), t.sem("xT_low")
        lin_ready = [t.sem(f"lin_ready{n}") for n in range(2)]
        gelu_ready = [t.sem(f"gelu_ready{n}") for n in range(2)]
        h_high, h_low = [t.sem(f"h_high{n}") for n in range(2)], [t.sem(f"h_low{n}") for n in range(2)]
        y_psum, y_ready = t.sem("y_psum"), t.sem("y_ready")
        y_stored = [t.sem(f"y_stored{i}") for i in range(2)]
        added, stored = t.sem("added"), t.sem("stored")
        block = t.block()
        NB = (NSLOT - 3) // 2
        rows_of = lambda dram, j: dram[ds(j * ST, ST), :].rearrange("(a p) d -> p a d", p=P)

        def tiles(eng, body):
            with eng.Fori(0, NB) as m:
                for par in range(2):
                    body(m * 2 + par, par, 2)
            for j in range(2 * NB, NSLOT):
                body(j, j % 2, min(2, NSLOT - 1 - j))

        @block.sync
        def _(sp):
            def load(j, par, ahead):
                sp.wait_ge(xT_ready, j + 1)
                sp.dma_start(xs[:, par, :, :], rows_of(sorted_x, j)).then_inc(xs_loaded[par], 16)

            def store(j, par):
                sp.wait_ge(y_ready, j + 2)
                sp.dma_start(rows_of(sorted_y, j), y[:, par, :, :]).then_inc(y_stored[par], 16)

            def body(j, par, ahead):
                if ahead >= 2:
                    load(j + 2, par, ahead)
                store(j, par)

            for k in range(3):
                feed.load(sp, NE - 3 + k, k)
            for layer in range(2):
                sp.dma_start(b12[:, layer, :], ins[f"L0_ffn_b{layer + 1}"].rearrange("e (m p) -> p (e m)", p=P),
                             allow_slow_non_contiguous=True).then_inc(biases, 16)
            sp.dma_start(b3b[:, :, :], ins["L0_ffn_b3"].unsqueeze(0).broadcast_to([P, NE, D])).then_inc(biases, 16)
            for par in range(2):
                sp.sem_inc(y_stored[par], 16)
            sp.wait_ge(scattered, 16 * TOPK * NT)
            load(0, 0, 2)
            load(1, 1, 2)
            tiles(sp, body)

        @block.gpsimd
        def _(pool):
            for n in range(NT):
                for k in range(TOPK):
                    pool.indirect_dma_start(out=sorted_x, out_offset=bass.IndirectOffsetOnAxis(ap=slots[:, k, n:n + 1], axis=0),
                                            in_=XN[:, n, :], in_offset=None).then_inc(scattered, 16)
            for par in range(2):
                pool.wait_ge(y_stored[par], 16 * ((NSLOT - par + 1) // 2) + 16)
            for n in range(NT):
                for k in range(TOPK):
                    i = n * TOPK + k
                    if i >= RING:
                        pool.wait_ge(added, i - RING + 1)
                    pool.indirect_dma_start(out=back[:, i % RING, :], out_offset=None, in_=sorted_y,
                                            in_offset=bass.IndirectOffsetOnAxis(ap=slots[:, k, n:n + 1], axis=0)
                                            ).then_inc(gathered[i % RING], 16)

        def expert_of(eng, j, scale):
            e = eng.value_load(tile_expert[0:1, ds(j, 1)] if not isinstance(j, int) else tile_expert[0:1, j:j + 1],
                               min_val=0, max_val=NE - 1)
            return e * scale

        @block.tensor
        def _(pe):
            pe.sem_inc(xT_ready, 2)

            def transpose_in(j, par):
                pe.wait_ge(xs_loaded[par], (j - par) * 8 + 16)
                for k in range(KD):
                    for a in range(2):
                        ins = pe.transpose(bank[0][:, k * ST + a * P:k * ST + (a + 1) * P], xs[:, par, a, k * P:(k + 1) * P],
                                           identf[:, :])
                ins.then_inc(xT_ready, 1)

            def layer1(j):
                w = expert_of(pe, j, WCOLS)
                pe.wait_ge(xT_low, j + 1)
                for m in range(KH):
                    for k in range(KD):
                        at = w + (k * H1 + m * P)
                        ins = product3(pe, bank[1 + m // 2][:, (m % 2) * ST:(m % 2 + 1) * ST],
                                       (WH[:, ds(at, P)], WL[:, ds(at, P)]), (xTh[:, k, :], xTl[:, k, :]), k == 0, k == KD - 1)
                    if m % 2:
                        ins.then_inc(lin_ready[0], 1)

            def layer2(j):
                w = expert_of(pe, j, WCOLS)
                pe.wait_ge(h_low[0], 2 * j + 2)
                for m in range(KH):
                    for k in range(KH):
                        at = w + (W2_AT + k * H1 + m * P)
                        ins = product3(pe, bank[3 + m // 2][:, (m % 2) * ST:(m % 2 + 1) * ST],
                                       (WH[:, ds(at, P)], WL[:, ds(at, P)]), (hh[0][:, k, :], hl[0][:, k, :]),
                                       k == 0, k == KH - 1)
                    if m % 2:
                        ins.then_inc(lin_ready[1], 1)

            def layer3(j):
                w = expert_of(pe, j, WCOLS)
                pe.wait_ge(h_low[1], 2 * j + 2)
                pe.wait_ge(y_ready, j + 1)
                for a in range(2):
                    for k in range(KH):
                        at = w + (W3_AT + k * D)
                        rows = slice(a * P, (a + 1) * P)
                        ins = product3(pe, bank[5][:, a * D:(a + 1) * D], (hh[1][:, k, rows], hl[1][:, k, rows]),
                                       (WH[:, ds(at, D)], WL[:, ds(at, D)]), k == 0, k == KH - 1)
                ins.then_inc(y_psum, 1)

            def body(j, par, ahead):
                layer2(j)
                if ahead >= 1:
                    layer1(j + 1)
                if ahead >= 2:
                    transpose_in(j + 2, par)
                layer3(j)

            feed.wait_all(pe, 3)
            transpose_in(0, 0)
            layer1(0)
            transpose_in(1, 1)
            tiles(pe, body)

        @block.scalar
        def _(act):
            for k in range(3):
                feed.high(act, NE - 3 + k, k)
            act.wait_ge(biases, 48)

            def gelus(layer, j):
                e = expert_of(act, j, KH)
                bias = b12[:, layer, :]
                for u in range(2):
                    act.wait_ge(lin_ready[layer], 2 * j + u + 1)
                    for m in (2 * u, 2 * u + 1):
                        ins = act.activation(h[layer][:, m, :], bank[1 + 2 * layer + u][:, (m % 2) * ST:(m % 2 + 1) * ST],
                                             ACT.Gelu, bias=bias[:, ds(e + m, 1)])
                    ins.then_inc(gelu_ready[layer], 1)

            def high_in(j):
                act.wait_ge(xT_ready, j + 3)
                act.activation(xTh[:, :, :].rearrange("p k n -> p (k n)"), bank[0][:, :], ACT.Copy).then_inc(xT_high, 1)

            def body(j, par, ahead):
                gelus(1, j)
                if ahead >= 1:
                    gelus(0, j + 1)
                if ahead >= 2:
                    high_in(j + 2)

            high_in(0)
            gelus(0, 0)
            high_in(1)
            tiles(act, body)

        @block.vector
        def _(dve):
            dve.sem_inc(y_ready, 1)
            feed.start(dve)
            for k in range(3):
                feed.low(dve, NE - 3 + k, k)
            dve.wait_ge(biases, 48)

            def low_in(j):
                dve.wait_ge(xT_high, j + 1)
                dve.tensor_tensor(xTl[:, :, :].rearrange("p k n -> p (k n)"), bank[0][:, :],
                                  xTh[:, :, :].rearrange("p k n -> p (k n)"), ALU.subtract).then_inc(xT_low, 1)

            def split(layer, j):
                for u in range(2):
                    dve.wait_ge(gelu_ready[layer], 2 * j + u + 1)
                    two = slice(2 * u, 2 * u + 2)
                    dve.tensor_copy(hh[layer][:, two, :], h[layer][:, two, :]).then_inc(h_high[layer], 1)
                    dve.wait_ge(h_high[layer], 2 * j + u + 1)
                    dve.tensor_tensor(hl[layer][:, two, :], h[layer][:, two, :], hh[layer][:, two, :],
                                      ALU.subtract).then_inc(h_low[layer], 1)

            def finish(j, par):
                e = expert_of(dve, j, 1)
                dve.wait_ge(y_psum, j + 1)
                dve.wait_ge(y_stored[par], (j - par) * 8 + 16)
                dve.tensor_tensor(y[:, par, :, :], bank[5][:, :].rearrange("p (a d) -> p a d", a=2),
                                  b3b[:, ds(e, 1), :].broadcast_to([P, 2, D]), ALU.add).then_inc(y_ready, 1)

            def body(j, par, ahead):
                split(1, j)
                if ahead >= 1:
                    split(0, j + 1)
                if ahead >= 2:
                    low_in(j + 2)
                finish(j, par)

            low_in(0)
            split(0, 0)
            low_in(1)
            tiles(dve, body)
            for i in range(NT * TOPK):
                dve.wait_ge(gathered[i % RING], 16 * (i // RING + 1))
                n, k = i // TOPK, i % TOPK
                if i:
                    dve.wait_ge(added, i)
                dve.scalar_tensor_tensor(X[:, n, :], back[:, i % RING, :], gate[:, n, k:k + 1], X[:, n, :],
                                         ALU.mult, ALU.add).then_inc(added, 1)


SH, SP_, SS, SK = 64, 8, 128, 4
SD = SH * SP_
CONV = SD + 2 * SS
CB = CONV // P
PROJ = SD + CONV + SH
XB = SD // P
LOG_TERMS = 8
UNSCALE = 2.0 ** -14


def ssm_weights_stage(nc, ins, wih, wil, conv_w, conv_b, dt_bias, neg_a, d_col):
    with ExitStack() as ctx:
        t = Tensors(nc, ctx, "ssmw")
        w = t.sb("w", [P, KD, PROJ])
        mup = t.sb("mup", [P, PROJ])
        a_log = t.sb("a_log", [P, 1])
        w_loaded, loaded = t.sem("w_loaded"), t.sem("loaded")
        scaled, high_ready, exp_ready = t.sem("scaled"), t.sem("high_ready"), t.sem("exp_ready")
        block = t.block()

        @block.sync
        def _(sp):
            col = lambda name: ins["L0_attn_b_" + name].unsqueeze(1)
            sp.dma_start(w[:, :, :], ins["L0_attn_b_W_in"].rearrange("(k p) n -> p k n", p=P)).then_inc(w_loaded, 16)
            sp.dma_start(mup[:, :], ins["L0_attn_b_mup_vector"].unsqueeze(0).broadcast_to([P, PROJ])).then_inc(w_loaded, 16)
            for half in range(2):
                rows = slice(half * SH, (half + 1) * SH)
                sp.dma_start(a_log[rows, :], col("A_log")).then_inc(loaded, 16)
                sp.dma_start(dt_bias[rows, :], col("dt_bias")).then_inc(loaded, 16)
            for c in range(XB):
                src = ins["L0_attn_b_D"][c * P // SP_:(c + 1) * P // SP_].unsqueeze(1).unsqueeze(2)
                sp.dma_start(d_col[:, c:c + 1], src.broadcast_to([P // SP_, SP_, 1])).then_inc(loaded, 16)
            sp.dma_start(conv_w[:, :, :], ins["L0_attn_b_conv_w"].rearrange("(c p) k -> p c k", p=P)).then_inc(loaded, 16)
            sp.dma_start(conv_b[:, :], ins["L0_attn_b_conv_b"].rearrange("(c p) -> p c", p=P),
                         allow_slow_non_contiguous=True).then_inc(loaded, 16)
            sp.wait_ge(loaded, (6 + XB) * 16)

        @block.vector
        def _(dve):
            dve.wait_ge(w_loaded, 32)
            dve.tensor_tensor(w[:, :, :], w[:, :, :], mup[:, :].unsqueeze(1).broadcast_to([P, KD, PROJ]),
                              ALU.mult).then_inc(scaled, 1)
            dve.wait_ge(high_ready, 1)
            dve.tensor_tensor(wil[:, :, :], w[:, :, :], wih[:, :, :], ALU.subtract)
            dve.wait_ge(exp_ready, 1)
            dve.tensor_scalar(neg_a[:, :], a_log[:, :], -1.0, None, ALU.mult)

        @block.scalar
        def _(act):
            act.wait_ge(loaded, (6 + XB) * 16)
            act.activation(a_log[:, :], a_log[:, :], ACT.Exp).then_inc(exp_ready, 1)
            act.wait_ge(scaled, 1)
            act.activation(wih[:, :, :], w[:, :, :], ACT.Copy).then_inc(high_ready, 1)


def ssm_out_weights_stage(nc, ins, wo, identf4, one_hot, select, eps, windows):
    with ExitStack() as ctx:
        t = Tensors(nc, ctx, "ssmo")
        norm_w = t.sb("norm_w", [P, XB])
        loaded, cleared = t.sem("loaded"), t.sem("cleared")
        block = t.block()

        @block.sync
        def _(sp):
            sp.dma_start(wo[:, :, :], ins["L0_attn_b_W_out"].rearrange("(k p) n -> p k n", p=P)).then_inc(loaded, 16)
            sp.dma_start(norm_w[:, :], ins["L0_attn_b_norm_w"].rearrange("(c p) -> p c", p=P),
                         allow_slow_non_contiguous=True).then_inc(loaded, 16)

        @block.vector
        def _(dve):
            dve.memset(windows[:, :, :, :], 0.0)
            dve.wait_ge(loaded, 2 * 16)
            for c in range(XB):
                dve.tensor_scalar(wo[:, c, :], wo[:, c, :], norm_w[:, c:c + 1], None, ALU.mult)

        @block.gpsimd
        def _(pool):
            pool.memset(eps[:, :], EPS)
            pool.memset(identf4[:, :, :], 0.0).then_inc(cleared, 1)
            pool.memset(one_hot[:, :], 0.0).then_inc(cleared, 1)
            pool.memset(select[:, :, :], 1.0).then_inc(cleared, 1)
            pool.wait_ge(cleared, 3)
            pool.affine_select(out=one_hot[:, :], in_=one_hot[:, :], compare_op=ALU.not_equal, fill=UNSCALE, base=0,
                               pattern=[[-1, SH]], channel_multiplier=1).then_inc(cleared, 1)
            pool.affine_select(out=select[:, :, :], in_=select[:, :, :], compare_op=ALU.is_ge, fill=0.0, base=SP_ - 1,
                               pattern=[[-P, 2 * XB], [-1, P]], channel_multiplier=SP_).then_inc(cleared, 1)
            pool.wait_ge(cleared, 5)
            pool.affine_select(out=one_hot[:, :], in_=one_hot[:, :], compare_op=ALU.not_equal, fill=UNSCALE, base=-SH,
                               pattern=[[-1, SH]], channel_multiplier=1)
            pool.affine_select(out=select[:, :, :], in_=select[:, :, :], compare_op=ALU.is_ge, fill=0.0, base=0,
                               pattern=[[P, 2 * XB], [1, P]], channel_multiplier=-SP_)
            pool.affine_select(out=identf4[:, :, :], in_=identf4[:, :, :], compare_op=ALU.not_equal, fill=1.0, base=0,
                               pattern=[[0, TB], [-1, P]], channel_multiplier=1)


def ssm_project_stage(nc, XTh, XTl, weights, outs, identf):
    wih, wil, conv_w, conv_b, dt_bias, neg_a = weights[:-1]
    zs, skip, dtx, Bt, G, CT, FT, Etok, dec, piece = outs
    d_col = weights[-1]
    PAIRS = B // 2
    NC = PAIRS * TB
    ORDER = [XB, XB + 1] + list(range(XB))
    with ExitStack() as ctx:
        t = Tensors(nc, ctx, "proj")
        sb, sem = t.sb, t.sem
        taps = sb("taps", [P, 2, S])
        xc = sb("xc", [P, XB, S])
        bc = sb("bc", [P, S])
        wdh, wdl = sb("wdh", [P, KD, 3 * SH], F16), sb("wdl", [P, KD, 3 * SH], F16)
        hi16, lo16 = sb("hi16", [P, PAIRS, S], F16), sb("lo16", [P, PAIRS, S], F16)
        dtt = sb("dtt", [P, B, TB, SH])
        xtr = sb("xtr", [P, 2, SD])
        late = NT // 2
        u, e, zz, z2 = (zs[:, late + PAIRS * k:late + PAIRS * (k + 1), :].rearrange("p a n -> p (a n)") for k in range(4))
        poly, dT, dA, Ftok = (skip[:, late + PAIRS * k:late + PAIRS * (k + 1), :].rearrange("p a n -> p (a n)") for k in range(4))
        starts = dtx[:, late:late + 2, :].rearrange("p a n -> p (a n)")
        suffix = [dtx[:, late + 2 + 3 * k:late + 5 + 3 * k, :].rearrange("p a n -> p (a n)").rearrange("p (c n) -> p c n", c=NC)
                  for k in range(2)]
        bank = t.banks()
        names = ("cleared wd_ready dt_psum dt_read dt_exp dt_u dt_done da_done ft_done suffix_done hi_done lo_done "
                 "conv_psum copied tapped silu z_psum z_done xt_psum xt_done b_psum b_done g_psum g_done "
                 "turn_psum turned spread_psum dec_done dtx_done pieces ordered pool_ordered passed").split()
        s = {n: sem(n) for n in names}
        block = t.block()

        @block.tensor
        def _(pe):
            pe.sem_inc(s["z_done"], 2)
            pe.sem_inc(s["xt_done"], 2)
            pe.wait_ge(s["wd_ready"], 1)
            for r in range(PAIRS):
                for bb in range(2):
                    tok = slice((2 * r + bb) * S, (2 * r + bb + 1) * S)
                    w = slice((1 - bb) * SH, (3 - bb) * SH)
                    for k in range(KD):
                        ins = product3(pe, bank[4 + r][:, :], (wdh[:, k, w], wdl[:, k, w]), (XTh[:, k, tok], XTl[:, k, tok]),
                                       bb == 0 and k == 0, bb == 1 and k == KD - 1)
                ins.then_inc(s["dt_psum"], 1)

            def project(b):
                tok = ds(b * S, S)

                def conv_block(n):
                    c = ORDER[n]
                    pe.wait_ge(s["tapped"], b * CB + n + 1)
                    for k in range(KD):
                        w = slice(SD + c * P, SD + (c + 1) * P)
                        ins = product3(pe, bank[n % 2][:, :], (wih[:, k, w], wil[:, k, w]), (XTh[:, k, tok], XTl[:, k, tok]),
                                       k == 0, k == KD - 1)
                    ins.then_inc(s["conv_psum"], 1)

                def gate(c):
                    pe.wait_ge(s["z_done"], b * XB + c + 1)
                    for k in range(KD):
                        w = slice(c * P, (c + 1) * P)
                        ins = product3(pe, bank[2 + c % 2][:, :], (wih[:, k, w], wil[:, k, w]), (XTh[:, k, tok], XTl[:, k, tok]),
                                       k == 0, k == KD - 1)
                    ins.then_inc(s["z_psum"], 1)

                for n in range(CB - 1):
                    conv_block(n)
                gate(0)
                conv_block(CB - 1)
                pe.wait_ge(s["silu"], b * CB + 3)
                pe.wait_ge(s["b_done"], b + 1)
                for i in range(TB - 1):
                    ins = pe.transpose(bank[7][:, i * P:(i + 1) * P], bc[:, i * P:(i + 1) * P], identf[:, :])
                ins.then_inc(s["b_psum"], 1)
                pe.wait_ge(s["silu"], b * CB + 4)
                pe.wait_ge(s["g_done"], b + 1)
                for i in range(TB):
                    one = slice(i * P, (i + 1) * P)
                    ins = pe.matmul(bank[4][:, one], bc[:, one], CT[:, ds(b * TB + i, 1), :].rearrange("p a n -> p (a n)"),
                                    start=True, stop=True)
                ins.then_inc(s["g_psum"], 1)
                for i in range(1, TB):
                    gate(i)
                pe.wait_ge(s["silu"], b * CB + CB + 2)
                for i in range(TB):
                    pe.wait_ge(s["xt_done"], b * TB + i + 1)
                    for c in range(XB):
                        ins = pe.transpose(bank[5 + i % 2][:, c * P:(c + 1) * P], xc[:, c, i * P:(i + 1) * P], identf[:, :])
                    ins.then_inc(s["xt_psum"], 1)

            def turn(rows, bks, chunks):
                for r in range(PAIRS):
                    for i in range(chunks):
                        ins = pe.transpose(bank[bks[r]][:, i * P:(i + 1) * P], rows(r, i), identf[:, :])
                    ins.then_inc(s["turn_psum"], 1)

            pe.wait_ge(s["dt_done"], 1)
            turn(lambda r, i: dT[:, r * S + i * P:r * S + (i + 1) * P], (5, 6), TB)
            pe.wait_ge(s["dt_read"], PAIRS)
            pe.wait_ge(s["turned"], PAIRS)
            with pe.Fori(0, B // 2) as b:
                project(b)
            pe.wait_ge(s["ft_done"], 1)
            pe.wait_ge(s["g_done"], 3)
            pe.wait_ge(s["b_done"], 3)
            turn(lambda r, i: FT[:, r, i * P:(i + 1) * P], (7, 4), TB)
            pe.wait_ge(s["suffix_done"], 1)
            pe.wait_ge(s["z_done"], 2 * XB + 2)
            turn(lambda r, i: suffix[1][:, r * TB + i, 0:P], (2, 3), TB - 1)
            pe.wait_ge(s["turned"], 3 * PAIRS)
            pe.wait_ge(s["xt_done"], 2 * TB + 2)
            for r in range(PAIRS):
                pe.matmul(bank[5 + r][:, :], identf[:, P - 1:P].broadcast_to([P, P]), Ftok[:, r * S:(r + 1) * S], start=True,
                          stop=True).then_inc(s["turn_psum"], 1)
            pe.wait_ge(s["turned"], 4 * PAIRS)
            with pe.Fori(B // 2, B) as b:
                project(b)

        @block.scalar
        def _(act):
            act.sem_inc(s["silu"], 2)
            for r in range(PAIRS):
                act.wait_ge(s["dt_psum"], r + 1)
                act.activation(u[:, r * S:(r + 1) * S], bank[4 + r][:, :], ACT.Identity, bias=dt_bias[:, :]).then_inc(s["dt_read"], 1)
            act.wait_ge(s["dt_read"], PAIRS)
            act.activation(e, u, ACT.Abs).then_inc(s["dt_exp"], 1)
            act.wait_ge(s["dt_exp"], 1)
            act.activation(e, e, ACT.Exp, scale=-1.0).then_inc(s["dt_exp"], 1)
            act.activation(u, u, ACT.Relu).then_inc(s["dt_u"], 1)
            act.wait_ge(s["dt_done"], 1)
            act.activation(dA, dT, ACT.Exp, scale=neg_a[:, :]).then_inc(s["da_done"], 1)

            def turned(out, bks, first, chunks):
                for r in range(PAIRS):
                    act.wait_ge(s["turn_psum"], first + r + 1)
                    act.activation(out(r), bank[bks[r]][:, 0:chunks * P].rearrange("p (i b h) -> p b i h", i=chunks, b=2),
                                   ACT.Copy).then_inc(s["turned"], 1)

            turned(lambda r: dtt[:, 2 * r:2 * r + 2, :, :], (5, 6), 0, TB)

            def project(b):
                tile = lambda a, i: a[:, ds(b * TB + i, 1), :].rearrange("p a n -> p (a n)")

                def first_tap(n):
                    act.wait_ge(s["conv_psum"], b * CB + n + 1)
                    act.wait_ge(s["silu"], b * CB + n + 1)
                    c = ORDER[n]
                    act.activation(taps[:, n % 2, :], bank[n % 2][:, :], ACT.Copy, scale=conv_w[:, c, SK - 1:SK]).then_inc(s["copied"], 1)

                def silu(n):
                    act.wait_ge(s["tapped"], b * CB + n + 3)
                    c = ORDER[n]
                    if n == 0:
                        out = bc[:, :]
                    elif n == 1:
                        out = CT[:, ds(b * TB, TB), :].rearrange("p a n -> p (a n)")
                    else:
                        out = xc[:, c, :]
                        if n > 2:
                            skipped(n - 3)
                    act.activation(out, taps[:, n % 2, :], ACT.Silu, bias=conv_b[:, c:c + 1]).then_inc(s["silu"], 1)

                def skipped(c):
                    act.wait_ge(s["silu"], b * CB + c + 5)
                    act.activation(tile(skip, c), xc[:, c, :], ACT.Copy, scale=d_col[:, c:c + 1])

                def gate(i):
                    act.wait_ge(s["z_psum"], b * TB + i + 1)
                    act.activation(tile(zs, i), bank[2 + i % 2][:, :], ACT.Silu).then_inc(s["z_done"], 1)

                first_tap(0)
                for n in range(1, CB):
                    first_tap(n)
                    silu(n - 1)
                gate(0)
                silu(CB - 1)
                act.wait_ge(s["b_psum"], b + 1)
                act.activation(Bt[:, ds(b * (TB - 1), TB - 1), :].rearrange("p i n -> p (i n)"), bank[7][:, 0:(TB - 1) * P],
                               ACT.Copy).then_inc(s["b_done"], 1)
                act.wait_ge(s["g_psum"], b + 1)
                act.activation(G[:, ds(b * TB, TB), :].rearrange("p i n -> p (i n)"), bank[4][:, :], ACT.Copy).then_inc(s["g_done"], 1)
                for i in range(1, TB):
                    gate(i)
                skipped(XB - 1)
                for i in range(TB):
                    act.wait_ge(s["xt_psum"], b * TB + i + 1)
                    act.wait_ge(s["dtx_done"], b * TB + i + 1)
                    act.activation(xtr[:, i % 2, :], bank[5 + i % 2][:, :], ACT.Copy).then_inc(s["xt_done"], 1)

            with act.Fori(0, B // 2) as b:
                project(b)
            for r in range(PAIRS):
                act.wait_ge(s["turn_psum"], PAIRS + r + 1)
                act.activation(Ftok[:, r * S:(r + 1) * S], bank[(7, 4)[r]][:, :], ACT.Copy).then_inc(s["turned"], 1)
            turned(lambda r: Etok[:, 2 * r:2 * r + 2, :, :], (2, 3), 2 * PAIRS, TB - 1)
            turned(lambda r: dec[:, 2 * r:2 * r + 2, :, :], (5, 6), 3 * PAIRS, TB - 1)
            with act.Fori(B // 2, B) as b:
                project(b)

        @block.vector
        def _(dve):
            dve.sem_inc(s["tapped"], 2)
            dve.sem_inc(s["b_done"], 1)
            dve.sem_inc(s["g_done"], 1)
            link = Chain(dve, s["ordered"])
            dve.memset(starts, 0.0)
            dve.memset(wdh[:, :, :], 0.0)
            link(dve.memset(wdl[:, :, :], 0.0))
            dve.tensor_copy(wdh[:, :, SH:2 * SH], wih[:, :, PROJ - SH:PROJ])
            dve.tensor_copy(wdl[:, :, SH:2 * SH], wil[:, :, PROJ - SH:PROJ]).then_inc(s["wd_ready"], 1)
            dve.wait_ge(s["dt_exp"], 2)
            link(dve.tensor_scalar(zz, e, 2.0, None, ALU.add))
            link(dve.reciprocal(zz, zz))
            link(dve.tensor_tensor(zz, zz, e, ALU.mult))
            link(dve.tensor_tensor(z2, zz, zz, ALU.mult))
            link(dve.tensor_scalar(poly, z2, 1.0 / (2 * LOG_TERMS + 1), None, ALU.mult))
            for k in range(LOG_TERMS - 1, 0, -1):
                link(dve.scalar_tensor_tensor(poly, poly, 1.0 / (2 * k + 1), z2, ALU.add, ALU.mult))
            link(dve.scalar_tensor_tensor(poly, poly, 1.0, zz, ALU.add, ALU.mult))
            dve.wait_ge(s["dt_u"], 1)
            dve.scalar_tensor_tensor(dT, poly, 2.0, u, ALU.mult, ALU.add).then_inc(s["dt_done"], 1)
            dve.wait_ge(s["da_done"], 1)
            first_steps = lambda a: a.rearrange("p (i n) -> p i n", n=P)[:, :, 0:1]
            link(dve.tensor_copy(first_steps(starts), first_steps(dA)))
            link(dve.memset(first_steps(dA), 0.0))
            dve.tensor_tensor_scan(FT[:, :, :].rearrange("p r n -> p (r n)"), dA, starts, 0.0, ALU.mult, ALU.add).then_inc(s["ft_done"], 1)
            link(dve.tensor_scalar(poly, dA, 1.0 / UNSCALE, None, ALU.mult))
            flat = lambda a: a[:, :, :].rearrange("p r n -> p (r n)")
            dve.tensor_copy(flat(hi16), poly).then_inc(s["hi_done"], 1)
            dve.wait_ge(s["hi_done"], 1)
            dve.tensor_tensor(flat(lo16), poly, flat(hi16), ALU.subtract).then_inc(s["lo_done"], 1)
            before_loop = link.n
            PER = CB * (SK - 2)

            with dve.Fori(0, B) as b:
                link.base, link.n = b * PER + before_loop, 0
                for n in range(CB):
                    dve.wait_ge(s["copied"], b * CB + n + 1)
                    c, x, acc = ORDER[n], bank[n % 2], taps[:, n % 2, :]
                    for back in range(1, SK):
                        w = conv_w[:, c, SK - 1 - back:SK - back]
                        ins = dve.scalar_tensor_tensor(acc[:, back:S], x[:, 0:S - back], w, acc[:, back:S], ALU.mult, ALU.add)
                        if back < SK - 1:
                            link(ins)
                    ins.then_inc(s["tapped"], 1)
                assert link.n == PER

        @block.gpsimd
        def _(pool):
            link = Chain(pool, s["pool_ordered"], s["passed"])
            pool.sem_inc(s["dtx_done"], 2)
            for buf in suffix:
                ins = pool.memset(buf[:, :, P - 1:], 1.0)
            link(ins)
            wait_alone(pool, s["da_done"], 1, s["passed"])
            link(pool.tensor_copy(suffix[0][:, :, 0:P - 1], dA.rearrange("p (c n) -> p c n", n=P)[:, :, 1:P]))
            for k in range(7):
                a, out = suffix[k % 2], suffix[1 - k % 2]
                ins = pool.tensor_tensor(out[:, :, 0:P], a[:, :, 0:P], a[:, :, (1 << k):(1 << k) + P], ALU.mult)
                if k < 6:
                    link(ins)
                else:
                    ins.then_inc(s["suffix_done"], 1)
            per_head = lambda a: a.rearrange("p (h q) -> p h q", q=SP_)
            wait_alone(pool, s["turned"], PAIRS, s["passed"])
            with pool.Fori(0, NT // 2) as m:
                for half in range(2):
                    n = m * 2 + half
                    wait_alone(pool, s["xt_done"], n + 3, s["passed"])
                    dt = dtt[:, :, :, :].rearrange("p b i h -> p (b i) h")[:, ds(n, 1), :].rearrange("p a h -> p (a h)")
                    pool.tensor_tensor(per_head(dtx[:, ds(n, 1), :].rearrange("p a n -> p (a n)")), per_head(xtr[:, half, :]),
                                       dt.unsqueeze(2).broadcast_to([P, SH, SP_]), ALU.mult).then_inc(s["dtx_done"], 1)

        @block.sync
        def _(sp):
            for part, (src, done) in enumerate(((hi16, "hi_done"), (lo16, "lo_done"))):
                sp.wait_ge(s[done], 1)
                for bb in range(2):
                    for r in range(PAIRS):
                        sp.dma_start(piece[part * SH:(part + 1) * SH, 2 * r + bb, :], src[bb * SH:(bb + 1) * SH, r, :]).then_inc(s["pieces"], 16)
            sp.wait_ge(s["pieces"], 4 * PAIRS * 16)


def ssm_heads_stage(nc, X, inputs, weights):
    zs, skip, dtx, Bt, G, CT, FT, Etok, dec, piece = inputs
    wo, identf4, one_hot, select, eps, windows = weights
    RING, WINDOWS, Q = 4, windows.shape[1], SH // TB
    NS = TB - 1
    AT = P - SP_
    dve_heads = [j for j in range(Q) if j % 8 in (1, 4, 6)]
    pool_heads = [j for j in range(Q) if j not in dve_heads]
    with ExitStack() as ctx:
        t = Tensors(nc, ctx, "ssm")
        sb, sem = t.sb, t.sem
        L, GL = sb("L", [P, RING, TB, P]), sb("GL", [P, RING, TB, P])
        Bq, Sq, select_q = sb("Bq", [P, P]), sb("Sq", [P, NS, P]), sb("select_q", [P, P])
        edtx, states = sb("edtx", [P, SD]), sb("states", [P, NS, SD])
        decay, carried = sb("decay", [P, NS * P]), sb("carried", [P, NS * P])
        g = sb("g", [P, XB, S])
        square, ones = sb("square", [P, S]), sb("ones", [P, 1])
        ssum, sd, rstd = sb("ssum", [P, TB]), sb("sd", [P, TB]), sb("rstd", [P, TB])
        Y = ctx.enter_context(nc.psum_tensor("ssm_Y", [P, TB * S], F32))
        bank = t.banks(4)
        names = ("bc_ready scan_done mult_pool mult_dve window_done y_done y_read select_kept state_kept b_kept "
                 "decay_psum decay_kept inter_psum inter_read mixed gated sq_done ss_psum ss_read edtx_done upd_psum state_done "
                 "sd_done rstd_done out_psum added ones_done scaled ordered pool_ordered passed pe_passed").split()
        s = {n: sem(n) for n in names}
        block = t.block()
        per_head = lambda a: a.rearrange("p (h q) -> p h q", q=SP_)
        wide = lambda a: a.unsqueeze(2).broadcast_to([P, SH, SP_])
        one = lambda a, n: a[:, ds(n, 1), :].rearrange("p a n -> p (a n)")
        per_token = lambda a, n: one(a[:, :, :, :].rearrange("p b i h -> p (b i) h"), n)
        flat = lambda a: a.rearrange("p i n -> p (i n)")

        def mult_count(qn, j):
            heads, name = (dve_heads, "mult_dve") if j % Q in dve_heads else (pool_heads, "mult_pool")
            at = heads.index(j % Q) + 1
            return s[name], qn * len(heads) + (at + len(heads) if j >= 0 else at)

        def over_quarters(eng, start, quarter, finish_last):
            def batch(b, finish_first):
                if start:
                    start(b)
                quarter(b, 0, finish_first)
                with eng.Fori(1, TB - 1) as q:
                    quarter(b, q, True)
                quarter(b, TB - 1, True)

            batch(0, False)
            with eng.Fori(1, B) as b:
                batch(b, True)
            finish_last()

        is_static = lambda q, n: isinstance(q, int) and q == n

        def finished(b, q):
            return (b - 1, XB - 1, b * TB - 1) if is_static(q, 0) else (b, q - 1, b * TB + q - 1)

        @block.tensor
        def _(pe):
            pe.sem_inc(s["y_done"], RING)
            pe.sem_inc(s["inter_psum"], 1)
            pe.sem_inc(s["decay_psum"], 1)
            pe.sem_inc(s["ss_psum"], 1)
            pe.sem_inc(s["upd_psum"], 1)

            def spread(b, h, j):
                pe.wait_ge(s["scan_done"], b * SH + h + 1)
                pe.matmul(bank[j % 2][:, :], one_hot[:, ds(h, 1)].broadcast_to([P, P]), one(piece, b),
                          start=True, stop=True).then_inc(s["bc_ready"], 1)

            def start(b):
                for h in range(3):
                    spread(b, h, h)

            def carry(fb, fc, n):
                pe.wait_ge(s["select_kept"], n + 1)
                pe.wait_ge(s["ss_read"], n + 1)
                pe.matmul(bank[2][:, :], select_q[:, :], one(FT, fb // 2), start=True, stop=True).then_inc(s["decay_psum"], 1)
                pe.wait_ge(s["state_kept"], n + 1)
                pe.wait_ge(s["inter_read"], n + 1)
                for i in range(NS):
                    ins = pe.matmul(bank[3][:, i * P:(i + 1) * P], Sq[:, i, :], one(CT, fb * TB + i + 1), start=True, stop=True)
                ins.then_inc(s["inter_psum"], 1)

            def sum_squares(n):
                pe.wait_ge(s["sq_done"], n + 1)
                pe.wait_ge(s["decay_kept"], n + 1)
                for i in range(TB):
                    ins = pe.matmul(bank[2][:, i:i + 1], square[:, i * P:(i + 1) * P], ones[:, :], start=True, stop=True)
                ins.then_inc(s["ss_psum"], 1)

            def update(b, i):
                v = b * NS + i
                pe.wait_ge(s["edtx_done"], v + 1)
                pe.wait_ge(s["b_kept"], v + 1)
                pe.wait_ge(s["state_done"], v + 1)
                pe.matmul(bank[3][:, :], Bq[:, :], edtx[:, :], start=True, stop=True).then_inc(s["upd_psum"], 1)

            def project(n, half):
                pe.wait_ge(s["gated"], n + 1)
                for i in range(2):
                    at = (2 * half + i) * P
                    for c in range(XB):
                        ins = pe.matmul(bank[2 + half][:, i * D:(i + 1) * D], g[:, c, at:at + P], wo[:, c, :], start=c == 0,
                                        stop=c == XB - 1)
                ins.then_inc(s["out_psum"], 1)

            def quarter(b, q, finish):
                qn = b * TB + q
                first, last = is_static(q, 0), is_static(q, TB - 1)
                fb, fc, n = finished(b, q)
                for j in range(Q):
                    h = q * Q + j
                    if not last or j + 3 < Q:
                        spread(b, h + 3, j + 3)
                    if j == 0:
                        pe.wait_ge(s["y_read"], qn + 1)
                    pe.wait_ge(s["window_done"], b * SH + h + 1)
                    wait_alone(pe, *mult_count(qn, j), s["pe_passed"])
                    for i in range(TB):
                        ins = pe.matmul(Y[:, ds(q * S + i * P, P)], windows[:, j % WINDOWS, i, AT - j * SP_:AT - j * SP_ + P],
                                        GL[:, j % RING, i, :], start=j == 0 and i == 0, stop=j == Q - 1 and i == TB - 1)
                    ins.then_inc(s["y_done"], 1)
                    if finish and j == (0 if first else 1):
                        if not first:
                            pe.wait_ge(s["added"], b * 2 + 1)
                        carry(fb, fc, n)
                    if first and j in (4, 7, 10):
                        if finish and j == 4:
                            pe.wait_ge(s["inter_read"], n + 2)
                        update(b, (j - 4) // 3)
                    if finish and j == (9 if first else 12):
                        sum_squares(n)
                    if finish and first and j == 12:
                        pe.wait_ge(s["ss_read"], n + 2)
                        project(n, 0)
                    if finish and first and j == 14:
                        pe.wait_ge(s["state_done"], b * NS + NS + 1)
                        project(n, 1)

            def finish_last():
                n = B * TB - 1
                carry(B - 1, XB - 1, n)
                sum_squares(n)
                pe.wait_ge(s["ss_read"], n + 2)
                project(n, 0)
                pe.wait_ge(s["inter_read"], n + 2)
                project(n, 1)

            pe.wait_ge(s["ones_done"], 1)
            over_quarters(pe, start, quarter, finish_last)

        @block.scalar
        def _(act):
            def keep(fb, fc, n):
                act.wait_ge(s["decay_psum"], n + 1)
                act.activation(select_q[:, :], one(select, fb % 2 * XB + fc), ACT.Copy).then_inc(s["select_kept"], 1)
                act.wait_ge(s["inter_psum"], n + 1)
                act.wait_ge(s["state_done"], (fb + 1) * NS + 1)
                act.activation(Sq[:, :, :], states[:, :, ds(fc * P, P)], ACT.Copy).then_inc(s["state_kept"], 1)

            def keep_decay(n):
                act.wait_ge(s["decay_psum"], n + 2)
                act.wait_ge(s["inter_read"], n + 1)
                act.activation(decay[:, :], bank[2][:, P:], ACT.Copy).then_inc(s["decay_kept"], 1)

            def square_up(fc, n):
                act.wait_ge(s["gated"], n + 1)
                act.wait_ge(s["ss_psum"], n + 1)
                act.activation(square[:, :], one(g, fc), ACT.Square).then_inc(s["sq_done"], 1)

            def root(b, n):
                act.wait_ge(s["ss_read"], n + 2)
                act.wait_ge(s["rstd_done"], b)
                act.activation(sd[:, :], ssum[:, :], ACT.Sqrt, scale=1.0 / SD, bias=eps[:, :]).then_inc(s["sd_done"], 1)

            def quarter(b, q, finish):
                first = is_static(q, 0)
                fb, fc, n = finished(b, q)
                for j in range(Q):
                    h = q * Q + j
                    if finish and j == 0:
                        keep(fb, fc, n)
                    act.wait_ge(s["y_done"], b * SH + h + 1 + RING - WINDOWS)
                    act.activation(windows[:, j % WINDOWS, :, AT:AT + SP_], dtx[:, ds(b * TB, TB), ds(h * SP_, SP_)],
                                   ACT.Copy).then_inc(s["window_done"], 1)
                    if first and j in (1, 7, 10):
                        v = b * NS + (1, 7, 10).index(j)
                        act.wait_ge(s["upd_psum"], v + 1)
                        act.activation(Bq[:, :], one(Bt, v), ACT.Copy).then_inc(s["b_kept"], 1)
                    if finish and j == (4 if first else 5):
                        keep_decay(n)
                    if finish and j == (11 if first else 13):
                        square_up(fc, n)
                    if finish and first and j == 15:
                        root(b, n)

            def finish_last():
                n = B * TB - 1
                keep(B - 1, XB - 1, n)
                keep_decay(n)
                square_up(XB - 1, n)
                root(B, n)

            over_quarters(act, None, quarter, finish_last)

        @block.vector
        def _(dve):
            dve.sem_inc(s["scan_done"], 2)
            dve.sem_inc(s["mult_dve"], len(dve_heads))
            for name in ("inter_read", "ss_read", "state_done", "added", "rstd_done"):
                dve.sem_inc(s[name], 1)
            dve.sem_inc(s["y_read"], TB)
            dve.memset(ones[:, :], 1.0).then_inc(s["ones_done"], 1)
            link = Chain(dve, s["ordered"])
            link(dve.memset(ssum[:, :], 0.0))
            before_loop = link.n

            def scan(b, q, j):
                dve.wait_ge(s["bc_ready"], b * SH + q * Q + j + 1)
                dve.wait_ge(*mult_count(b * TB + q, j - RING))
                dve.tensor_tensor_scan(flat(L[:, j % RING, :, :]), bank[j % 2][:, :], flat(identf4[:, :, :]), 0.0,
                                       ALU.mult, ALU.add).then_inc(s["scan_done"], 1)

            def start(b):
                scan(b, 0, 0)

            def read_block(fb, fc, n, qn):
                dve.wait_ge(s["y_done"], qn * Q + RING)
                dve.tensor_tensor(one(g, fc), Y[:, ds(fc * S, S)], one(skip, fb * XB + fc), ALU.add).then_inc(s["y_read"], 1)

            def read_inter(n):
                dve.wait_ge(s["inter_psum"], n + 2)
                dve.wait_ge(s["decay_kept"], n + 1)
                dve.wait_ge(s["mixed"], n + 1)
                dve.tensor_tensor(carried[:, :], bank[3][:, 0:NS * P], decay[:, :], ALU.mult).then_inc(s["inter_read"], 1)

            def read_squares(n):
                dve.wait_ge(s["ss_psum"], n + 2)
                dve.tensor_tensor(ssum[:, :], ssum[:, :], bank[2][:, 0:TB], ALU.add).then_inc(s["ss_read"], 1)

            def read_update(b, i):
                v = b * NS + i
                link.base, link.n = (before_loop if is_static(b, 0) else b * 3 + before_loop - 1), max(i - 1, 0)
                if i == 0:
                    if not is_static(b, 0):
                        dve.wait_ge(s["state_kept"], b * TB)
                else:
                    dve.wait_ge(s["state_done"], v + 1)
                    link(dve.tensor_tensor(per_head(states[:, i, :]), per_head(states[:, i - 1, :]),
                                           wide(per_token(dec, v)), ALU.mult))
                dve.wait_ge(s["upd_psum"], v + 2)
                if i == 0:
                    dve.tensor_copy(states[:, 0, :], bank[3][:, :]).then_inc(s["state_done"], 1)
                else:
                    dve.tensor_tensor(states[:, i, :], states[:, i, :], bank[3][:, :], ALU.add).then_inc(s["state_done"], 1)

            def add_outputs(b, n):
                dve.wait_ge(s["sd_done"], b)
                dve.wait_ge(s["added"], b * 2 - 1)
                dve.reciprocal(rstd[:, :], sd[:, :]).then_inc(s["rstd_done"], 1)
                link.base, link.n = b * 3 + before_loop - 1 + (0 if is_static(b, B) else 2), 0
                link(dve.memset(ssum[:, :], 0.0))
                dve.wait_ge(s["rstd_done"], b + 1)
                for half in range(2):
                    dve.wait_ge(s["out_psum"], b * 2 - 1 + half)
                    for i in range(2):
                        at = 2 * half + i
                        x = one(X, b * TB - TB + at)
                        ins = dve.scalar_tensor_tensor(x, bank[2 + half][:, i * D:(i + 1) * D], rstd[:, at:at + 1], x,
                                                       ALU.mult, ALU.add)
                    ins.then_inc(s["added"], 1)

            def quarter(b, q, finish):
                qn = b * TB + q
                first, last = is_static(q, 0), is_static(q, TB - 1)
                fb, fc, n = finished(b, q)
                for j in range(Q):
                    gh = b * SH + q * Q + j
                    if not last or j + 1 < Q:
                        scan(b, q, j + 1)
                    if j in dve_heads:
                        dve.wait_ge(s["scan_done"], gh + 3)
                        dve.wait_ge(s["y_done"], gh + 1)
                        dve.tensor_tensor(GL[:, j % RING, :, :], L[:, j % RING, :, :], G[:, ds(b * TB, TB), :],
                                          ALU.mult).then_inc(s["mult_dve"], 1)
                    if finish and j == (1 if first else 2):
                        read_block(fb, fc, n, qn)
                    if finish and j == (3 if first else 5):
                        read_inter(n)
                    if first and j in (6, 9, 12):
                        read_update(b, (j - 6) // 3)
                    if finish and j == (11 if first else 14):
                        read_squares(n)
                    if finish and first and j == 15:
                        add_outputs(b, n)

            def finish_last():
                n = B * TB - 1
                read_block(B - 1, XB - 1, n, B * TB)
                read_inter(n)
                read_squares(n)
                add_outputs(B, n)

            over_quarters(dve, start, quarter, finish_last)

        @block.gpsimd
        def _(pool):
            pool.sem_inc(s["mult_pool"], len(pool_heads))
            pool.sem_inc(s["mixed"], 1)

            def gate(fb, fc, n):
                wait_alone(pool, s["inter_read"], n + 2, s["passed"])
                wait_alone(pool, s["y_read"], n + 1 + TB, s["passed"])
                block_g = one(g, fc)
                pool.tensor_tensor(block_g[:, P:], block_g[:, P:], carried[:, :], ALU.add).then_inc(s["mixed"], 1)
                wait_alone(pool, s["mixed"], n + 2, s["passed"])
                pool.tensor_tensor(block_g, block_g, one(zs, fb * XB + fc), ALU.mult).then_inc(s["gated"], 1)

            def quarter(b, q, finish):
                qn = b * TB + q
                first = is_static(q, 0)
                fb, fc, n = finished(b, q)
                for j in range(Q):
                    if j in pool_heads:
                        gh = b * SH + q * Q + j
                        wait_alone(pool, s["scan_done"], gh + 3, s["passed"])
                        wait_alone(pool, s["y_done"], gh + 1, s["passed"])
                        pool.tensor_tensor(GL[:, j % RING, :, :], L[:, j % RING, :, :], G[:, ds(b * TB, TB), :],
                                           ALU.mult).then_inc(s["mult_pool"], 1)
                    if first and j in (0, 5, 8):
                        i = (0, 5, 8).index(j)
                        v = b * NS + i
                        wait_alone(pool, s["upd_psum"], v + 1, s["passed"])
                        pool.tensor_tensor(per_head(edtx[:, :]), per_head(one(dtx, b * TB + i)), wide(per_token(Etok, v)),
                                           ALU.mult).then_inc(s["edtx_done"], 1)
                    if finish and j == (3 if first else 6):
                        gate(fb, fc, n)

            def finish_last():
                gate(B - 1, XB - 1, B * TB - 1)

            over_quarters(pool, None, quarter, finish_last)


def ssm_layer(nc, ins, X, c):
    with ExitStack() as ctx:
        t = Tensors(nc, ctx, "ssml")
        inputs = (t.sb("zs", [P, B * XB, S]), t.sb("skip", [P, B * XB, S]), t.sb("dtx", [P, NT, SD]),
                  t.sb("Bt", [P, B * (TB - 1), P]), t.sb("G", [P, NT, P]), t.sb("CT", [P, NT, P]),
                  t.sb("FT", [P, B // 2, S]), t.sb("Etok", [P, B, TB - 1, SH]), t.sb("dec", [P, B, TB - 1, SH]),
                  t.sb("piece", [2 * SH, B, S], F16))
        with ExitStack() as inner:
            t = Tensors(nc, inner, "ssmi")
            XTh, XTl = t.sb("XTh", [P, KD, B * S], F16), t.sb("XTl", [P, KD, B * S], F16)
            weights = (t.sb("wih", [P, KD, PROJ], F16), t.sb("wil", [P, KD, PROJ], F16), t.sb("conv_w", [P, CB, SK]),
                       t.sb("conv_b", [P, CB]), t.sb("dt_bias", [P, 1]), t.sb("neg_a", [P, 1]), t.sb("d_col", [P, XB]))
            ssm_weights_stage(nc, ins, *weights)
            layer_norm_stage(nc, "ln2", X, None, XTh, XTl, c["identf"])
            ssm_project_stage(nc, XTh, XTl, weights, inputs, c["identf"])
        t = Tensors(nc, ctx, "ssmh")
        weights = (t.sb("wo", [P, XB, D]), t.sb("identf4", [P, TB, P]), t.sb("one_hot", [P, SH], F16),
                   t.sb("select", [P, 2 * XB, P]), t.sb("eps", [P, 1]), t.sb("windows", [P, 2, TB, 2 * P - SP_]))
        ssm_out_weights_stage(nc, ins, *weights)
        ssm_heads_stage(nc, X, inputs, weights)


def store_stage(nc, X, out):
    with ExitStack() as ctx:
        t = Tensors(nc, ctx, "store")
        stored = t.sem("stored")
        block = t.block()

        @block.sync
        def _(sp):
            sp.dma_start(out.rearrange("b (t p) d -> p (b t) d", p=P), X[:, :, :]).then_inc(stored, 16)
            sp.wait_ge(stored, 16)


def attention_layer(nc, ins, X, c, sorted_x):
    with ExitStack() as ctx:
        t = Tensors(nc, ctx, "attw")
        pair = lambda name, shape: (t.sb(name + "h", shape, F16), t.sb(name + "l", shape, F16))
        XTh, XTl = pair("XT", [P, KD, B * S])
        wq, wd, wk = pair("wq", [P, KD, NH * HD]), pair("wd", [P, KD, LAT]), pair("wk", [P, KD, DR])
        wu, wo = pair("wu", [LAT, NH * 2 * DH]), pair("wo", [P, KD, D])
        rows = lambda a: a.rearrange("(k p) n -> p k n", p=P)
        split_weights(nc, "attsplit", [
            (rows(ins["L0_attn_a_Wq"]), *wq), (rows(ins["L0_attn_a_Wdkv"]), *wd), (rows(ins["L0_attn_a_Wkr"]), *wk),
            (ins["L0_attn_a_Wukv"], *wu), (rows(ins["L0_attn_a_Wo"]), *wo)])
        layer_norm_stage(nc, "ln0", X, None, XTh, XTl, c["identf"])
        attention_stage(nc, X, XTh, XTl, (wq, wd, wk, wu, wo), c["identf"], c["ident16"], c["identb"], c["upper_neg"],
                        c["cosr"], c["sinr"], sorted_x)


def ffn_layer(nc, stage, ins, X, experts, sorted_x, sorted_y, row_moves, c):
    with ExitStack() as ctx:
        t = Tensors(nc, ctx, stage)
        XN = t.sb("XN", [P, NT, D])
        gate = t.sb("gate", [P, NT, TOPK])
        slots = t.sb("slots", [P, TOPK, NT], I32)
        tile_expert = t.sb("tile_expert", [P, NSLOT], I32)
        with ExitStack() as inner:
            t = Tensors(nc, inner, stage + "t")
            XTh, XTl = t.sb("XTh", [P, KD, B * S], F16), t.sb("XTl", [P, KD, B * S], F16)
            layer_norm_stage(nc, stage + "ln", X, XN, XTh, XTl, c["identf"], (ins, *experts))
            routing_stage(nc, stage + "r", ins, XTh, XTl, gate, slots, tile_expert, *experts)
        experts_stage(nc, stage + "x", ins, X, XN, *experts, gate, slots, tile_expert, c["identf"], sorted_x, sorted_y,
                      row_moves)


def build(nc, ins, out, layers=("attn", "ffn", "ssm", "ffn")):
    with ExitStack() as ctx:
        t = Tensors(nc, ctx, "main")
        X = t.sb("X", [P, NT, D])
        c = {"identf": t.sb("identf", [P, P]), "ident16": t.sb("ident16", [P, P], F16), "identb": t.sb("identb", [P, P], BF16),
             "upper_neg": t.sb("upper_neg", [P, P], BF16), "cosr": t.sb("cosr", [P, TB, HALF]), "sinr": t.sb("sinr", [P, TB, HALF])}
        constants_stage(nc, ins["x"], ins["cos"], ins["sin"], X, **c)
        row_moves = {n: [ctx.enter_context(nc.semaphore(f"{name}_{n}")) for name in ["scattered"] + [f"gathered{i}" for i in range(8)]]
                     for n, layer in enumerate(layers) if layer == "ffn"}
        sorted_x = nc.dram_tensor("sorted_x", [NSLOT * ST, D], F32, kind="Internal").ap()
        sorted_y = nc.dram_tensor("sorted_y", [NSLOT * ST, D], F32, kind="Internal").ap()
        for n, layer in enumerate(layers):
            if layer == "attn":
                attention_layer(nc, ins, X, c, sorted_x)
            if layer == "ssm":
                ssm_layer(nc, ins, X, c)
            if layer == "ffn":
                with ExitStack() as inner:
                    w = Tensors(nc, inner, f"ew{n}")
                    experts = (w.sb("WH", [P, NE * WCOLS], F16), w.sb("WL", [P, NE * WCOLS], F16))
                    ffn_layer(nc, f"ffn{n}", ins, X, experts, sorted_x, sorted_y, row_moves[n], c)
        store_stage(nc, X, out)


def rope_tables():
    inv_freq = np.float32(1.0) / np.power(np.float32(10000.0), np.arange(0, DR, 2, dtype=np.float32) / np.float32(DR))
    freqs = np.arange(S, dtype=np.float32)[:, None] * inv_freq[None, :]
    return np.cos(freqs), np.sin(freqs)


_INS = ["L0_attn_a_Wq", "L0_attn_a_Wdkv", "L0_attn_a_Wkr", "L0_attn_a_Wukv", "L0_attn_a_Wo", "L0_attn_b_W_in",
        "L0_attn_b_conv_w", "L0_attn_b_conv_b", "L0_attn_b_A_log", "L0_attn_b_D", "L0_attn_b_dt_bias", "L0_attn_b_norm_w",
        "L0_attn_b_W_out", "L0_attn_b_mup_vector", "L0_ffn_W1", "L0_ffn_b1", "L0_ffn_W2", "L0_ffn_b2", "L0_ffn_W3",
        "L0_ffn_b3", "L0_ffn_Wg", "L0_ffn_bg"]


def kernel(**inputs):
    import concourse.bacc as bacc
    from concourse.bass_utils import run_bass_kernel_spmd as run

    cos, sin = rope_tables()
    arrays = {"x": inputs["L0_attn_a_x"], "cos": cos, "sin": sin} | {n: inputs[n] for n in _INS}
    nc = bacc.Bacc("TRN2", target_bir_lowering=False, num_devices=1)
    given, placed = {}, {}
    for name, a in arrays.items():
        given[f"in_{name}"] = np.ascontiguousarray(a)
        placed[name] = nc.dram_tensor(f"in_{name}", given[f"in_{name}"].shape, mybir.dt.from_np(given[f"in_{name}"].dtype),
                                      kind="ExternalInput").ap()
    out = nc.dram_tensor("out", (B, S, D), F32, kind="ExternalOutput").ap()
    build(nc, placed, out)
    r = run(nc, [given], core_ids=[0])
    return r.results[0]["out"]
```
